# Optimizing a Trainium2 kernel written in Bass

```python
import numpy as np
import jax
import jax.numpy as jnp

def _softmax(x, axis=-1):
    return jax.nn.softmax(x, axis=axis)

def _gelu(x):
    return jax.nn.gelu(x, approximate=True)

def _silu(x):
    return jax.nn.silu(x)

def _sigmoid(x):
    return jax.nn.sigmoid(x)

def _layernorm(x, axis=-1, eps=1e-05):
    m = jnp.mean(x, axis=axis, keepdims=True)
    v = jnp.var(x, axis=axis, keepdims=True)
    return (x - m) / jnp.sqrt(v + eps)

def _scatter_add(tgt, idx, src, axis=0):
    return tgt.at[idx].add(src)

def _segment_sum(src, seg, n):
    return jax.ops.segment_sum(src, seg, n)
kernel_name = 'mk_gps_d2_gnn_r32_153e01'

def setup_inputs(seed: int=0):
    np.random.seed(seed)
    _w = jnp.asarray

    def _rec_inputs():
        import jax
        import jax.numpy as jnp
        _gk = jax.random.key(seed)
        x = -0.0003713 + 1 * jax.random.normal(jax.random.fold_in(_gk, 1), (3125, 256), jnp.float32)
        _s = jax.random.randint(jax.random.fold_in(_gk, 2), (25000,), 0, 3125, jnp.int32)
        _d = jax.random.randint(jax.random.fold_in(_gk, 3), (25000,), 0, 3125, jnp.int32)
        _loop = jnp.arange(3125, dtype=jnp.int32)
        src = jnp.concatenate([_s, _d, _loop])
        dst = jnp.concatenate([_d, _s, _loop])
        _o = jnp.argsort(dst, stable=True)
        src = src[_o]
        dst = dst[_o]
        edge_weight = jax.random.uniform(jax.random.fold_in(_gk, 13), (53125,), jnp.float32, 0.0, 1)
        return (x, src, dst, edge_weight)
    x, src, dst, edge_weight = _rec_inputs()

    def _L0_gnn_setup():
        import jax, jax.numpy as jnp
        import numpy as np
        N_NODES = 50000
        N_EDGES = 25000
        F_IN = 256
        F_OUT = 64
        HEADS = 4
        LEAKY_ALPHA = 0.2
        key = jax.random.key(seed)
        ks = jax.random.split(key, 8)
        x = jax.random.normal(ks[0], (N_NODES, F_IN), dtype=jnp.float32)
        W = jax.random.normal(ks[1], (HEADS, F_IN, F_OUT), dtype=jnp.float32) * 0.05
        a_self = jax.random.normal(ks[2], (HEADS, F_OUT), dtype=jnp.float32) * 0.05
        a_neigh = jax.random.normal(ks[3], (HEADS, F_OUT), dtype=jnp.float32) * 0.05
        bias = jnp.zeros((HEADS, F_OUT), dtype=jnp.float32)
        adj_val = jnp.ones((N_EDGES,), dtype=jnp.float32)
        edge_row = jax.random.randint(ks[4], (N_EDGES,), 0, N_NODES, dtype=jnp.int32)
        edge_col = jax.random.randint(ks[5], (N_EDGES,), 0, N_NODES, dtype=jnp.int32)
        return {'x': x, 'W': W, 'a_self': a_self, 'a_neigh': a_neigh, 'bias': bias, 'adj_val': adj_val, 'edge_row': edge_row, 'edge_col': edge_col}
    _L0_gnn_all = _L0_gnn_setup()
    _L0_gnn_in = {k: v for k, v in _L0_gnn_all.items() if k in ('W', 'a_self', 'a_neigh', 'bias')}
    del _L0_gnn_all

    def _L0_mix_setup():
        import jax, jax.numpy as jnp
        import numpy as np
        B, S, D = (8, 64, 256)
        H, KD = (8, 256)
        M = 256
        EPS_LN = 1e-06
        EPS_ATT = 1e-06

        def _layernorm(x, g, b):
            mu = jnp.mean(x, axis=-1, keepdims=True)
            var = jnp.mean(jnp.square(x - mu), axis=-1, keepdims=True)
            return (x - mu) * jax.lax.rsqrt(var + EPS_LN) * g + b

        def _phi(x, proj):
            u = jnp.einsum('bshd,md->bshm', x, proj)
            sq = 0.5 * jnp.sum(jnp.square(x), axis=-1, keepdims=True)
            return jnp.exp(u - sq) * (1.0 / np.sqrt(M)) + EPS_ATT
        key = jax.random.key(seed)
        ks = jax.random.split(key, 16)
        sd = lambda *s: 1.0 / np.sqrt(s[0])
        return {'inputs': jax.random.normal(ks[0], (B, S, D), dtype=jnp.float32), 'Wq': jax.random.normal(ks[1], (D, H, KD), jnp.float32) * sd(D), 'bq': jnp.zeros((H, KD), jnp.float32), 'Wk': jax.random.normal(ks[2], (D, H, KD), jnp.float32) * sd(D), 'bk': jnp.zeros((H, KD), jnp.float32), 'Wv': jax.random.normal(ks[3], (D, H, KD), jnp.float32) * sd(D), 'bv': jnp.zeros((H, KD), jnp.float32), 'Wo': jax.random.normal(ks[4], (H, KD, D), jnp.float32) * sd(H * KD), 'bo': jnp.zeros((D,), jnp.float32), 'proj': jax.random.normal(ks[5], (M, KD), jnp.float32), 'W1': jax.random.normal(ks[6], (D, D), jnp.float32) * sd(D), 'bias1': jnp.zeros((D,), jnp.float32), 'W2': jax.random.normal(ks[7], (D, D), jnp.float32) * sd(D), 'bias2': jnp.zeros((D,), jnp.float32), 'g1': jnp.ones((D,), jnp.float32), 'beta1': jnp.zeros((D,), jnp.float32), 'g2': jnp.ones((D,), jnp.float32), 'beta2': jnp.zeros((D,), jnp.float32)}
    _L0_mix_all = _L0_mix_setup()
    _L0_mix_in = {k: v for k, v in _L0_mix_all.items() if k in ('Wq', 'bq', 'Wk', 'bk', 'Wv', 'bv', 'Wo', 'bo', 'proj', 'W1', 'bias1', 'W2', 'bias2', 'g1', 'beta1', 'g2', 'beta2')}
    del _L0_mix_all

    def _L0_ffn_setup():
        import jax, jax.numpy as jnp
        import numpy as np
        B, S, D = (8, 128, 256)
        H = 4 * D
        CAPACITY = 0.5
        key = jax.random.key(seed)
        ks = jax.random.split(key, 6)
        x = jax.random.normal(ks[0], (B, S, D), dtype=jnp.float32)
        attention_mask = jnp.zeros((B, 1, 1, S), dtype=jnp.float32)
        wr = jax.random.normal(ks[1], (D, 1), dtype=jnp.float32) * 0.02
        br = jnp.zeros((1,), dtype=jnp.float32)
        w1 = jax.random.normal(ks[2], (D, H), dtype=jnp.float32) * 0.02
        b1 = jnp.zeros((H,), dtype=jnp.float32)
        w2 = jax.random.normal(ks[3], (H, D), dtype=jnp.float32) * 0.02
        b2 = jnp.zeros((D,), dtype=jnp.float32)
        return {'x': x, 'attention_mask': attention_mask, 'wr': wr, 'br': br, 'w1': w1, 'b1': b1, 'w2': w2, 'b2': b2}
    _L0_ffn_all = _L0_ffn_setup()
    _L0_ffn_in = {k: v for k, v in _L0_ffn_all.items() if k in ('attention_mask', 'wr', 'br', 'w1', 'b1', 'w2', 'b2')}
    del _L0_ffn_all

    def _L1_gnn_setup():
        import jax, jax.numpy as jnp
        import numpy as np
        N, E = (50000, 25000)
        D_IN, H1, F1 = (256, 4, 64)
        H2, F2 = (1, 256)
        NEG_SLOPE = 0.2

        def gat_conv(x, src, dst, W, a_src, a_dst, b, heads, feats, n_nodes):
            h = (x @ W).reshape(n_nodes, heads, feats)
            s_src = jnp.einsum('nhf,hf->nh', h, a_src)
            s_dst = jnp.einsum('nhf,hf->nh', h, a_dst)
            e = jax.nn.leaky_relu(s_src[src] + s_dst[dst], NEG_SLOPE)
            emax = jax.lax.stop_gradient(jax.ops.segment_max(e, dst, num_segments=n_nodes))[dst]
            ex = jnp.exp(e - emax)
            denom = jax.ops.segment_sum(ex, dst, num_segments=n_nodes)[dst]
            alpha = ex / denom
            msg = h[src] * alpha[:, :, None]
            out = jax.ops.segment_sum(msg, dst, num_segments=n_nodes)
            return out.reshape(n_nodes, heads * feats) + b
        key = jax.random.key(seed)
        ks = jax.random.split(key, 12)
        s = 0.05
        return {'node_feats': jax.random.normal(ks[0], (N, D_IN), dtype=jnp.float32), 'edge_index': jax.random.randint(ks[1], (2, E), 0, N, dtype=jnp.int64), 'W1': jax.random.normal(ks[2], (D_IN, H1 * F1), dtype=jnp.float32) * s, 'a_src1': jax.random.normal(ks[3], (H1, F1), dtype=jnp.float32) * s, 'a_dst1': jax.random.normal(ks[4], (H1, F1), dtype=jnp.float32) * s, 'b1': jnp.zeros((H1 * F1,), dtype=jnp.float32), 'W2': jax.random.normal(ks[5], (H1 * F1, H2 * F2), dtype=jnp.float32) * s, 'a_src2': jax.random.normal(ks[6], (H2, F2), dtype=jnp.float32) * s, 'a_dst2': jax.random.normal(ks[7], (H2, F2), dtype=jnp.float32) * s, 'b2': jnp.zeros((H2 * F2,), dtype=jnp.float32)}
    _L1_gnn_all = _L1_gnn_setup()
    _L1_gnn_in = {k: v for k, v in _L1_gnn_all.items() if k in ('W1', 'a_src1', 'a_dst1', 'b1', 'W2', 'a_src2', 'a_dst2', 'b2')}
    del _L1_gnn_all

    def _L1_mix_setup():
        import jax, jax.numpy as jnp
        import numpy as np
        A, Bc, Cc = (0.5, 1.0, 1.0)
        H = 8
        EPS = 1e-12

        def _normalize(t):
            n = jnp.linalg.norm(t, axis=-1, keepdims=True)
            return t / jnp.maximum(n, EPS)
        key = jax.random.key(seed)
        ks = jax.random.split(key, 5)
        B, N, C = (8, 64, 256)
        D = C // H
        x = jax.random.normal(ks[0], (B, N, C), dtype=jnp.float32)
        Wqkv = jax.random.normal(ks[1], (3 * H * D, C), dtype=jnp.float32) * 0.02
        bqkv = jnp.zeros((3 * H * D,), dtype=jnp.float32)
        Wproj = jax.random.normal(ks[2], (C, H * D), dtype=jnp.float32) * 0.02
        bproj = jnp.zeros((C,), dtype=jnp.float32)
        temperature = jnp.ones((1, H, 1, 1), dtype=jnp.float32)
        return {'x': x, 'Wqkv': Wqkv, 'bqkv': bqkv, 'Wproj': Wproj, 'bproj': bproj, 'temperature': temperature}
    _L1_mix_all = _L1_mix_setup()
    _L1_mix_in = {k: v for k, v in _L1_mix_all.items() if k in ('Wqkv', 'bqkv', 'Wproj', 'bproj', 'temperature')}
    del _L1_mix_all

    def _L1_ffn_setup():
        import jax, jax.numpy as jnp
        import numpy as np
        B, S, H, F, E, K = (8, 128, 256, 512, 16, 2)
        EPS = 1e-05
        key = jax.random.key(seed)
        ks = jax.random.split(key, 9)
        sc = 0.02
        return {'x': jax.random.normal(ks[0], (B, S, H), dtype=jnp.float32), 'gate_w': jax.random.normal(ks[1], (H, E), dtype=jnp.float32) * sc, 'gate_b': jnp.zeros((E,), dtype=jnp.float32), 'w1': jax.random.normal(ks[2], (E, H, F), dtype=jnp.float32) * sc, 'b1': jnp.zeros((E, F), dtype=jnp.float32), 'w2': jax.random.normal(ks[3], (E, F, H), dtype=jnp.float32) * sc, 'b2': jnp.zeros((E, H), dtype=jnp.float32), 'gamma': jnp.ones((H,), dtype=jnp.float32), 'beta': jnp.zeros((H,), dtype=jnp.float32)}
    _L1_ffn_all = _L1_ffn_setup()
    _L1_ffn_in = {k: v for k, v in _L1_ffn_all.items() if k in ('gate_w', 'gate_b', 'w1', 'b1', 'w2', 'b2', 'gamma', 'beta')}
    del _L1_ffn_all
    return {'x': x, 'src': src, 'dst': dst, 'edge_weight': edge_weight, 'L0_gnn_W': _L0_gnn_in['W'], 'L0_gnn_a_self': _L0_gnn_in['a_self'], 'L0_gnn_a_neigh': _L0_gnn_in['a_neigh'], 'L0_gnn_bias': _L0_gnn_in['bias'], 'L0_mix_Wq': _L0_mix_in['Wq'], 'L0_mix_bq': _L0_mix_in['bq'], 'L0_mix_Wk': _L0_mix_in['Wk'], 'L0_mix_bk': _L0_mix_in['bk'], 'L0_mix_Wv': _L0_mix_in['Wv'], 'L0_mix_bv': _L0_mix_in['bv'], 'L0_mix_Wo': _L0_mix_in['Wo'], 'L0_mix_bo': _L0_mix_in['bo'], 'L0_mix_proj': _L0_mix_in['proj'], 'L0_mix_W1': _L0_mix_in['W1'], 'L0_mix_bias1': _L0_mix_in['bias1'], 'L0_mix_W2': _L0_mix_in['W2'], 'L0_mix_bias2': _L0_mix_in['bias2'], 'L0_mix_g1': _L0_mix_in['g1'], 'L0_mix_beta1': _L0_mix_in['beta1'], 'L0_mix_g2': _L0_mix_in['g2'], 'L0_mix_beta2': _L0_mix_in['beta2'], 'L0_ffn_attention_mask': _L0_ffn_in['attention_mask'], 'L0_ffn_wr': _L0_ffn_in['wr'], 'L0_ffn_br': _L0_ffn_in['br'], 'L0_ffn_w1': _L0_ffn_in['w1'], 'L0_ffn_b1': _L0_ffn_in['b1'], 'L0_ffn_w2': _L0_ffn_in['w2'], 'L0_ffn_b2': _L0_ffn_in['b2'], 'L1_gnn_W1': _L1_gnn_in['W1'], 'L1_gnn_a_src1': _L1_gnn_in['a_src1'], 'L1_gnn_a_dst1': _L1_gnn_in['a_dst1'], 'L1_gnn_b1': _L1_gnn_in['b1'], 'L1_gnn_W2': _L1_gnn_in['W2'], 'L1_gnn_a_src2': _L1_gnn_in['a_src2'], 'L1_gnn_a_dst2': _L1_gnn_in['a_dst2'], 'L1_gnn_b2': _L1_gnn_in['b2'], 'L1_mix_Wqkv': _L1_mix_in['Wqkv'], 'L1_mix_bqkv': _L1_mix_in['bqkv'], 'L1_mix_Wproj': _L1_mix_in['Wproj'], 'L1_mix_bproj': _L1_mix_in['bproj'], 'L1_mix_temperature': _L1_mix_in['temperature'], 'L1_ffn_gate_w': _L1_ffn_in['gate_w'], 'L1_ffn_gate_b': _L1_ffn_in['gate_b'], 'L1_ffn_w1': _L1_ffn_in['w1'], 'L1_ffn_b1': _L1_ffn_in['b1'], 'L1_ffn_w2': _L1_ffn_in['w2'], 'L1_ffn_b2': _L1_ffn_in['b2'], 'L1_ffn_gamma': _L1_ffn_in['gamma'], 'L1_ffn_beta': _L1_ffn_in['beta']}

def reference(x, src, dst, edge_weight, L0_gnn_W, L0_gnn_a_self, L0_gnn_a_neigh, L0_gnn_bias, L0_mix_Wq, L0_mix_bq, L0_mix_Wk, L0_mix_bk, L0_mix_Wv, L0_mix_bv, L0_mix_Wo, L0_mix_bo, L0_mix_proj, L0_mix_W1, L0_mix_bias1, L0_mix_W2, L0_mix_bias2, L0_mix_g1, L0_mix_beta1, L0_mix_g2, L0_mix_beta2, L0_ffn_attention_mask, L0_ffn_wr, L0_ffn_br, L0_ffn_w1, L0_ffn_b1, L0_ffn_w2, L0_ffn_b2, L1_gnn_W1, L1_gnn_a_src1, L1_gnn_a_dst1, L1_gnn_b1, L1_gnn_W2, L1_gnn_a_src2, L1_gnn_a_dst2, L1_gnn_b2, L1_mix_Wqkv, L1_mix_bqkv, L1_mix_Wproj, L1_mix_bproj, L1_mix_temperature, L1_ffn_gate_w, L1_ffn_gate_b, L1_ffn_w1, L1_ffn_b1, L1_ffn_w2, L1_ffn_b2, L1_ffn_gamma, L1_ffn_beta):
    import jax
    import jax.numpy as jnp

    def _L0_gnn_ref(x, W, a_self, a_neigh, bias, adj_val, edge_row, edge_col):
        import jax, jax.numpy as jnp
        import numpy as np
        N_NODES = 50000
        N_EDGES = 25000
        F_IN = 256
        F_OUT = 64
        HEADS = 4
        LEAKY_ALPHA = 0.2
        N = x.shape[0]
        feats = jnp.einsum('nf,hfo->hno', x, W)
        s_self = jnp.einsum('hno,ho->hn', feats, a_self)
        s_neigh = jnp.einsum('hno,ho->hn', feats, a_neigh)
        z = s_self[:, edge_row] + s_neigh[:, edge_col]
        e = jnp.where(z > 0, z, LEAKY_ALPHA * z) * adj_val[None, :]

        def seg_softmax(e_h):
            m = jax.ops.segment_max(e_h, edge_row, num_segments=N)
            ex = jnp.exp(e_h - m[edge_row])
            s = jax.ops.segment_sum(ex, edge_row, num_segments=N)
            return ex / s[edge_row]
        alpha = jax.vmap(seg_softmax)(e)

        def aggregate(alpha_h, feat_h):
            return jax.ops.segment_sum(alpha_h[:, None] * feat_h[edge_col], edge_row, num_segments=N)
        out = jax.vmap(aggregate)(alpha, feats) + bias[:, None, :]
        out = jnp.transpose(out, (1, 0, 2)).reshape(N, -1)
        return jax.nn.relu(out)

    def _L0_mix_ref(inputs, Wq, bq, Wk, bk, Wv, bv, Wo, bo, proj, W1, bias1, W2, bias2, g1, beta1, g2, beta2):
        import jax, jax.numpy as jnp
        import numpy as np
        B, S, D = (8, 64, 256)
        H, KD = (8, 256)
        M = 256
        EPS_LN = 1e-06
        EPS_ATT = 1e-06

        def _layernorm(x, g, b):
            mu = jnp.mean(x, axis=-1, keepdims=True)
            var = jnp.mean(jnp.square(x - mu), axis=-1, keepdims=True)
            return (x - mu) * jax.lax.rsqrt(var + EPS_LN) * g + b

        def _phi(x, proj):
            u = jnp.einsum('bshd,md->bshm', x, proj)
            sq = 0.5 * jnp.sum(jnp.square(x), axis=-1, keepdims=True)
            return jnp.exp(u - sq) * (1.0 / np.sqrt(M)) + EPS_ATT
        scale = KD ** (-0.25)
        q = (jnp.einsum('bsd,dhk->bshk', inputs, Wq) + bq) * scale
        k = (jnp.einsum('bsd,dhk->bshk', inputs, Wk) + bk) * scale
        v = jnp.einsum('bsd,dhk->bshk', inputs, Wv) + bv
        phi_q = _phi(q, proj)
        phi_k = _phi(k, proj)
        kv = jnp.einsum('bshm,bshk->bhmk', phi_k, v)
        z = jnp.einsum('bshm,bhm->bsh', phi_q, phi_k.sum(axis=1))
        attn = jnp.einsum('bshm,bhmk->bshk', phi_q, kv) / z[..., None]
        attn_out = jnp.einsum('bshk,hkd->bsd', attn, Wo) + bo
        out1 = _layernorm(inputs + attn_out, g1, beta1)
        h = jax.nn.relu(out1 @ W1 + bias1)
        ffn_out = h @ W2 + bias2
        return _layernorm(out1 + ffn_out, g2, beta2)

    def _L0_ffn_ref(x, attention_mask, wr, br, w1, b1, w2, b2):
        import jax, jax.numpy as jnp
        import numpy as np
        B, S, D = (8, 128, 256)
        H = 4 * D
        CAPACITY = 0.5
        b, s, d = x.shape
        weights = (jnp.einsum('bsd,do->bso', x, wr) + br)[..., 0]
        k = max(1, int(CAPACITY * s))
        kk = k - 1 if k > 1 else 1
        _, idx = jax.lax.top_k(weights, k)
        sel_idx = idx[:, :kk]
        sel = jnp.take_along_axis(x, sel_idx[:, :, None], axis=1)
        h = jax.nn.gelu(jnp.einsum('bkd,dh->bkh', sel, w1) + b1)
        y = jnp.einsum('bkh,hd->bkd', h, w2) + b2
        w_sel = jnp.take_along_axis(weights, sel_idx, axis=1)
        y = y * w_sel[..., None]
        batch_idx = jnp.arange(b)[:, None]
        processed = jnp.zeros_like(x).at[batch_idx, sel_idx].set(y)
        return processed + x

    def _L1_gnn_ref(node_feats, edge_index, W1, a_src1, a_dst1, b1, W2, a_src2, a_dst2, b2):
        import jax, jax.numpy as jnp
        import numpy as np
        N, E = (50000, 25000)
        D_IN, H1, F1 = (256, 4, 64)
        H2, F2 = (1, 256)
        NEG_SLOPE = 0.2

        def gat_conv(x, src, dst, W, a_src, a_dst, b, heads, feats, n_nodes):
            h = (x @ W).reshape(n_nodes, heads, feats)
            s_src = jnp.einsum('nhf,hf->nh', h, a_src)
            s_dst = jnp.einsum('nhf,hf->nh', h, a_dst)
            e = jax.nn.leaky_relu(s_src[src] + s_dst[dst], NEG_SLOPE)
            emax = jax.lax.stop_gradient(jax.ops.segment_max(e, dst, num_segments=n_nodes))[dst]
            ex = jnp.exp(e - emax)
            denom = jax.ops.segment_sum(ex, dst, num_segments=n_nodes)[dst]
            alpha = ex / denom
            msg = h[src] * alpha[:, :, None]
            out = jax.ops.segment_sum(msg, dst, num_segments=n_nodes)
            return out.reshape(n_nodes, heads * feats) + b
        src, dst = (edge_index[0], edge_index[1])
        n = node_feats.shape[0]
        x = jax.nn.relu(gat_conv(node_feats, src, dst, W1, a_src1, a_dst1, b1, H1, F1, n))
        x = jax.nn.relu(gat_conv(x, src, dst, W2, a_src2, a_dst2, b2, H2, F2, n))
        return x

    def _L1_mix_ref(x, Wqkv, bqkv, Wproj, bproj, temperature):
        import jax, jax.numpy as jnp
        import numpy as np
        A, Bc, Cc = (0.5, 1.0, 1.0)
        H = 8
        EPS = 1e-12

        def _normalize(t):
            n = jnp.linalg.norm(t, axis=-1, keepdims=True)
            return t / jnp.maximum(n, EPS)
        B, N, C = x.shape
        D = C // H
        scale = float(D) ** 0.25
        qkv = (x @ Wqkv.T + bqkv).reshape(B, N, 3, H, D)
        qkv = jnp.transpose(qkv, (2, 0, 3, 1, 4))
        q, k, v = (qkv[0], qkv[1], qkv[2])
        q = q * scale
        v1 = jnp.concatenate([jnp.ones((B, H, N, 1), dtype=v.dtype), v], axis=-1)
        qn = _normalize(q) * (scale * temperature)
        kn = _normalize(k) * scale
        vN = v1 / N
        kv_mod = jnp.einsum('bhni,bhnj,bhne->bhije', kn, kn, vN)
        kv = jnp.einsum('bhnd,bhne->bhde', kn, vN)
        vsum = jnp.sum(vN, axis=-2)[:, :, None, :]
        y = A * jnp.einsum('bhni,bhnj,bhije->bhne', qn, qn, kv_mod) + scale ** 2 * Bc * jnp.einsum('bhnd,bhde->bhne', qn, kv) + scale ** 4 * Cc * vsum
        y_norm, y = (y[..., :1], y[..., 1:])
        y = y / y_norm
        out = jnp.transpose(y, (0, 2, 1, 3)).reshape(B, N, H * D)
        return out @ Wproj.T + bproj

    def _L1_ffn_ref(x, gate_w, gate_b, w1, b1, w2, b2, gamma, beta):
        import jax, jax.numpy as jnp
        import numpy as np
        B, S, H, F, E, K = (8, 128, 256, 512, 16, 2)
        EPS = 1e-05
        gate_logits = x @ gate_w + gate_b
        topk_vals, topk_idx = jax.lax.top_k(gate_logits, K)
        topk_w = jax.nn.softmax(topk_vals, axis=-1)
        h = jax.nn.relu(jnp.einsum('bsh,ehf->bsef', x, w1) + b1)
        expert_out = jnp.einsum('bsef,efh->bseh', h, w2) + b2
        sel = jnp.take_along_axis(expert_out, topk_idx[:, :, :, None], axis=2)
        moe = jnp.sum(topk_w[..., None] * sel, axis=2)
        y = x + moe
        mu = jnp.mean(y, axis=-1, keepdims=True)
        var = jnp.var(y, axis=-1, keepdims=True)
        return (y - mu) / jnp.sqrt(var + EPS) * gamma + beta
    edge_index = jnp.stack([src, dst])
    xn = _layernorm(x, axis=-1)
    x = x + _L0_gnn_ref(xn, L0_gnn_W, L0_gnn_a_self, L0_gnn_a_neigh, L0_gnn_bias, edge_weight, src, dst) + _L0_mix_ref(xn[None], L0_mix_Wq, L0_mix_bq, L0_mix_Wk, L0_mix_bk, L0_mix_Wv, L0_mix_bv, L0_mix_Wo, L0_mix_bo, L0_mix_proj, L0_mix_W1, L0_mix_bias1, L0_mix_W2, L0_mix_bias2, L0_mix_g1, L0_mix_beta1, L0_mix_g2, L0_mix_beta2)[0]
    x = x + _L0_ffn_ref(_layernorm(x, axis=-1)[None], L0_ffn_attention_mask, L0_ffn_wr, L0_ffn_br, L0_ffn_w1, L0_ffn_b1, L0_ffn_w2, L0_ffn_b2)[0]
    xn = _layernorm(x, axis=-1)
    x = x + _L1_gnn_ref(xn, edge_index, L1_gnn_W1, L1_gnn_a_src1, L1_gnn_a_dst1, L1_gnn_b1, L1_gnn_W2, L1_gnn_a_src2, L1_gnn_a_dst2, L1_gnn_b2) + _L1_mix_ref(xn[None], L1_mix_Wqkv, L1_mix_bqkv, L1_mix_Wproj, L1_mix_bproj, L1_mix_temperature)[0]
    x = x + _L1_ffn_ref(_layernorm(x, axis=-1)[None], L1_ffn_gate_w, L1_ffn_gate_b, L1_ffn_w1, L1_ffn_b1, L1_ffn_w2, L1_ffn_b2, L1_ffn_gamma, L1_ffn_beta)[0]
    return x

_drawn_inputs = setup_inputs


def setup_inputs(seed=0):
    import zlib

    import numpy as np

    out = dict(_drawn_inputs(seed))
    spreads = {'L0_gnn_bias': (0.0, 0.1),
     'L0_mix_bq': (0.0, 0.1),
     'L0_mix_bk': (0.0, 0.1),
     'L0_mix_bv': (0.0, 0.1),
     'L0_mix_bo': (0.0, 0.1),
     'L0_mix_bias1': (0.0, 0.1),
     'L0_mix_bias2': (0.0, 0.1),
     'L0_mix_g1': (1.0, 0.2),
     'L0_mix_beta1': (0.0, 0.1),
     'L0_mix_g2': (1.0, 0.2),
     'L0_mix_beta2': (0.0, 0.1),
     'L0_ffn_b1': (0.0, 0.8),
     'L0_ffn_b2': (0.0, 0.8),
     'L1_gnn_b1': (0.0, 0.8),
     'L1_gnn_b2': (0.0, 0.323),
     'L1_mix_bqkv': (0.0, 0.713),
     'L1_mix_bproj': (0.0, 0.55),
     'L1_mix_temperature': (1.0, 0.6),
     'L1_ffn_gate_b': (0.0, 0.497),
     'L1_ffn_b1': (0.0, 0.8),
     'L1_ffn_b2': (0.0, 1.375),
     'L1_ffn_gamma': (1.0, 0.6),
     'L1_ffn_beta': (0.0, 0.329)}
    factors = {'edge_weight': 7.232,
     'L0_gnn_a_self': 8.0,
     'L0_gnn_a_neigh': 5.756,
     'L0_ffn_wr': 5.452,
     'L0_ffn_w1': 7.011,
     'L0_ffn_w2': 6.633,
     'L1_gnn_W1': 2.909,
     'L1_gnn_a_src1': 8.0,
     'L1_gnn_a_dst1': 8.0,
     'L1_gnn_a_src2': 8.0,
     'L1_gnn_a_dst2': 64.0,
     'L1_mix_Wqkv': 7.175,
     'L1_mix_Wproj': 4.422,
     'L1_ffn_w1': 3.57,
     'L1_ffn_w2': 2.837}
    for name, (base, spread) in spreads.items():
        noise = np.random.default_rng([zlib.crc32(name.encode()), seed]).standard_normal(out[name].shape)
        drawn = base * np.exp(spread * noise) if base else spread * noise
        out[name] = jnp.asarray(drawn.astype(out[name].dtype))
    for name, factor in factors.items():
        out[name] = (out[name] * factor).astype(out[name].dtype)
    return out
```

```python
import numpy as np
import concourse.bass as bass
from concourse import mybir
from contextlib import ExitStack

FP32 = mybir.dt.float32
BF16 = mybir.dt.bfloat16
I32 = mybir.dt.int32
U32 = mybir.dt.uint32
ALU = mybir.AluOpType
ACT = mybir.ActivationFunctionType
AX = mybir.AxisListType

N, D = 3125, 256
ROWS = 125
TILES = N // ROWS
SLOTS = TILES + 1
NE = 53125
ECOLS = 416
LAST = NE - 127 * ECOLS
CHUNKS = 448
SET = 8
BIG = 2.0 ** 120
HG = 4
H, KD = 8, 256
KSCALE = KD ** -0.25
KK = 1561
HID = 1024
HD = 32
OFFS = HD // 2 + 1
FEAT = 640
QUAD = OFFS * HD
EXPERTS, EF = 16, 512


class Steps:

    def __init__(self, sem, names, lead=1):
        self.sem, self.names, self.lead, self.at = sem, list(names), lead, 0

    def prime(self, eng):
        eng.sem_inc(self.sem, self.lead * len(self.names))

    def did(self, name):
        assert self.names[self.at % len(self.names)] == name, (self.names[self.at % len(self.names)], name)
        self.at += 1
        return self.sem, 1

    def back(self, t, rounds, name):
        assert rounds <= self.lead
        return self.sem, t * len(self.names) + ((self.lead - rounds) * len(self.names) + self.names.index(name) + 1)

    def now(self, t, name):
        return self.back(t, 0, name)

    def before(self, t, name):
        return self.back(t, 1, name)


class Build:

    def __init__(self, nc, ins, out):
        self.nc, self.ins, self.out = nc, ins, out
        self.count = 0
        self.used = []

    def sem(self, ctx, name):
        self.count += 1
        self.used.append(ctx.enter_context(self.nc.semaphore(f"{name}_{self.count}")))
        return self.used[-1]

    def sem_of_gathers(self, name):
        self.count += 1
        return self.whole.enter_context(self.nc.semaphore(f"{name}_{self.count}"))

    def sb(self, ctx, name, shape, dt=FP32):
        self.count += 1
        return ctx.enter_context(self.nc.sbuf_tensor(f"{name}_{self.count}", shape, dt))

    def dram(self, name, shape, dt=FP32):
        return self.nc.dram_tensor(name, shape, dt, kind="Internal").ap()


def constants(b, ctx):
    nc = b.nc
    b.x = b.sb(ctx, "x", [ROWS, TILES, D])
    b.ident = b.sb(ctx, "ident", [128, 128])
    b.identb = b.sb(ctx, "identb", [128, 128], BF16)
    b.before_me = b.sb(ctx, "before_me", [128, 128])
    b.ones = b.sb(ctx, "ones", [128, 128])
    b.onesb = b.sb(ctx, "onesb", [128, 128], BF16)
    b.row_no = b.sb(ctx, "row_no", [128, CHUNKS])
    b.half = b.sb(ctx, "half", [128, 1])
    b.ps = ctx.enter_context(nc.psum_tensor("ps", [128, 8, 512], FP32))
    b.table = [b.dram(f"table{i}", [SLOTS * ROWS, D]) for i in range(3)]
    b.score = [b.dram(f"score{i}", [SLOTS * ROWS, heads]) for i, heads in enumerate((HG, HG, 1))]
    zeros = b.sb(ctx, "zeros", [ROWS, D])
    with ExitStack() as c:
        pool_did = b.sem(c, "const_pool")
        dve_did = b.sem(c, "const_dve")
        loaded = b.sem(c, "x_loaded")
        stored = b.sem(c, "zeros_stored")
        block = c.enter_context(nc.Block())

        @block.sync
        def _(sp):
            sp.dma_start(b.x[:], b.ins["x"].rearrange("(t p) d -> p t d", p=ROWS)).then_inc(loaded, 16)
            sp.wait_ge(dve_did, 4)
            for i in range(3):
                sp.dma_start(b.table[i][N:SLOTS * ROWS, :], zeros[:]).then_inc(stored, 16)
                sp.dma_start(b.score[i][N:SLOTS * ROWS, :], zeros[:, 0:(HG, HG, 1)[i]]).then_inc(stored, 16)
            sp.wait_ge(stored, 96)
            sp.wait_ge(loaded, 16)

        @block.vector
        def _(dve):
            dve.memset(b.ones[:], 1.0).then_inc(dve_did, 1)
            dve.memset(b.onesb[:], 1.0).then_inc(dve_did, 1)
            dve.memset(b.half[:], -0.5).then_inc(dve_did, 1)
            dve.memset(zeros[:], 0.0).then_inc(dve_did, 1)
            dve.wait_ge(pool_did, 2)
            dve.tensor_copy(b.identb[:], b.ident[:]).then_inc(dve_did, 1)

        @block.gpsimd
        def _(pool):
            pool.memset(b.ident[:], 0.0).then_inc(pool_did, 1)
            pool.wait_ge(pool_did, 1)
            pool.affine_select(out=b.ident[:], in_=b.ident[:], compare_op=ALU.not_equal, fill=1.0, base=0,
                               pattern=[[-1, 128]], channel_multiplier=1).then_inc(pool_did, 1)
            pool.wait_ge(dve_did, 1)
            pool.affine_select(out=b.before_me[:], in_=b.ones[:], compare_op=ALU.is_gt, fill=0.0, base=0,
                               pattern=[[1, 128]], channel_multiplier=-1).then_inc(pool_did, 1)
            pool.iota(b.row_no[:], [[1, CHUNKS]], base=0, channel_multiplier=0,
                      allow_small_or_imprecise_dtypes=True).then_inc(pool_did, 1)


def sort_edges(b, ctx, which, key_name, nbr_name, weighted):
    nc, ps = b.nc, b.ps
    got = {
        "nbr": b.sb(ctx, "nbr", [128, CHUNKS], I32),
        "lane": b.sb(ctx, "lane", [128, CHUNKS]),
        "tile": b.sb(ctx, "tile", [1, CHUNKS], I32),
        "w": b.sb(ctx, "w", [128, CHUNKS]) if weighted else None,
    }
    listed = b.dram(f"listed{which}", [128 * CHUNKS, 4])
    with ExitStack() as c:
        raw = b.sb(c, "raw", [128, 2, ECOLS], I32)
        rec = b.sb(c, "rec", [128, ECOLS, 4])
        key = b.sb(c, "key", [128, ECOLS])
        start = b.sb(c, "start", [128, SLOTS + 1])
        ge = b.sb(c, "ge", [128, ECOLS])
        inside = b.sb(c, "inside", [128, SLOTS, ECOLS], BF16)
        upto = b.sb(c, "upto", [128, SLOTS, ECOLS])
        small = b.sb(c, "small", [128, 8, SLOTS])
        smalli = b.sb(c, "smalli", [128, SLOTS], I32)
        zero = b.sb(c, "zero", [128, ECOLS])
        pos = b.sb(c, "pos", [128, ECOLS])
        part = b.sb(c, "part", [128, ECOLS])
        posi = b.sb(c, "posi", [128, 3, ECOLS], I32)
        pad = b.sb(c, "pad", [128, CHUNKS, 4])
        back = b.sb(c, "back", [128, CHUNKS, 4])
        tilef = b.sb(c, "tilef", [128, CHUNKS])
        stage = b.sb(c, "stage", [128, 2, SET, 4])
        stagep = b.sb(c, "stagep", [128, 2, SET], I32)
        loaded, dve_did = b.sem(c, "edges_loaded"), b.sem(c, "sort_dve")
        pe_did, pool_did, padded = b.sem(c, "sort_pe"), b.sem(c, "sort_pool"), b.sem(c, "padded")
        ready = b.sem(c, "slots_ready")
        scattered = [b.sem_of_gathers(f"scattered{i}") for i in range(2)]
        relisted = b.sem(c, "relisted")
        staged, stage_free = b.sem(c, "staged"), b.sem(c, "stage_free")
        block = c.enter_context(nc.Block())
        links = [0]

        @block.sync
        def _(sp):
            sp.wait_ge(pool_did, 3)
            k = 0
            for i, name in enumerate((key_name, nbr_name)):
                src = b.ins[name]
                sp.dma_start(raw[0:127, i, :], src[0:127 * ECOLS].rearrange("(p c) -> p c", c=ECOLS)).then_inc(loaded, 16)
                sp.dma_start(raw[127:128, i, 0:LAST], src[127 * ECOLS:NE].unsqueeze(0)).then_inc(loaded, 16)
                k += 32
            if weighted:
                src = b.ins["edge_weight"]
                sp.dma_start(ge[0:127, :], src[0:127 * ECOLS].rearrange("(p c) -> p c", c=ECOLS)).then_inc(loaded, 16)
                sp.dma_start(ge[127:128, 0:LAST], src[127 * ECOLS:NE].unsqueeze(0)).then_inc(loaded, 16)
            sp.wait_ge(pool_did, 5)
            sp.dma_start(listed.rearrange("(p c) f -> p (c f)", p=128), pad[:].rearrange("p c f -> p (c f)")).then_inc(padded, 16)
            sp.wait_ge(padded, 16)
            sp.sem_inc(stage_free, 2)
            with sp.Fori(0, ECOLS // (2 * SET)) as r:
                for i in range(2):
                    sp.wait_ge(scattered[i], r * (SET * 16) + SET * 16)
                    sp.sem_inc(stage_free, 1)
            sp.dma_start(back[:].rearrange("p c f -> p (c f)"), listed.rearrange("(p c) f -> p (c f)", p=128)).then_inc(relisted, 16)
            sp.wait_ge(relisted, 16)

        @block.gpsimd
        def _(pool):
            pool.memset(raw[:], N).then_inc(pool_did, 1)
            pool.iota(start[:], [[ROWS, SLOTS + 1]], base=0, channel_multiplier=0,
                      allow_small_or_imprecise_dtypes=True).then_inc(pool_did, 1)
            pool.memset(ge[:], 0.0).then_inc(pool_did, 1)
            pool.memset(pad[:, :, 0:2], float(N)).then_inc(pool_did, 1)
            pool.memset(pad[:, :, 2:4], 0.0).then_inc(pool_did, 1)
            pool.wait_ge(ready, 1)
            pool.wait_ge(padded, 16)
            with pool.Fori(0, ECOLS // (2 * SET)) as r:
                for i in range(2):
                    pool.wait_ge(stage_free, r * 2 + (i + 1))
                    pool.tensor_copy(stage[:, i], rec[:, bass.ds(r * (2 * SET) + i * SET, SET), :]).then_inc(pool_did, 1)
                    pool.tensor_copy(stagep[:, i], posi[:, 2, bass.ds(r * (2 * SET) + i * SET, SET)]).then_inc(pool_did, 1)
                    pool.wait_ge(pool_did, r * 4 + (5 + 2 * i + 2))
                    pool.sem_inc(staged, 1)
                    for j in range(SET):
                        pool.indirect_dma_start(listed[:, :], bass.IndirectOffsetOnAxis(ap=stagep[:, i, j:j + 1], axis=0),
                                                stage[:, i, j, :], None).then_inc(scattered[i], 16)

        @block.tensor
        def _(pe):
            pe.wait_ge(dve_did, 4 + 3 * SLOTS + 1)
            pe.matmul(ps[:, 0, 0:SLOTS], lhsT=b.before_me[:], rhs=small[:, 0, :], start=True, stop=True).then_inc(pe_did, 1)
            pe.matmul(ps[:, 1, 0:SLOTS], lhsT=b.ones[:], rhs=small[:, 0, :], start=True, stop=True).then_inc(pe_did, 1)

        @block.vector
        def _(dve):
            def link(ins):
                links[0] += 1
                ins.then_inc(dve_did, 1)
                dve.wait_ge(dve_did, links[0])

            link(dve.memset(rec[:], 0.0))
            link(dve.memset(zero[:], 0.0))
            dve.wait_ge(loaded, 96 if weighted else 64)
            dve.wait_ge(pool_did, 2)
            link(dve.tensor_copy(rec[:, :, 0:2].rearrange("p c f -> p f c"), raw[:]))
            if weighted:
                link(dve.tensor_copy(rec[:, :, 2], ge[:]))
            else:
                link(dve.tensor_copy(rec[:, :, 2], zero[:]))
            base = links[0]
            with dve.Fori(0, SLOTS) as t:
                dve.tensor_scalar(ge[:], rec[:, :, 0], start[:, bass.ds(t, 1)], None, ALU.is_ge).then_inc(dve_did, 1)
                dve.wait_ge(dve_did, t * 3 + (base + 1))
                dve.scalar_tensor_tensor(out=inside[:, bass.ds(t, 1), :].rearrange("p a c -> p (a c)"), in0=rec[:, :, 0],
                                         scalar=start[:, bass.ds(t + 1, 1)], in1=ge[:], op0=ALU.is_lt,
                                         op1=ALU.mult).then_inc(dve_did, 1)
                dve.wait_ge(dve_did, t * 3 + (base + 2))
                dve.tensor_tensor_scan(upto[:, bass.ds(t, 1), :].rearrange("p a c -> p (a c)"), zero[:],
                                       inside[:, bass.ds(t, 1), :].rearrange("p a c -> p (a c)"), 0.0, ALU.add,
                                       ALU.add).then_inc(dve_did, 1)
                dve.wait_ge(dve_did, t * 3 + (base + 3))
            links[0] = base + 3 * SLOTS
            link(dve.tensor_copy(small[:, 0, :], upto[:, :, ECOLS - 1]))
            dve.wait_ge(pe_did, 2)
            link(dve.tensor_scalar(smalli[:], ps[:, 1, 0:SLOTS], 127.0, None, ALU.add))
            link(dve.tensor_scalar(smalli[:], smalli[:], 7, None, ALU.arith_shift_right))
            link(dve.tensor_copy(small[:, 1, :], smalli[:]))
            link(dve.tensor_tensor_scan(small[:, 2, :], zero[:, 0:SLOTS], small[:, 1, :], 0.0, ALU.add, ALU.add))
            link(dve.tensor_tensor(small[:, 3, :], small[:, 2, :], small[:, 1, :], ALU.subtract))
            link(dve.tensor_scalar(small[:, 4, :], small[:, 3, :], 128.0, -1.0, ALU.mult, ALU.add))
            link(dve.tensor_tensor(small[:, 5, :], small[:, 4, :], ps[:, 0, 0:SLOTS], ALU.add))
            link(dve.memset(pos[:], 0.0))
            link(dve.memset(tilef[:], 0.0))
            base = links[0]
            with dve.Fori(0, SLOTS) as t:
                dve.scalar_tensor_tensor(out=part[:], in0=upto[:, bass.ds(t, 1), :].rearrange("p a c -> p (a c)"),
                                         scalar=small[:, 5, bass.ds(t, 1)],
                                         in1=inside[:, bass.ds(t, 1), :].rearrange("p a c -> p (a c)"), op0=ALU.add,
                                         op1=ALU.mult).then_inc(dve_did, 1)
                dve.wait_ge(dve_did, t * 3 + (base + 1))
                dve.tensor_tensor(pos[:], pos[:], part[:], ALU.add).then_inc(dve_did, 1)
                dve.scalar_tensor_tensor(out=tilef[:], in0=b.row_no[:], scalar=small[:, 2, bass.ds(t, 1)], in1=tilef[:],
                                         op0=ALU.is_ge, op1=ALU.add).then_inc(dve_did, 1)
                dve.wait_ge(dve_did, t * 3 + (base + 3))
            links[0] = base + 3 * SLOTS
            link(dve.tensor_copy(posi[:, 0, :], pos[:]))
            link(dve.tensor_scalar(posi[:, 1, :], posi[:, 0, :], 7, None, ALU.arith_shift_right))
            link(dve.tensor_scalar(posi[:, 0, :], posi[:, 0, :], 127, None, ALU.bitwise_and))
            link(dve.tensor_copy(pos[:], posi[:, 0, :]))
            link(dve.tensor_copy(part[:], posi[:, 1, :]))
            link(dve.scalar_tensor_tensor(out=pos[:], in0=pos[:], scalar=float(CHUNKS), in1=part[:], op0=ALU.mult, op1=ALU.add))
            link(dve.tensor_copy(posi[:, 2, :], pos[:]))
            link(dve.tensor_scalar(tilef[:], tilef[:], float(TILES), None, ALU.min))
            dve.tensor_copy(got["tile"][:], tilef[0:1, :]).then_inc(ready, 1)
            dve.wait_ge(relisted, 16)
            link(dve.tensor_copy(got["nbr"][:], back[:, :, 1]))
            link(dve.scalar_tensor_tensor(out=got["lane"][:], in0=tilef[:], scalar=-float(ROWS), in1=back[:, :, 0],
                                          op0=ALU.mult, op1=ALU.add))
            if weighted:
                link(dve.tensor_copy(got["w"][:], back[:, :, 2]))
    return got


def other(steps, r, i, name):
    return steps.now(r, name.format(0)) if i else steps.before(r, name.format(1))


class RowNorm:

    def __init__(self, b, ctx, dve, pool, tag=""):
        self.b, self.dve, self.pool, self.tag = b, dve, pool, tag
        self.stats = b.sb(ctx, "stats", [ROWS, 6])
        self.mean = b.sb(ctx, "mean", [ROWS, 2])
        self.root = b.sb(ctx, "root", [ROWS, 1])
        self.passed = b.sem(ctx, "stats_passed")

    @staticmethod
    def steps(tag=""):
        return [tag + "stats", tag + "mean", tag + "eps"]

    def vector(self, v, t, row, eps):
        dve, tag = self.dve, self.tag
        v.bn_stats(self.stats[:], row).then_inc(*dve.did(tag + "stats"))
        v.wait_ge(*dve.now(t, tag + "stats"))
        v.sem_inc(self.passed, 1)
        v.bn_aggr(self.mean[:], self.stats[:]).then_inc(*dve.did(tag + "mean"))
        v.wait_ge(*dve.now(t, tag + "mean"))
        v.tensor_scalar(self.mean[:, 1:2], self.mean[:, 1:2], eps, None, ALU.add).then_inc(*dve.did(tag + "eps"))
        v.wait_ge(*self.pool.now(t, tag + "root"))

    def gpsimd(self, p, t):
        p.wait_ge(*self.dve.now(t, self.tag + "eps"))
        p.tensor_tensor(self.root[:], self.mean[:, 1:2], self.b.half[0:ROWS, :], ALU.pow).then_inc(*self.pool.did(self.tag + "root"))

    def scaled(self, v, out, row):
        return v.tensor_scalar(out, row, self.mean[:, 0:1], self.root[:], ALU.subtract, ALU.mult)


def node_tables(b, ctx, which, source, layer_norm, weights, heads):
    nc, ps = b.nc, b.ps
    width = D + 2 * heads
    own = b.sb(ctx, "own", [ROWS, SLOTS * heads])
    table, score = b.table[which], b.score[which]
    with ExitStack() as c:
        dve = Steps(b.sem(c, "tab_dve"), (RowNorm.steps() if layer_norm else []) + ["xn"])
        pool = Steps(b.sem(c, "tab_pool"), ["root"])
        pe = Steps(b.sem(c, "tab_pe"), ["turn", "proj"])
        act = Steps(b.sem(c, "tab_act"), ["xt", "rows", "own"])
        stored, rows_free = b.sem(c, "tab_stored"), b.sem(c, "rows_free")
        cleared = b.sem(c, "tab_cleared")
        norm = RowNorm(b, c, dve, pool)
        xn = b.sb(c, "xn", [ROWS, D])
        xt = b.sb(c, "xt", [128, 2, ROWS])
        rows = b.sb(c, "rows", [ROWS, width])
        block = c.enter_context(nc.Block())

        @block.vector
        def _(v):
            dve.prime(v)
            v.memset(own[:, TILES * heads:], 0.0).then_inc(cleared, 1)
            with v.Fori(0, TILES) as t:
                x_t = source[:, bass.ds(t, 1), :].rearrange("p a d -> p (a d)")
                if layer_norm:
                    norm.vector(v, t, x_t, 1e-5)
                    v.wait_ge(*pe.before(t, "turn"))
                    norm.scaled(v, xn[:], x_t).then_inc(*dve.did("xn"))
                    v.wait_ge(*dve.now(t, "xn"))
                else:
                    v.wait_ge(*pe.before(t, "turn"))
                    v.tensor_scalar(xn[:], x_t, 1.0, None, ALU.mult).then_inc(*dve.did("xn"))

        @block.gpsimd
        def _(p):
            pool.prime(p)
            if layer_norm:
                with p.Fori(0, TILES) as t:
                    norm.gpsimd(p, t)

        @block.tensor
        def _(e):
            pe.prime(e)
            with e.Fori(0, TILES) as t:
                e.wait_ge(*dve.now(t, "xn"))
                e.wait_ge(*act.before(t, "xt"))
                e.transpose(ps[:, 0, 0:ROWS], xn[:, 0:128], b.ident[0:ROWS, 0:ROWS])
                e.transpose(ps[:, 0, ROWS:2 * ROWS], xn[:, 128:256], b.ident[0:ROWS, 0:ROWS]).then_inc(*pe.did("turn"))
                e.wait_ge(*act.now(t, "xt"))
                e.wait_ge(*act.before(t, "rows"))
                for k in range(2):
                    last = e.matmul(ps[0:ROWS, 1, 0:width], lhsT=xt[:, k, :], rhs=weights[:, k, :], start=k == 0, stop=k == 1)
                last.then_inc(*pe.did("proj"))

        @block.scalar
        def _(a):
            act.prime(a)
            with a.Fori(0, TILES) as t:
                a.wait_ge(*pe.now(t, "turn"))
                a.wait_ge(*pe.before(t, "proj"))
                a.activation(xt[:].rearrange("p k n -> p (k n)"), ps[:, 0, 0:2 * ROWS], ACT.Copy).then_inc(*act.did("xt"))
                a.wait_ge(*pe.now(t, "proj"))
                a.wait_ge(rows_free, t + 1)
                a.wait_ge(*act.before(t, "own"))
                a.activation(rows[:], ps[0:ROWS, 1, 0:width], ACT.Copy).then_inc(*act.did("rows"))
                a.wait_ge(*act.now(t, "rows"))
                a.activation(own[:, bass.ds(t * heads, heads)], rows[:, D:D + heads], ACT.Copy).then_inc(*act.did("own"))

        @block.sync
        def _(sp):
            sp.sem_inc(rows_free, 1)
            with sp.Fori(0, TILES) as t:
                sp.wait_ge(*act.now(t, "rows"))
                sp.dma_start(table[bass.ds(t * ROWS, ROWS), :], rows[:, 0:D]).then_inc(stored, 16)
                sp.dma_start(score[bass.ds(t * ROWS, ROWS), :], rows[:, D + heads:width]).then_inc(stored, 16)
                sp.wait_ge(stored, t * 32 + 32)
                sp.sem_inc(rows_free, 1)
    return own


def edge_scores(b, g, score, own, heads, e_all, top):
    nc, ps = b.nc, b.ps
    q = SET * heads
    sets = range(2)
    with ExitStack() as c:
        dve = Steps(b.sem(c, "sc_dve"), [n.format(i) for i in sets for n in
                    ["s{}_0", "s{}_1", "sum{}", "leak{}", "e{}", "hi{}", "r1{}", "mid{}", "r2{}", "lo{}"]
                    + [f"{m}{{}}_{j}" for j in range(SET) for m in ("red", "top")]])
        pe = Steps(b.sem(c, "sc_pe"), [n.format(i) for i in sets for n in
                   ["st{}_0", "st{}_1", "own{}", "et{}"] + [f"mx{{}}_{j}" for j in range(SET)]])
        act = Steps(b.sem(c, "sc_act"), [n.format(i) for i in sets for n in ["st{}_0", "st{}_1", "et{}"]])
        pool = Steps(b.sem(c, "sc_pool"), ["idx0", "idx1"])
        staged, const, consv = b.sem(c, "staged"), b.sem(c, "sc_const"), b.sem(c, "sc_consv")
        gathered = [b.sem_of_gathers(f"gathered{i}") for i in sets]
        idx = b.sb(c, "idx", [128, 2, SET], I32)
        got = b.sb(c, "got", [128, 2, SET, heads])
        sel = b.sb(c, "sel", [128, 2, SET, ROWS], BF16)
        selt = b.sb(c, "selt", [ROWS, SET, 128])
        z = b.sb(c, "z", [128, q])
        parts = b.sb(c, "parts", [128, 3, q], BF16)
        rest = b.sb(c, "rest", [128, q])
        partst = b.sb(c, "partst", [3 * q, 128], BF16)
        pick = b.sb(c, "pick", [3 * q, q, ROWS], BF16)
        bigi = b.sb(c, "bigi", [128, heads, 128], BF16)
        minus = b.sb(c, "minus", [1, heads * 128], BF16)
        red = b.sb(c, "red", [ROWS, heads])
        block = c.enter_context(nc.Block())

        @block.gpsimd
        def _(p):
            pool.prime(p)
            p.memset(pick[:], 0.0).then_inc(const, 1)
            for n in range(3):
                p.wait_ge(const, n + 1)
                p.affine_select(out=pick[:], in_=pick[:], compare_op=ALU.not_equal, fill=1.0, base=-q * n,
                                pattern=[[-1, q], [0, ROWS]], channel_multiplier=1).then_inc(const, 1)
            with p.Fori(0, CHUNKS // (2 * SET)) as r:
                for i in sets:
                    p.wait_ge(*dve.before(r, f"sum{i}"))
                    p.tensor_copy(idx[:, i], g["nbr"][:, bass.ds(r * (2 * SET) + i * SET, SET)]).then_inc(*pool.did(f"idx{i}"))
                    p.wait_ge(*pool.now(r, f"idx{i}"))
                    p.sem_inc(staged, 1)
                    for j in range(SET):
                        p.indirect_dma_start(got[:, i, j, :], None, score[:, :],
                                             bass.IndirectOffsetOnAxis(ap=idx[:, i, j:j + 1], axis=0)).then_inc(gathered[i], 16)

        @block.vector
        def _(v):
            dve.prime(v)
            v.memset(top[:], -BIG).then_inc(consv, 1)
            v.memset(minus[:], -BIG).then_inc(consv, 1)
            for h in range(heads):
                v.tensor_scalar(bigi[:, h, :], b.ident[:], BIG, None, ALU.mult).then_inc(consv, 1)
            v.wait_ge(consv, 2 + heads)
            tiles = [v.alloc_register(f"sc_v{which}{j}") for which in [b.count] for j in range(SET)]
            with v.Fori(0, CHUNKS // (2 * SET)) as r:
                for i in sets:
                    k0 = r * (2 * SET) + i * SET
                    v.wait_ge(*pe.before(r, f"mx{i}_{SET - 1}"))
                    for m in range(2):
                        v.tensor_tensor(sel[:, i, 4 * m:4 * m + 4, :],
                                        b.row_no[:, 0:ROWS].unsqueeze(1).to_broadcast([128, 4, ROWS]),
                                        g["lane"][:, bass.ds(k0 + 4 * m, 4)].unsqueeze(2).to_broadcast([128, 4, ROWS]),
                                        ALU.is_equal).then_inc(*dve.did(f"s{i}_{m}"))
                    v.reg_load(tiles, g["tile"][0:1, bass.ds(k0, SET)])
                    v.wait_ge(*pe.now(r, f"own{i}"))
                    v.wait_ge(gathered[i], (r + 1) * (SET * 16))
                    v.tensor_tensor(z[:], ps[:, 2 + i, 0:q], got[:, i].rearrange("p j h -> p (j h)"), ALU.add).then_inc(*dve.did(f"sum{i}"))
                    v.wait_ge(*dve.now(r, f"sum{i}"))
                    v.scalar_tensor_tensor(out=rest[:], in0=z[:], scalar=0.2, in1=z[:], op0=ALU.mult, op1=ALU.max).then_inc(*dve.did(f"leak{i}"))
                    v.wait_ge(*dve.now(r, f"leak{i}"))
                    e_k = e_all[:, bass.ds(k0, SET), 0:heads]
                    if g["w"] is not None:
                        v.tensor_tensor(e_k, rest[:].rearrange("p (j h) -> p j h", h=heads),
                                        g["w"][:, bass.ds(k0, SET)].unsqueeze(2).to_broadcast([128, SET, heads]),
                                        ALU.mult).then_inc(*dve.did(f"e{i}"))
                    else:
                        v.tensor_scalar(e_k, rest[:].rearrange("p (j h) -> p j h", h=heads), 1.0, None, ALU.mult).then_inc(*dve.did(f"e{i}"))
                    v.wait_ge(*dve.now(r, f"e{i}"))
                    v.wait_ge(*other(pe, r, i, "et{}"))
                    p3 = parts[:].rearrange("p n (j h) -> p n j h", h=heads)
                    r3 = rest[:].rearrange("p (j h) -> p j h", h=heads)
                    v.tensor_scalar(p3[:, 0], e_k, 1.0, None, ALU.mult).then_inc(*dve.did(f"hi{i}"))
                    v.wait_ge(*dve.now(r, f"hi{i}"))
                    v.tensor_tensor(r3, e_k, p3[:, 0], ALU.subtract).then_inc(*dve.did(f"r1{i}"))
                    v.wait_ge(*dve.now(r, f"r1{i}"))
                    v.tensor_copy(parts[:, 1], rest[:]).then_inc(*dve.did(f"mid{i}"))
                    v.wait_ge(*dve.now(r, f"mid{i}"))
                    v.tensor_tensor(rest[:], rest[:], parts[:, 1], ALU.subtract).then_inc(*dve.did(f"r2{i}"))
                    v.wait_ge(*dve.now(r, f"r2{i}"))
                    v.tensor_copy(parts[:, 2], rest[:]).then_inc(*dve.did(f"lo{i}"))
                    v.wait_ge(*dve.now(r, f"lo{i}"))
                    for j in range(SET):
                        tile = v.snap(tiles[j], min_val=0, max_val=TILES)
                        v.wait_ge(*pe.now(r, f"mx{i}_{j}"))
                        v.tensor_reduce(red[:], ps[0:ROWS, 5 + j % 2, 0:heads * 128].rearrange("p (h e) -> p h e", h=heads),
                                        AX.X, ALU.max).then_inc(*dve.did(f"red{i}_{j}"))
                        v.wait_ge(*dve.now(r, f"red{i}_{j}"))
                        top_k = top[:, bass.ds(tile * heads, heads)]
                        v.tensor_tensor(top_k, top_k, red[:], ALU.max).then_inc(*dve.did(f"top{i}_{j}"))
                        v.wait_ge(*dve.now(r, f"top{i}_{j}"))

        @block.tensor
        def _(e):
            pe.prime(e)
            e.wait_ge(const, 4)
            e.wait_ge(consv, 2 + heads)
            tiles = [e.alloc_register(f"sc_t{which}{j}") for which in [b.count] for j in range(SET)]
            turned = ps[:, 0:2, :].bitcast(BF16)
            with e.Fori(0, CHUNKS // (2 * SET)) as r:
                for i in sets:
                    k0 = r * (2 * SET) + i * SET
                    e.reg_load(tiles, g["tile"][0:1, bass.ds(k0, SET)])
                    for m in range(2):
                        e.wait_ge(*dve.now(r, f"s{i}_{m}"))
                        e.wait_ge(*other(act, r, i, f"st{{}}_{m}"))
                        for j in range(4):
                            last = e.transpose(turned[0:ROWS, m, 128 * j:128 * j + 128], sel[:, i, 4 * m + j, :], b.identb[:])
                        last.then_inc(*pe.did(f"st{i}_{m}"))
                    e.wait_ge(*act.now(r, f"st{i}_1"))
                    e.wait_ge(*dve.before(r, f"sum{i}"))
                    for j in range(SET):
                        tile = e.snap(tiles[j], min_val=0, max_val=TILES)
                        last = e.matmul(ps[:, 2 + i, j * heads:(j + 1) * heads], lhsT=selt[:, j, :],
                                        rhs=own[:, bass.ds(tile * heads, heads)], start=True, stop=True)
                    last.then_inc(*pe.did(f"own{i}"))
                    e.wait_ge(*dve.now(r, f"lo{i}"))
                    e.wait_ge(*other(act, r, i, "et{}"))
                    e.transpose(ps[0:3 * q, 4, :].bitcast(BF16)[:, 0:128], parts[:].rearrange("p n k -> p (n k)"),
                                b.identb[:]).then_inc(*pe.did(f"et{i}"))
                    e.wait_ge(*act.now(r, f"et{i}"))
                    for j in range(SET):
                        e.wait_ge(*(dve.now(r, f"red{i}_{j - 2}") if j >= 2 else other(dve, r, i, f"red{{}}_{SET - 2 + j}")))
                        bank = ps[0:ROWS, 5 + j % 2, 0:heads * 128]
                        e.matmul(bank, lhsT=b.onesb[0:1, 0:ROWS], rhs=minus[:], start=True, stop=False)
                        e.matmul(bank, lhsT=sel[:, i, j, :], rhs=bigi[:].rearrange("p h e -> p (h e)"), start=False, stop=False)
                        for h in range(heads):
                            last = e.matmul(bank[:, 128 * h:128 * h + 128], lhsT=pick[:, j * heads + h, :], rhs=partst[:],
                                            start=False, stop=h == heads - 1)
                        last.then_inc(*pe.did(f"mx{i}_{j}"))

        @block.scalar
        def _(a):
            act.prime(a)
            turned = ps[:, 0:2, :].bitcast(BF16)
            with a.Fori(0, CHUNKS // (2 * SET)) as r:
                for i in sets:
                    for m in range(2):
                        a.wait_ge(*pe.now(r, f"st{i}_{m}"))
                        if m == 0:
                            a.wait_ge(*other(pe, r, i, "own{}"))
                        a.activation(selt[:, 4 * m:4 * m + 4, :].rearrange("p j e -> p (j e)"), turned[0:ROWS, m, 0:512],
                                     ACT.Copy).then_inc(*act.did(f"st{i}_{m}"))
                    a.wait_ge(*pe.now(r, f"et{i}"))
                    a.wait_ge(*other(pe, r, i, f"mx{{}}_{SET - 1}"))
                    a.activation(partst[:], ps[0:3 * q, 4, :].bitcast(BF16)[:, 0:128], ACT.Copy).then_inc(*act.did(f"et{i}"))


def edge_sums(b, g, table, heads, e_all, top, acc):
    nc, ps = b.nc, b.ps
    q = SET * heads
    width = D + heads
    sets = range(2)
    with ExitStack() as c:
        dve = Steps(b.sem(c, "su_dve"), [n.format(i) for i in sets for n in
                    ["s{}_0", "s{}_1", "diff{}", "low{}", "msg{}_0", "msg{}_1"] + [f"acc{{}}_{j}" for j in range(SET)]])
        pe = Steps(b.sem(c, "su_pe"), [n.format(i) for i in sets for n in
                   ["st{}_0", "st{}_1", "top{}"] + [f"sum{{}}_{j}" for j in range(SET)]])
        act = Steps(b.sem(c, "su_act"), [n.format(i) for i in sets for n in ["st{}_0", "st{}_1", "ex{}"]])
        pool = Steps(b.sem(c, "su_pool"), ["idx0", "idx1"])
        staged, cleared = b.sem(c, "staged"), b.sem(c, "su_cleared")
        gathered = [b.sem_of_gathers(f"gathered{i}") for i in sets]
        idx = b.sb(c, "idx", [128, 2, SET], I32)
        got = b.sb(c, "got", [128, 2, SET, D])
        sel = b.sb(c, "sel", [128, 2, SET, ROWS])
        selt = b.sb(c, "selt", [ROWS, SET, 128])
        diff = b.sb(c, "diff", [128, 2, SET, heads])
        msg = b.sb(c, "msg", [128, 2, SET, width])
        block = c.enter_context(nc.Block())

        @block.gpsimd
        def _(p):
            pool.prime(p)
            with p.Fori(0, CHUNKS // (2 * SET)) as r:
                for i in sets:
                    p.wait_ge(*dve.before(r, f"msg{i}_1"))
                    p.tensor_copy(idx[:, i], g["nbr"][:, bass.ds(r * (2 * SET) + i * SET, SET)]).then_inc(*pool.did(f"idx{i}"))
                    p.wait_ge(*pool.now(r, f"idx{i}"))
                    p.sem_inc(staged, 1)
                    for j in range(SET):
                        p.indirect_dma_start(got[:, i, j, :], None, table[:, :],
                                             bass.IndirectOffsetOnAxis(ap=idx[:, i, j:j + 1], axis=0)).then_inc(gathered[i], 16)

        @block.vector
        def _(v):
            dve.prime(v)
            v.memset(acc[:], 0.0).then_inc(cleared, 1)
            v.wait_ge(cleared, 1)
            tiles = [v.alloc_register(f"su_v{which}{j}") for which in [b.count] for j in range(SET)]
            with v.Fori(0, CHUNKS // (2 * SET)) as r:
                for i in sets:
                    k0 = r * (2 * SET) + i * SET
                    v.wait_ge(*pe.before(r, f"sum{i}_{SET - 1}"))
                    for m in range(2):
                        v.tensor_tensor(sel[:, i, 4 * m:4 * m + 4, :],
                                        b.row_no[:, 0:ROWS].unsqueeze(1).to_broadcast([128, 4, ROWS]),
                                        g["lane"][:, bass.ds(k0 + 4 * m, 4)].unsqueeze(2).to_broadcast([128, 4, ROWS]),
                                        ALU.is_equal).then_inc(*dve.did(f"s{i}_{m}"))
                    v.reg_load(tiles, g["tile"][0:1, bass.ds(k0, SET)])
                    v.wait_ge(*pe.now(r, f"top{i}"))
                    v.wait_ge(*act.before(r, f"ex{i}"))
                    v.tensor_tensor(diff[:, i], e_all[:, bass.ds(k0, SET), 0:heads],
                                    ps[:, 2 + i, 0:q].rearrange("p (j h) -> p j h", h=heads),
                                    ALU.subtract).then_inc(*dve.did(f"diff{i}"))
                    v.wait_ge(*dve.now(r, f"diff{i}"))
                    v.tensor_scalar(diff[:, i], diff[:, i], 0.0, None, ALU.min).then_inc(*dve.did(f"low{i}"))
                    v.wait_ge(*act.now(r, f"ex{i}"))
                    v.wait_ge(gathered[i], (r + 1) * (SET * 16))
                    for m in range(2):
                        part = slice(4 * m, 4 * m + 4)
                        v.tensor_tensor(msg[:, i, part, 0:D].rearrange("p j (h f) -> p j h f", h=heads),
                                        got[:, i, part, :].rearrange("p j (h f) -> p j h f", h=heads),
                                        msg[:, i, part, D:width].unsqueeze(3).to_broadcast([128, 4, heads, D // heads]),
                                        ALU.mult).then_inc(*dve.did(f"msg{i}_{m}"))
                    for j in range(SET):
                        tile = v.snap(tiles[j], min_val=0, max_val=TILES)
                        v.wait_ge(*pe.now(r, f"sum{i}_{j}"))
                        acc_k = acc[:, bass.ds(tile * width, width)]
                        v.tensor_tensor(acc_k, acc_k, ps[0:ROWS, 4 + j % 4, 0:width], ALU.add).then_inc(*dve.did(f"acc{i}_{j}"))
                        v.wait_ge(*dve.now(r, f"acc{i}_{j}"))

        @block.tensor
        def _(e):
            pe.prime(e)
            tiles = [e.alloc_register(f"su_t{which}{j}") for which in [b.count] for j in range(SET)]
            with e.Fori(0, CHUNKS // (2 * SET)) as r:
                for i in sets:
                    k0 = r * (2 * SET) + i * SET
                    e.reg_load(tiles, g["tile"][0:1, bass.ds(k0, SET)])
                    for m in range(2):
                        e.wait_ge(*dve.now(r, f"s{i}_{m}"))
                        e.wait_ge(*other(act, r, i, f"st{{}}_{m}"))
                        for j in range(4):
                            last = e.transpose(ps[0:ROWS, m, 128 * j:128 * j + 128], sel[:, i, 4 * m + j, :], b.ident[:])
                        last.then_inc(*pe.did(f"st{i}_{m}"))
                    e.wait_ge(*act.now(r, f"st{i}_1"))
                    e.wait_ge(*dve.before(r, f"diff{i}"))
                    for j in range(SET):
                        tile = e.snap(tiles[j], min_val=0, max_val=TILES)
                        last = e.matmul(ps[:, 2 + i, j * heads:(j + 1) * heads], lhsT=selt[:, j, :],
                                        rhs=top[:, bass.ds(tile * heads, heads)], start=True, stop=True)
                    last.then_inc(*pe.did(f"top{i}"))
                    for j in range(SET):
                        e.wait_ge(*dve.now(r, f"msg{i}_{j // 4}"))
                        e.wait_ge(*(dve.now(r, f"acc{i}_{j - 4}") if j >= 4 else other(dve, r, i, f"acc{{}}_{SET - 4 + j}")))
                        e.matmul(ps[0:ROWS, 4 + j % 4, 0:width], lhsT=sel[:, i, j, :], rhs=msg[:, i, j, :],
                                 start=True, stop=True).then_inc(*pe.did(f"sum{i}_{j}"))

        @block.scalar
        def _(a):
            act.prime(a)
            with a.Fori(0, CHUNKS // (2 * SET)) as r:
                for i in sets:
                    for m in range(2):
                        a.wait_ge(*pe.now(r, f"st{i}_{m}"))
                        if m == 0:
                            a.wait_ge(*other(pe, r, i, "top{}"))
                        a.activation(selt[:, 4 * m:4 * m + 4, :].rearrange("p j e -> p (j e)"), ps[0:ROWS, m, :],
                                     ACT.Copy).then_inc(*act.did(f"st{i}_{m}"))
                    a.wait_ge(*dve.now(r, f"low{i}"))
                    a.wait_ge(*pe.before(r, f"sum{i}_{SET - 1}"))
                    a.activation(msg[:, i, :, D:width], diff[:, i], ACT.Exp).then_inc(*act.did(f"ex{i}"))


def edge_mean(b, acc, heads, bias, into, add):
    nc = b.nc
    width = D + heads
    with ExitStack() as c:
        dve = Steps(b.sem(c, "mean_dve"), ["den", "inv", "mean", "bias", "out"])
        den = b.sb(c, "den", [ROWS, heads])
        out = b.sb(c, "mean", [ROWS, D])
        block = c.enter_context(nc.Block())

        @block.vector
        def _(v):
            dve.prime(v)
            with v.Fori(0, TILES) as t:
                v.tensor_scalar(den[:], acc[:, bass.ds(t * width + D, heads)], 1e-30, None, ALU.max).then_inc(*dve.did("den"))
                v.wait_ge(*dve.now(t, "den"))
                v.reciprocal(den[:], den[:]).then_inc(*dve.did("inv"))
                v.wait_ge(*dve.now(t, "inv"))
                v.tensor_tensor(out[:].rearrange("p (h f) -> p h f", h=heads),
                                acc[:, bass.ds(t * width, D)].rearrange("p (h f) -> p h f", h=heads),
                                den[:].unsqueeze(2).to_broadcast([ROWS, heads, D // heads]), ALU.mult).then_inc(*dve.did("mean"))
                v.wait_ge(*dve.now(t, "mean"))
                v.tensor_tensor(out[:], out[:], bias, ALU.add).then_inc(*dve.did("bias"))
                v.wait_ge(*dve.now(t, "bias"))
                into_t = into[:, bass.ds(t, 1), :].rearrange("p a d -> p (a d)")
                if add:
                    v.scalar_tensor_tensor(out=into_t, in0=out[:], scalar=0.0, in1=into_t, op0=ALU.max, op1=ALU.add).then_inc(*dve.did("out"))
                else:
                    v.tensor_scalar(into_t, out[:], 0.0, None, ALU.max).then_inc(*dve.did("out"))
                v.wait_ge(*dve.now(t, "out"))


def broadcast(ap, rows=128):
    return bass.AP(tensor=ap.tensor, offset=ap.offset, ap=[[0, rows], [1, int(np.prod(ap.shape))]])


def graph_weights(b, ctx, w_name, own_name, nbr_name, heads):
    nc = b.nc
    weights = b.sb(ctx, "gw", [128, 2, D + 2 * heads])
    with ExitStack() as c:
        a = b.sb(c, "a", [128, 2, D])
        prod = b.sb(c, "prod", [128, D])
        loaded, done = b.sem(c, "gw_loaded"), b.sem(c, "gw_done")
        block = c.enter_context(nc.Block())

        @block.sync
        def _(sp):
            sp.dma_start(weights[:, :, 0:D], b.ins[w_name].rearrange("(k p) n -> p k n", p=128)).then_inc(loaded, 16)
            for i, name in enumerate((own_name, nbr_name)):
                sp.dma_start(a[:, i, :], broadcast(b.ins[name])).then_inc(loaded, 16)

        @block.vector
        def _(v):
            v.wait_ge(loaded, 48)
            n = 0
            for k in range(2):
                for i in range(2):
                    v.tensor_tensor(prod[:], weights[:, k, 0:D], a[:, i, :], ALU.mult).then_inc(done, 1)
                    v.wait_ge(done, n + 1)
                    v.tensor_reduce(weights[:, k, D + i * heads:D + (i + 1) * heads],
                                    prod[:].rearrange("p (h f) -> p h f", h=heads), AX.X, ALU.add).then_inc(done, 1)
                    v.wait_ge(done, n + 2)
                    n += 2
    return weights


def load(b, pairs):
    with ExitStack() as c:
        loaded = b.sem(c, "loaded")
        block = c.enter_context(b.nc.Block())

        @block.sync
        def _(sp):
            for dst, src in pairs:
                sp.dma_start(dst, src).then_inc(loaded, 16)
            sp.wait_ge(loaded, 16 * len(pairs))


def tile_of(source, t):
    return source[:, bass.ds(t, 1), :].rearrange("p a d -> p (a d)")


def phi_weights(b, ctx, side):
    nc, ps = b.nc, b.ps
    w = b.sb(ctx, "w", [128, 2, H * KD])
    wp = b.sb(ctx, "wp", [128, 2, H * KD])
    bias = b.sb(ctx, "bias", [3, 2, H * KD], BF16)
    with ExitStack() as c:
        wt = b.sb(c, "wt", [128, 2 * H, D])
        projt = b.sb(c, "projt", [128, 2, KD])
        column = b.sb(c, "column", [128, 2 * H])
        row = b.sb(c, "row", [1, 2, H * KD])
        parts = b.sb(c, "parts", [1, 3, 2, H * KD], BF16)
        load(b, [(w[:], b.ins[f"L0_mix_W{side}"].rearrange("(k p) n -> p k n", p=128)),
                 (wt[:], b.ins[f"W{side}_T"].rearrange("(k p) n -> p k n", p=128)),
                 (projt[:], b.ins["proj_T"].rearrange("(k p) n -> p k n", p=128)),
                 (column[:], b.ins[f"b{side}_columns"]),
                 (row[:, 0, :], b.ins[f"L0_mix_b{side}"].unsqueeze(0))])
        pe_did, act_did, dve_did = b.sem(c, "phw_pe"), b.sem(c, "phw_act"), b.sem(c, "phw_dve")
        spread = b.sem(c, "spread")
        block = c.enter_context(nc.Block())

        @block.tensor
        def _(e):
            for h in range(H):
                for m in range(3):
                    n = 3 * h + m
                    if n >= 4:
                        e.wait_ge(act_did, n - 3)
                    for k in range(2):
                        if m < 2:
                            last = e.matmul(ps[:, n % 4, 0:KD], lhsT=wt[:, 2 * h + k, 128 * m:128 * m + 128],
                                            rhs=projt[:, k, :], start=k == 0, stop=k == 1)
                        else:
                            last = e.matmul(ps[0:1, n % 4, 0:KD], lhsT=column[:, 2 * h + k:2 * h + k + 1],
                                            rhs=projt[:, k, :], start=k == 0, stop=k == 1)
                    last.then_inc(pe_did, 1)

        @block.scalar
        def _(a):
            for h in range(H):
                for m in range(3):
                    n = 3 * h + m
                    a.wait_ge(pe_did, n + 1)
                    if m < 2:
                        a.activation(wp[:, m, h * KD:(h + 1) * KD], ps[:, n % 4, 0:KD], ACT.Copy).then_inc(act_did, 1)
                    else:
                        a.activation(row[:, 1, h * KD:(h + 1) * KD], ps[0:1, n % 4, 0:KD], ACT.Copy).then_inc(act_did, 1)

        @block.vector
        def _(v):
            v.wait_ge(act_did, 3 * H)
            v.tensor_copy(parts[:, 0], row[:]).then_inc(dve_did, 1)
            v.wait_ge(dve_did, 1)
            v.tensor_tensor(row[:], row[:], parts[:, 0], ALU.subtract).then_inc(dve_did, 1)
            v.wait_ge(dve_did, 2)
            v.tensor_copy(parts[:, 1], row[:]).then_inc(dve_did, 1)
            v.wait_ge(dve_did, 3)
            v.tensor_tensor(row[:], row[:], parts[:, 1], ALU.subtract).then_inc(dve_did, 1)
            v.wait_ge(dve_did, 4)
            v.tensor_copy(parts[:, 2], row[:]).then_inc(dve_did, 1)

        @block.sync
        def _(sp):
            sp.wait_ge(dve_did, 5)
            for i in range(3):
                sp.dma_start(bias[i:i + 1].rearrange("p a n -> p (a n)"), parts[:, i].rearrange("p a n -> p (a n)")).then_inc(spread, 16)
            sp.wait_ge(spread, 48)
    return w, wp, bias


def phi_projections(e, b, w, xt, bank, bias, which, col, n):
    out = bank[:, 0:n]
    e.matmul(out, lhsT=b.onesb[0:3, 0:ROWS], rhs=bias[:, which, col:col + n], start=True, stop=False)
    e.matmul(out, lhsT=xt[:, 0, :], rhs=w[:, 0, col:col + n], start=False, stop=False)
    return e.matmul(out, lhsT=xt[:, 1, :], rhs=w[:, 1, col:col + n], start=False, stop=True)


def head_steps(lag):
    order = []
    for h in range(H + lag):
        if h < H:
            order += ([("pair", h // 2)] if h % 2 == 0 else []) + [("u", h)]
        if h >= lag:
            order += [("g", h - lag)]
    return order


def mix0_keys(b, gram, w, wp, bias):
    nc, ps = b.nc, b.ps
    order = head_steps(2)
    with ExitStack() as c:
        dve_order = []
        for h in range(H + 1):
            if h < H:
                dve_order += ([("shift", h // 2)] if h % 2 == 0 else []) + [("phi", h)]
            if h >= 1:
                dve_order += [("add", h - 1)]
        dve = Steps(b.sem(c, "key_dve"), RowNorm.steps() + ["xn"] + [n for kind, h in dve_order for n in
                    ([f"add{h}_0", f"add{h}_1"] if kind == "add" else [f"{kind}{h}"])])
        pool = Steps(b.sem(c, "key_pool"), ["root"])
        pe = Steps(b.sem(c, "key_pe"), ["turn"] + [n for kind, h in order for n in
                   ([f"g{h}_0", f"g{h}_1"] if kind == "g" else [f"{kind}{h}"])])
        act = Steps(b.sem(c, "key_act"), ["xt"] + [f"{n}{2 * g + i}" for g in range(H // 2) for n in ("sq", "exp") for i in range(2)])
        cleared = b.sem(c, "key_cleared")
        norm = RowNorm(b, c, dve, pool)
        xn = b.sb(c, "xn", [ROWS, D + 1])
        xt = b.sb(c, "xt", [128, 2, ROWS])
        junk = b.sb(c, "junk", [ROWS, 2, KD])
        sq = b.sb(c, "sq", [ROWS, H])
        shift = b.sb(c, "shift", [ROWS, H])
        phi = b.sb(c, "phi", [ROWS, 2, KD])
        phi1 = b.sb(c, "phi1", [ROWS, 2, KD])
        block = c.enter_context(nc.Block())

        @block.vector
        def _(v):
            dve.prime(v)
            v.memset(gram[:], 0.0).then_inc(cleared, 1)
            v.memset(xn[:, D:D + 1], 1.0).then_inc(cleared, 1)
            v.wait_ge(cleared, 2)
            with v.Fori(0, TILES) as t:
                norm.vector(v, t, tile_of(b.x, t), 1e-5)
                v.wait_ge(*pe.before(t, f"g{H - 1}_1"))
                norm.scaled(v, xn[:, 0:D], tile_of(b.x, t)).then_inc(*dve.did("xn"))
                for kind, h in dve_order:
                    if kind == "shift":
                        v.wait_ge(*act.now(t, f"sq{2 * h + 1}"))
                        v.wait_ge(*act.before(t, f"exp{2 * h + 1}"))
                        v.tensor_scalar(shift[:, 2 * h:2 * h + 2], sq[:, 2 * h:2 * h + 2], -0.5 * KSCALE * KSCALE, None,
                                        ALU.mult).then_inc(*dve.did(f"shift{h}"))
                    elif kind == "phi":
                        v.wait_ge(*act.now(t, f"exp{h}"))
                        v.wait_ge(*(pe.now(t, f"g{h - 2}_1") if h >= 2 else pe.before(t, f"g{H - 2 + h}_1")))
                        v.tensor_scalar(phi1[:, h % 2, :], phi[:, h % 2, :], KD ** -0.5, 1e-6, ALU.mult,
                                        ALU.add).then_inc(*dve.did(f"phi{h}"))
                    else:
                        for m in range(2):
                            v.wait_ge(*pe.now(t, f"g{h}_{m}"))
                            v.wait_ge(*dve.before(t, f"add{h}_{m}"))
                            v.tensor_tensor(gram[:, 2 * h + m, :], gram[:, 2 * h + m, :], ps[:, 6 + m, 0:D + 1],
                                            ALU.add).then_inc(*dve.did(f"add{h}_{m}"))

        @block.gpsimd
        def _(p):
            pool.prime(p)
            with p.Fori(0, TILES) as t:
                norm.gpsimd(p, t)

        @block.tensor
        def _(e):
            pe.prime(e)
            with e.Fori(0, TILES) as t:
                e.wait_ge(*dve.now(t, "xn"))
                e.wait_ge(*act.before(t, "xt"))
                for k in range(2):
                    last = e.transpose(ps[:, 0, k * ROWS:(k + 1) * ROWS], xn[:, 128 * k:128 * k + 128], b.ident[0:ROWS, 0:ROWS])
                last.then_inc(*pe.did("turn"))
                e.wait_ge(*act.now(t, "xt"))
                for kind, h in order:
                    if kind == "pair":
                        g = 2 * h + 1
                        e.wait_ge(*(act.now(t, f"sq{g - 4}") if g >= 4 else act.before(t, f"sq{H - 4 + g}")))
                        phi_projections(e, b, w, xt, ps[0:ROWS, 2 + h % 2, :], bias, 0, h * 512, 512).then_inc(*pe.did(f"pair{h}"))
                    elif kind == "u":
                        e.wait_ge(*(act.now(t, f"exp{h - 2}") if h >= 2 else act.before(t, f"exp{H - 2 + h}")))
                        phi_projections(e, b, wp, xt, ps[0:ROWS, 4 + h % 2, :], bias, 1, h * KD, KD).then_inc(*pe.did(f"u{h}"))
                    else:
                        e.wait_ge(*dve.now(t, f"phi{h}"))
                        for m in range(2):
                            e.wait_ge(*(dve.now(t, f"add{h - 1}_{m}") if h else dve.before(t, f"add{H - 1}_{m}")))
                            e.matmul(ps[:, 6 + m, 0:D + 1], lhsT=phi1[:, h % 2, 128 * m:128 * m + 128], rhs=xn[:],
                                     start=True, stop=True).then_inc(*pe.did(f"g{h}_{m}"))

        @block.scalar
        def _(a):
            act.prime(a)
            with a.Fori(0, TILES) as t:
                a.wait_ge(*pe.now(t, "turn"))
                a.wait_ge(*pe.before(t, f"u{H - 1}"))
                a.activation(xt[:].rearrange("p k n -> p (k n)"), ps[:, 0, 0:2 * ROWS], ACT.Copy).then_inc(*act.did("xt"))
                for g in range(H // 2):
                    a.wait_ge(*pe.now(t, f"pair{g}"))
                    a.wait_ge(*dve.before(t, f"shift{g}"))
                    for h in (2 * g, 2 * g + 1):
                        a.wait_ge(*(act.now(t, f"sq{h - 2}") if h >= 2 else act.before(t, f"sq{H - 2 + h}")))
                        a.activation(junk[:, h % 2, :], ps[0:ROWS, 2 + g % 2, (h % 2) * KD:(h % 2 + 1) * KD], ACT.Square,
                                     accum_out=sq[:, h:h + 1]).then_inc(*act.did(f"sq{h}"))
                    for h in (2 * g, 2 * g + 1):
                        a.wait_ge(*dve.now(t, f"shift{g}"))
                        a.wait_ge(*pe.now(t, f"u{h}"))
                        a.wait_ge(*(dve.now(t, f"phi{h - 2}") if h >= 2 else dve.before(t, f"phi{H - 2 + h}")))
                        a.activation(phi[:, h % 2, :], ps[0:ROWS, 4 + h % 2, 0:KD], ACT.Exp, bias=shift[:, h:h + 1],
                                     scale=KSCALE).then_inc(*act.did(f"exp{h}"))


def mix0_values(b, kvo, gram):
    nc, ps = b.nc, b.ps
    with ExitStack() as c:
        wv = b.sb(c, "wv", [128, 2, H * KD])
        bv = b.sb(c, "bv", [1, H * KD])
        wo = b.sb(c, "wo", [128, 2 * H, D])
        gt = b.sb(c, "gt", [128, 2, 256])
        sums = b.sb(c, "sums", [1, 256])
        kvt = b.sb(c, "kvt", [128, 2, 256])
        load(b, [(wv[:], b.ins["L0_mix_Wv"].rearrange("(k p) n -> p k n", p=128)),
                 (bv[:], b.ins["L0_mix_bv"].unsqueeze(0)),
                 (wo[:], b.ins["L0_mix_Wo"].rearrange("(k p) n -> p k n", p=128))])
        pe_did, act_did, dve_did = b.sem(c, "val_pe"), b.sem(c, "val_act"), b.sem(c, "val_dve")
        block = c.enter_context(nc.Block())

        @block.tensor
        def _(e):
            for h in range(H):
                if h:
                    e.wait_ge(act_did, 7 * h)
                for k in range(2):
                    for m in range(2):
                        last = e.transpose(ps[:, k, 128 * m:128 * m + 128], gram[:, 2 * h + m, 128 * k:128 * k + 128], b.ident[:])
                    last.then_inc(pe_did, 1)
                for m in range(2):
                    last = e.transpose(ps[0:1, 2, 128 * m:128 * m + 128], gram[:, 2 * h + m, D:D + 1], b.ident[:])
                last.then_inc(pe_did, 1)
                e.wait_ge(act_did, 7 * h + 3)
                for n in range(2):
                    col = h * KD + 128 * n
                    e.matmul(ps[:, 3 + n, 0:256], lhsT=bv[:, col:col + 128], rhs=sums[:], start=True, stop=False)
                    for k in range(2):
                        last = e.matmul(ps[:, 3 + n, 0:256], lhsT=wv[:, k, col:col + 128], rhs=gt[:, k, :], start=False, stop=k == 1)
                    last.then_inc(pe_did, 1)
                e.wait_ge(act_did, 7 * h + 5)
                for m in range(2):
                    for k in range(2):
                        last = e.matmul(ps[:, 5 + m, 0:D], lhsT=kvt[:, k, 128 * m:128 * m + 128], rhs=wo[:, 2 * h + k, :],
                                        start=k == 0, stop=k == 1)
                    last.then_inc(pe_did, 1)

        @block.scalar
        def _(a):
            for h in range(H):
                for k in range(2):
                    a.wait_ge(pe_did, 7 * h + k + 1)
                    a.activation(gt[:, k, :], ps[:, k, 0:256], ACT.Copy).then_inc(act_did, 1)
                a.wait_ge(pe_did, 7 * h + 3)
                a.activation(sums[:], ps[0:1, 2, 0:256], ACT.Copy).then_inc(act_did, 1)
                for n in range(2):
                    a.wait_ge(pe_did, 7 * h + 4 + n)
                    a.activation(kvt[:, n, :], ps[:, 3 + n, 0:256], ACT.Copy).then_inc(act_did, 1)
                for m in range(2):
                    a.wait_ge(pe_did, 7 * h + 6 + m)
                    a.activation(kvo[:, 2 * h + m, 0:D], ps[:, 5 + m, 0:D], ACT.Copy).then_inc(act_did, 1)

        @block.vector
        def _(v):
            v.tensor_copy(kvo[:, :, D:D + 1], gram[:, :, D:D + 1]).then_inc(dve_did, 1)


def mix0_queries(b, w, wp, bias, kvo):
    nc, ps = b.nc, b.ps
    order = head_steps(2)
    names = ("bo", "g1", "beta1", "bias2", "g2", "beta2")
    with ExitStack() as c:
        vec = {n: b.sb(c, n, [ROWS, D]) for n in names}
        w1 = b.sb(c, "w1", [128, 2, D])
        w2 = b.sb(c, "w2", [128, 2, D])
        bias1 = b.sb(c, "bias1", [128, 2])
        load(b, [(vec[n][:], broadcast(b.ins[f"L0_mix_{n}"], ROWS)) for n in names]
             + [(w1[:], b.ins["L0_mix_W1"].rearrange("(k p) n -> p k n", p=128)),
                (w2[:], b.ins["L0_mix_W2"].rearrange("(k p) n -> p k n", p=128)),
                (bias1[:], b.ins["bias1_columns"])])
        dve_order = []
        for h in range(H + 2):
            if h < H:
                dve_order += ([("shift", h // 2)] if h % 2 == 0 else []) + [("phi", h)]
            if h >= 2:
                dve_order += [("add", h - 2)]
        dve = Steps(b.sem(c, "q_dve"), RowNorm.steps() + ["xn", "start"] + [n for kind, h in dve_order for n in
                    ([f"inv{h}", f"add{h}"] if kind == "add" else [f"{kind}{h}"])]
                    + RowNorm.steps("a") + ["a1", "a2", "out1", "f1", "f2"] + RowNorm.steps("b") + ["b1", "b2", "b3", "x"])
        pool = Steps(b.sem(c, "q_pool"), ["root", "aroot", "broot"])
        pe = Steps(b.sem(c, "q_pe"), ["turn"] + [n for kind, h in order for n in
                   ([f"pt{h}", f"g{h}"] if kind == "g" else [f"{kind}{h}"])] + ["turn1", "h", "ff"])
        act_order = [("sq", 0), ("sq", 1), ("exp", 0), ("exp", 1), ("sq", 2), ("sq", 3)]
        for h in range(H):
            act_order += ([("exp", h + 2)] if h + 2 < H else []) + [("pt", h)]
            act_order += [("sq", h + 3), ("sq", h + 4)] if h % 2 and h + 4 < H else []
        act = Steps(b.sem(c, "q_act"), ["xt"] + [f"{k}{h}" for k, h in act_order] + ["xt1", "h0", "h1"])
        norm, norm_a, norm_b = (RowNorm(b, c, dve, pool, tag) for tag in ("", "a", "b"))
        xn = b.sb(c, "xn", [ROWS, D])
        xt = b.sb(c, "xt", [128, 2, ROWS])
        junk = b.sb(c, "junk", [ROWS, 2, KD])
        sq = b.sb(c, "sq", [ROWS, H])
        shift = b.sb(c, "shift", [ROWS, H])
        phi = b.sb(c, "phi", [ROWS, 2, KD])
        phi1 = b.sb(c, "phi1", [ROWS, 2, KD])
        phit = b.sb(c, "phit", [128, 2, 2 * ROWS])
        inv = b.sb(c, "inv", [ROWS, 1])
        y = b.sb(c, "y", [ROWS, D])
        out1 = b.sb(c, "out1", [ROWS, D])
        xt1 = b.sb(c, "xt1", [128, 2, ROWS])
        hidden = b.sb(c, "hidden", [128, 2, ROWS])
        block = c.enter_context(nc.Block())

        @block.vector
        def _(v):
            dve.prime(v)
            with v.Fori(0, TILES) as t:
                def step(ins, name):
                    ins.then_inc(*dve.did(name))
                    v.wait_ge(*dve.now(t, name))

                norm.vector(v, t, tile_of(b.x, t), 1e-5)
                v.wait_ge(*pe.before(t, "turn"))
                step(norm.scaled(v, xn[:], tile_of(b.x, t)), "xn")
                step(v.tensor_tensor(y[:], xn[:], vec["bo"][:], ALU.add), "start")
                for kind, h in dve_order:
                    if kind == "shift":
                        v.wait_ge(*act.now(t, f"sq{2 * h + 1}"))
                        v.wait_ge(*act.before(t, f"exp{2 * h + 1}"))
                        v.tensor_scalar(shift[:, 2 * h:2 * h + 2], sq[:, 2 * h:2 * h + 2], -0.5 * KSCALE * KSCALE, None,
                                        ALU.mult).then_inc(*dve.did(f"shift{h}"))
                    elif kind == "phi":
                        v.wait_ge(*act.now(t, f"exp{h}"))
                        v.wait_ge(*(pe.now(t, f"pt{h - 2}") if h >= 2 else pe.before(t, f"pt{H - 2 + h}")))
                        v.tensor_scalar(phi1[:, h % 2, :], phi[:, h % 2, :], KD ** -0.5, 1e-6, ALU.mult,
                                        ALU.add).then_inc(*dve.did(f"phi{h}"))
                    else:
                        v.wait_ge(*pe.now(t, f"g{h}"))
                        step(v.reciprocal(inv[:], ps[0:ROWS, 7, D:D + 1]), f"inv{h}")
                        step(v.scalar_tensor_tensor(out=y[:], in0=ps[0:ROWS, 7, 0:D], scalar=inv[:], in1=y[:], op0=ALU.mult,
                                                    op1=ALU.add), f"add{h}")
                norm_a.vector(v, t, y[:], 1e-6)
                step(norm_a.scaled(v, y[:], y[:]), "a1")
                step(v.tensor_tensor(y[:], y[:], vec["g1"][:], ALU.mult), "a2")
                step(v.tensor_tensor(out1[:], y[:], vec["beta1"][:], ALU.add), "out1")
                v.wait_ge(*pe.now(t, "ff"))
                step(v.tensor_tensor(y[:], ps[0:ROWS, 7, 0:D], out1[:], ALU.add), "f1")
                step(v.tensor_tensor(y[:], y[:], vec["bias2"][:], ALU.add), "f2")
                norm_b.vector(v, t, y[:], 1e-6)
                step(norm_b.scaled(v, y[:], y[:]), "b1")
                step(v.tensor_tensor(y[:], y[:], vec["g2"][:], ALU.mult), "b2")
                step(v.tensor_tensor(y[:], y[:], vec["beta2"][:], ALU.add), "b3")
                step(v.tensor_tensor(tile_of(b.x, t), tile_of(b.x, t), y[:], ALU.add), "x")

        @block.gpsimd
        def _(p):
            pool.prime(p)
            with p.Fori(0, TILES) as t:
                for one in (norm, norm_a, norm_b):
                    one.gpsimd(p, t)

        @block.tensor
        def _(e):
            pe.prime(e)
            with e.Fori(0, TILES) as t:
                def turn(source, name):
                    for k in range(2):
                        last = e.transpose(ps[:, 0, k * ROWS:(k + 1) * ROWS], source[:, 128 * k:128 * k + 128], b.ident[0:ROWS, 0:ROWS])
                    last.then_inc(*pe.did(name))

                e.wait_ge(*dve.now(t, "xn"))
                e.wait_ge(*act.before(t, "h1"))
                turn(xn, "turn")
                e.wait_ge(*act.now(t, "xt"))
                for kind, h in order:
                    if kind == "pair":
                        g = 2 * h + 1
                        e.wait_ge(*(act.now(t, f"sq{g - 4}") if g >= 4 else act.before(t, f"sq{H - 4 + g}")))
                        phi_projections(e, b, w, xt, ps[0:ROWS, 1 + h % 2, :], bias, 0, h * 512, 512).then_inc(*pe.did(f"pair{h}"))
                    elif kind == "u":
                        e.wait_ge(*(act.now(t, f"exp{h - 2}") if h >= 2 else act.before(t, f"exp{H - 2 + h}")))
                        phi_projections(e, b, wp, xt, ps[0:ROWS, 3 + h % 2, :], bias, 1, h * KD, KD).then_inc(*pe.did(f"u{h}"))
                    else:
                        e.wait_ge(*dve.now(t, f"phi{h}"))
                        e.wait_ge(*(act.now(t, f"pt{h - 2}") if h >= 2 else act.before(t, f"pt{H - 2 + h}")))
                        for m in range(2):
                            last = e.transpose(ps[:, 5 + h % 2, m * ROWS:(m + 1) * ROWS], phi1[:, h % 2, 128 * m:128 * m + 128],
                                               b.ident[0:ROWS, 0:ROWS])
                        last.then_inc(*pe.did(f"pt{h}"))
                        e.wait_ge(*act.now(t, f"pt{h}"))
                        e.wait_ge(*(dve.now(t, f"add{h - 1}") if h else dve.before(t, "f1")))
                        for m in range(2):
                            last = e.matmul(ps[0:ROWS, 7, 0:D + 1], lhsT=phit[:, h % 2, m * ROWS:(m + 1) * ROWS],
                                            rhs=kvo[:, 2 * h + m, :], start=m == 0, stop=m == 1)
                        last.then_inc(*pe.did(f"g{h}"))
                e.wait_ge(*dve.now(t, "out1"))
                turn(out1, "turn1")
                e.wait_ge(*act.now(t, "xt1"))
                for m in range(2):
                    for k in range(2):
                        last = e.matmul(ps[:, 0, m * ROWS:(m + 1) * ROWS], lhsT=w1[:, k, 128 * m:128 * m + 128], rhs=xt1[:, k, :],
                                        start=k == 0, stop=k == 1)
                last.then_inc(*pe.did("h"))
                e.wait_ge(*act.now(t, "h1"))
                for k in range(2):
                    last = e.matmul(ps[0:ROWS, 7, 0:D], lhsT=hidden[:, k, :], rhs=w2[:, k, :], start=k == 0, stop=k == 1)
                last.then_inc(*pe.did("ff"))

        @block.scalar
        def _(a):
            act.prime(a)
            with a.Fori(0, TILES) as t:
                a.wait_ge(*pe.now(t, "turn"))
                a.activation(xt[:].rearrange("p k n -> p (k n)"), ps[:, 0, 0:2 * ROWS], ACT.Copy).then_inc(*act.did("xt"))
                for kind, h in act_order:
                    g = h // 2
                    if kind == "sq":
                        a.wait_ge(*pe.now(t, f"pair{g}"))
                        a.wait_ge(*dve.before(t, f"shift{g}"))
                        a.wait_ge(*(act.now(t, f"sq{h - 2}") if h >= 2 else act.before(t, f"sq{H - 2 + h}")))
                        a.activation(junk[:, h % 2, :], ps[0:ROWS, 1 + g % 2, (h % 2) * KD:(h % 2 + 1) * KD], ACT.Square,
                                     accum_out=sq[:, h:h + 1]).then_inc(*act.did(f"sq{h}"))
                    elif kind == "exp":
                        a.wait_ge(*dve.now(t, f"shift{g}"))
                        a.wait_ge(*pe.now(t, f"u{h}"))
                        a.wait_ge(*(dve.now(t, f"phi{h - 2}") if h >= 2 else dve.before(t, f"phi{H - 2 + h}")))
                        a.activation(phi[:, h % 2, :], ps[0:ROWS, 3 + h % 2, 0:KD], ACT.Exp, bias=shift[:, h:h + 1],
                                     scale=KSCALE).then_inc(*act.did(f"exp{h}"))
                    else:
                        a.wait_ge(*pe.now(t, f"pt{h}"))
                        a.wait_ge(*(pe.now(t, f"g{h - 2}") if h >= 2 else pe.before(t, f"g{H - 2 + h}")))
                        a.activation(phit[:, h % 2, :], ps[:, 5 + h % 2, 0:2 * ROWS], ACT.Copy).then_inc(*act.did(f"pt{h}"))
                a.wait_ge(*pe.now(t, "turn1"))
                a.activation(xt1[:].rearrange("p k n -> p (k n)"), ps[:, 0, 0:2 * ROWS], ACT.Copy).then_inc(*act.did("xt1"))
                a.wait_ge(*pe.now(t, "h"))
                for m in range(2):
                    a.activation(hidden[:, m, :], ps[:, 0, m * ROWS:(m + 1) * ROWS], ACT.Relu,
                                 bias=bias1[:, m:m + 1]).then_inc(*act.did(f"h{m}"))


def choose_rows(b, ctx, chosen):
    nc, ps = b.nc, b.ps
    weights_row = b.dram("router_row", [N])
    with ExitStack() as c:
        wr = b.sb(c, "wr", [ROWS, D])
        br = b.sb(c, "br", [ROWS, 1])
        load(b, [(wr[:], broadcast(b.ins["L0_ffn_wr"], ROWS)), (br[:], broadcast(b.ins["L0_ffn_br"], ROWS))])
        dve = Steps(b.sem(c, "rt_dve"), RowNorm.steps() + ["xn", "dot"])
        pool = Steps(b.sem(c, "rt_pool"), ["root"])
        weight = b.sb(c, "weight", [ROWS, TILES])
        every = b.sb(c, "every", [ROWS, N])
        norm = RowNorm(b, c, dve, pool)
        xn = b.sb(c, "xn", [ROWS, D])
        junk = b.sb(c, "junk", [ROWS, D])
        flags = b.sb(c, "flags", [ROWS, N], BF16)
        above = b.sb(c, "above", [ROWS, 3, TILES])
        tri = b.sb(c, "tri", [ROWS, ROWS])
        tied = b.sb(c, "tied", [ROWS, ROWS])
        added, turned, copied = b.sem(c, "added"), b.sem(c, "turned"), b.sem(c, "copied")
        stored, ranked, tri_ready = b.sem(c, "stored"), b.sem(c, "ranked"), b.sem(c, "tri_ready")
        turned_weight = b.sb(c, "turned_weight", [TILES, ROWS])
        block = c.enter_context(nc.Block())

        @block.gpsimd
        def _(p):
            pool.prime(p)
            p.affine_select(out=tri[:], in_=b.ones[0:ROWS, 0:ROWS], compare_op=ALU.is_gt, fill=0.0, base=0,
                            pattern=[[-1, ROWS]], channel_multiplier=1).then_inc(tri_ready, 1)
            with p.Fori(0, TILES) as t:
                norm.gpsimd(p, t)

        @block.tensor
        def _(e):
            e.wait_ge(added, 1)
            e.transpose(ps[0:TILES, 0, 0:ROWS], weight[:], b.ident[0:ROWS, 0:ROWS]).then_inc(turned, 1)

        @block.scalar
        def _(a):
            a.wait_ge(turned, 1)
            a.activation(turned_weight[:], ps[0:TILES, 0, 0:ROWS], ACT.Copy).then_inc(copied, 1)

        @block.sync
        def _(sp):
            sp.wait_ge(copied, 1)
            sp.dma_start(weights_row.rearrange("(t p) -> t p", p=ROWS), turned_weight[:]).then_inc(stored, 16)
            sp.wait_ge(stored, 16)
            sp.dma_start(every[:], broadcast(weights_row, ROWS)).then_inc(stored, 16)

        @block.vector
        def _(v):
            dve.prime(v)
            with v.Fori(0, TILES) as t:
                norm.vector(v, t, tile_of(b.x, t), 1e-5)
                norm.scaled(v, xn[:], tile_of(b.x, t)).then_inc(*dve.did("xn"))
                v.wait_ge(*dve.now(t, "xn"))
                v.scalar_tensor_tensor(out=junk[:], in0=xn[:], scalar=1.0, in1=wr[:], op0=ALU.mult, op1=ALU.mult,
                                       accum_out=weight[:, bass.ds(t, 1)]).then_inc(*dve.did("dot"))
                v.wait_ge(*dve.now(t, "dot"))
            v.tensor_scalar(weight[:], weight[:], br[:], None, ALU.add).then_inc(added, 1)
            v.wait_ge(stored, 32)
            v.wait_ge(added, 1)
            v.wait_ge(tri_ready, 1)
            n = 0
            v.memset(above[:], 0.0).then_inc(ranked, 1)
            v.wait_ge(ranked, 1)
            n = 1

            def count(ins):
                nonlocal n
                n += 1
                ins.then_inc(ranked, 1)
                v.wait_ge(ranked, n)

            for t in range(TILES):
                mine, lo, hi = weight[:, t:t + 1], t * ROWS, (t + 1) * ROWS
                if t:
                    count(v.tensor_scalar(flags[:, 0:lo], every[:, 0:lo], mine, 0.0, ALU.is_ge, ALU.add,
                                          accum_out=above[:, 0, t:t + 1]))
                count(v.tensor_scalar(flags[:, lo:N], every[:, lo:N], mine, 0.0, ALU.is_gt, ALU.add,
                                      accum_out=above[:, 1, t:t + 1]))
                count(v.scalar_tensor_tensor(out=tied[:], in0=every[:, lo:hi], scalar=mine, in1=tri[:], op0=ALU.is_equal,
                                             op1=ALU.mult, accum_out=above[:, 2, t:t + 1]))
            count(v.tensor_tensor(above[:, 0, :], above[:, 0, :], above[:, 1, :], ALU.add))
            count(v.tensor_tensor(above[:, 0, :], above[:, 0, :], above[:, 2, :], ALU.add))
            count(v.scalar_tensor_tensor(out=chosen[:], in0=above[:, 0, :], scalar=float(KK), in1=weight[:], op0=ALU.is_lt,
                                         op1=ALU.mult))


def ffn0(b, chosen):
    nc, ps = b.nc, b.ps
    parts = HID // 128
    with ExitStack() as c:
        w1 = b.sb(c, "w1", [128, 2, HID])
        w2 = b.sb(c, "w2", [128, parts, D])
        b1 = b.sb(c, "b1", [128, parts])
        b2 = b.sb(c, "b2", [ROWS, D])
        load(b, [(w1[:], b.ins["L0_ffn_w1"].rearrange("(k p) n -> p k n", p=128)),
                 (w2[:], b.ins["L0_ffn_w2"].rearrange("(k p) n -> p k n", p=128)),
                 (b1[:], b.ins["ffn_b1_columns"]), (b2[:], broadcast(b.ins["L0_ffn_b2"], ROWS))])
        dve = Steps(b.sem(c, "f_dve"), RowNorm.steps() + ["xn", "res", "y1", "y2", "x"])
        pool = Steps(b.sem(c, "f_pool"), ["root"])
        pe = Steps(b.sem(c, "f_pe"), ["turn"] + [f"h{m}" for m in range(parts)] + ["y"])
        act = Steps(b.sem(c, "f_act"), ["xt"] + [f"h{m}" for m in range(parts)])
        norm = RowNorm(b, c, dve, pool)
        xn = b.sb(c, "xn", [ROWS, D])
        res = b.sb(c, "res", [ROWS, D])
        y = b.sb(c, "y", [ROWS, D])
        xt = b.sb(c, "xt", [128, 2, ROWS])
        hidden = b.sb(c, "hidden", [128, parts, ROWS])
        block = c.enter_context(nc.Block())

        @block.vector
        def _(v):
            dve.prime(v)
            with v.Fori(0, TILES) as t:
                def step(ins, name):
                    ins.then_inc(*dve.did(name))
                    v.wait_ge(*dve.now(t, name))

                norm.vector(v, t, tile_of(b.x, t), 1e-5)
                v.wait_ge(*pe.before(t, "turn"))
                step(norm.scaled(v, xn[:], tile_of(b.x, t)), "xn")
                step(v.tensor_tensor(res[:], tile_of(b.x, t), xn[:], ALU.add), "res")
                v.wait_ge(*pe.now(t, "y"))
                step(v.tensor_tensor(y[:], ps[0:ROWS, 3, 0:D], b2[:], ALU.add), "y1")
                step(v.tensor_scalar(y[:], y[:], chosen[:, bass.ds(t, 1)], None, ALU.mult), "y2")
                step(v.tensor_tensor(tile_of(b.x, t), y[:], res[:], ALU.add), "x")

        @block.gpsimd
        def _(p):
            pool.prime(p)
            with p.Fori(0, TILES) as t:
                norm.gpsimd(p, t)

        @block.tensor
        def _(e):
            pe.prime(e)
            with e.Fori(0, TILES) as t:
                e.wait_ge(*dve.now(t, "xn"))
                e.wait_ge(*act.before(t, "xt"))
                for k in range(2):
                    last = e.transpose(ps[:, 0, k * ROWS:(k + 1) * ROWS], xn[:, 128 * k:128 * k + 128], b.ident[0:ROWS, 0:ROWS])
                last.then_inc(*pe.did("turn"))
                e.wait_ge(*act.now(t, "xt"))
                for m in range(parts):
                    e.wait_ge(*(act.now(t, f"h{m - 2}") if m >= 2 else act.before(t, f"h{parts - 2 + m}")))
                    for k in range(2):
                        last = e.matmul(ps[:, 1 + m % 2, 0:ROWS], lhsT=w1[:, k, 128 * m:128 * m + 128], rhs=xt[:, k, :],
                                        start=k == 0, stop=k == 1)
                    last.then_inc(*pe.did(f"h{m}"))
                e.wait_ge(*dve.before(t, "y1"))
                for m in range(parts):
                    e.wait_ge(*act.now(t, f"h{m}"))
                    last = e.matmul(ps[0:ROWS, 3, 0:D], lhsT=hidden[:, m, :], rhs=w2[:, m, :], start=m == 0, stop=m == parts - 1)
                last.then_inc(*pe.did("y"))

        @block.scalar
        def _(a):
            act.prime(a)
            with a.Fori(0, TILES) as t:
                a.wait_ge(*pe.now(t, "turn"))
                a.activation(xt[:].rearrange("p k n -> p (k n)"), ps[:, 0, 0:2 * ROWS], ACT.Copy).then_inc(*act.did("xt"))
                for m in range(parts):
                    a.wait_ge(*pe.now(t, f"h{m}"))
                    if m == 0:
                        a.wait_ge(*pe.before(t, "y"))
                    a.activation(hidden[:, m, :], ps[:, 1 + m % 2, 0:ROWS], ACT.Gelu_apprx_tanh,
                                 bias=b1[:, m:m + 1]).then_inc(*act.did(f"h{m}"))


def products(unit, feat, h):
    whole = unit[:]
    rows, step = whole.ap[0][1], whole.ap[0][0]
    base = whole.offset + h * (HD + HD // 2)
    two = bass.AP(tensor=whole.tensor, offset=base, ap=[[step, rows], [1, OFFS], [1, HD]])
    one = bass.AP(tensor=whole.tensor, offset=base, ap=[[step, rows], [0, OFFS], [1, HD]])
    return feat[:, h, 0:QUAD].rearrange("p (o i) -> p o i", i=HD), two, one


def mix1(b, keys, moments):
    nc, ps = b.nc, b.ps
    cols = 2 * D if keys else D
    chunks = FEAT // 128
    units = H * chunks
    wide = HD + 1
    scale = float(HD) ** 0.25
    with ExitStack() as c:
        w = b.sb(c, "w", [128, 2, cols])
        bias = b.sb(c, "bias", [ROWS, cols])
        first = D if keys else 0
        pairs = [(w[:], b.ins["Wqkv_T"].rearrange("(k p) n -> p k n", p=128)[:, :, first:first + cols]),
                 (bias[:], broadcast(b.ins["L1_mix_bqkv"][first:first + cols], ROWS))]
        if not keys:
            temp = b.sb(c, "temp", [ROWS, H])
            proj = b.sb(c, "proj", [128, 2, D])
            bproj = b.sb(c, "bproj", [ROWS, D])
            pairs += [(temp[:], broadcast(b.ins["L1_mix_temperature"], ROWS)),
                      (proj[:], b.ins["Wproj_T"].rearrange("(k p) n -> p k n", p=128)),
                      (bproj[:], broadcast(b.ins["L1_mix_bproj"], ROWS))]
        else:
            coef = b.sb(c, "coef", [128, chunks])
            pairs += [(coef[:], b.ins["mix1_coef"])]
        load(b, pairs)
        dve = Steps(b.sem(c, "m1_dve"), RowNorm.steps() + ["xn", "bias", "sq", "len2", "max", "inv", "inv2", "unit", "again"]
                    + (["values"] + [f"f{h}" for h in range(H)] + [f"mo{i}" for i in range(3)] if keys else
                       [f"f{h}" for h in range(H)] + ["div", "out", "x0", "x"]))
        pool = Steps(b.sem(c, "m1_pool"), ["root", "len"])
        pe = Steps(b.sem(c, "m1_pe"), ["turn", "qkv"] + ([f"mo{i}" for i in range(3)] if keys else
                   [n for h in range(H) for n in (f"ft{h}_0", f"ft{h}_1", f"y{h}")] + ["turn1", "proj"]))
        act = Steps(b.sem(c, "m1_act"), ["xt"] + [f"lin{h}" for h in range(H)] + ([] if keys else
                    [n for h in range(H) for n in (f"ft{h}_0", f"ft{h}_1")] + ["xt1"]))
        cleared = b.sem(c, "m1_cleared")
        norm = RowNorm(b, c, dve, pool)
        xn = b.sb(c, "xn", [ROWS, D])
        xt = b.sb(c, "xt", [128, 2, ROWS])
        rows = b.sb(c, "rows", [ROWS, cols])
        sq = b.sb(c, "sq", [ROWS, D])
        length = b.sb(c, "length", [ROWS, 4, H])
        power = b.sb(c, "power", [ROWS, H])
        unit = b.sb(c, "unit", [ROWS, H, HD + HD // 2])
        feat = b.sb(c, "feat", [ROWS, H, FEAT])
        if keys:
            values = b.sb(c, "values", [ROWS, H, wide])
        else:
            featt = b.sb(c, "featt", [128, 2, chunks, ROWS])
            y = b.sb(c, "y", [ROWS, D])
            inv = b.sb(c, "inv", [ROWS, H])
            xt1 = b.sb(c, "xt1", [128, 2, ROWS])
        block = c.enter_context(nc.Block())
        moments2 = moments[:].rearrange("p u e -> p (u e)")
        bank_units = 512 // wide
        spans = [(i * bank_units, min(units, (i + 1) * bank_units)) for i in range(3)]

        @block.vector
        def _(v):
            dve.prime(v)
            v.memset(feat[:, :, QUAD:FEAT], 0.0).then_inc(cleared, 1)
            v.memset(power[:], 0.5).then_inc(cleared, 1)
            v.wait_ge(cleared, 2)
            v.memset(feat[:, :, QUAD + HD:QUAD + HD + 1], 1.0).then_inc(cleared, 1)
            if keys:
                v.memset(moments[:], 0.0).then_inc(cleared, 1)
                v.memset(values[:], 1.0).then_inc(cleared, 1)
            v.wait_ge(cleared, 5 if keys else 3)
            with v.Fori(0, TILES) as t:
                def step(ins, name):
                    ins.then_inc(*dve.did(name))
                    v.wait_ge(*dve.now(t, name))

                norm.vector(v, t, tile_of(b.x1, t), 1e-5)
                v.wait_ge(*pe.before(t, "turn"))
                step(norm.scaled(v, xn[:], tile_of(b.x1, t)), "xn")
                v.wait_ge(*pe.now(t, "qkv"))
                step(v.tensor_tensor(rows[:], ps[0:ROWS, 1, 0:cols], bias[:], ALU.add), "bias")
                step(v.tensor_tensor(sq[:], rows[:, 0:D], rows[:, 0:D], ALU.mult), "sq")
                step(v.tensor_reduce(length[:, 0, :], sq[:].rearrange("p (h i) -> p h i", h=H), AX.X, ALU.add), "len2")
                v.wait_ge(*pool.now(t, "len"))
                step(v.tensor_scalar(length[:, 2, :], length[:, 1, :], 1.0 if keys else scale, 1e-12, ALU.mult, ALU.max), "max")
                step(v.reciprocal(length[:, 3, :], length[:, 2, :]), "inv")
                if keys:
                    step(v.tensor_scalar(length[:, 3, :], length[:, 3, :], scale, None, ALU.mult), "inv2")
                else:
                    step(v.scalar_tensor_tensor(out=length[:, 3, :], in0=length[:, 3, :], scalar=scale * scale, in1=temp[:],
                                                op0=ALU.mult, op1=ALU.mult), "inv2")
                v.wait_ge(*act.before(t, f"lin{H - 1}"))
                step(v.tensor_tensor(unit[:, :, 0:HD], rows[:, 0:D].rearrange("p (h i) -> p h i", h=H),
                                     length[:, 3, :].unsqueeze(2).to_broadcast([ROWS, H, HD]), ALU.mult), "unit")
                step(v.tensor_scalar(unit[:, :, HD:], unit[:, :, 0:HD // 2], 1.0, None, ALU.mult), "again")
                if keys:
                    v.wait_ge(*pe.before(t, "mo2"))
                    v.tensor_scalar(values[:, :, 1:wide], rows[:, D:2 * D].rearrange("p (h i) -> p h i", h=H), 1.0, None,
                                    ALU.mult).then_inc(*dve.did("values"))
                for h in range(H):
                    if not keys:
                        v.wait_ge(*pe.before(t, f"ft{h}_1"))
                    out, two, one = products(unit, feat, h)
                    v.tensor_tensor(out, two, one, ALU.mult).then_inc(*dve.did(f"f{h}"))
                if keys:
                    for i, (lo, hi) in enumerate(spans):
                        v.wait_ge(*pe.now(t, f"mo{i}"))
                        step(v.tensor_tensor(moments2[:, lo * wide:hi * wide], moments2[:, lo * wide:hi * wide],
                                             ps[:, 2 + i, 0:(hi - lo) * wide], ALU.add), f"mo{i}")
                else:
                    v.wait_ge(*pe.now(t, f"y{H - 1}"))
                    sums = ps[0:ROWS, 2, 0:H * wide].rearrange("p (h e) -> p h e", h=H)
                    step(v.reciprocal(inv[:], sums[:, :, 0]), "div")
                    v.wait_ge(*pe.before(t, "turn1"))
                    step(v.tensor_tensor(y[:].rearrange("p (h e) -> p h e", h=H), sums[:, :, 1:wide],
                                         inv[:].unsqueeze(2).to_broadcast([ROWS, H, HD]), ALU.mult), "out")
                    v.wait_ge(*pe.now(t, "proj"))
                    step(v.tensor_tensor(tile_of(b.x, t), tile_of(b.x, t), ps[0:ROWS, 1, 0:D], ALU.add), "x0")
                    step(v.tensor_tensor(tile_of(b.x, t), tile_of(b.x, t), bproj[:], ALU.add), "x")
            if keys:
                for h in range(H):
                    part = moments[:, h * chunks:(h + 1) * chunks, :]
                    v.tensor_tensor(part, part, coef[:].unsqueeze(2).to_broadcast([128, chunks, wide]), ALU.mult).then_inc(cleared, 1)

        @block.gpsimd
        def _(p):
            pool.prime(p)
            p.wait_ge(cleared, 3)
            with p.Fori(0, TILES) as t:
                norm.gpsimd(p, t)
                p.wait_ge(*dve.now(t, "len2"))
                p.tensor_tensor(length[:, 1, :], length[:, 0, :], power[:], ALU.pow).then_inc(*pool.did("len"))

        @block.tensor
        def _(e):
            pe.prime(e)
            with e.Fori(0, TILES) as t:
                e.wait_ge(*dve.now(t, "xn"))
                e.wait_ge(*act.before(t, "xt" if keys else "xt1"))
                for k in range(2):
                    last = e.transpose(ps[:, 0, k * ROWS:(k + 1) * ROWS], xn[:, 128 * k:128 * k + 128], b.ident[0:ROWS, 0:ROWS])
                last.then_inc(*pe.did("turn"))
                e.wait_ge(*act.now(t, "xt"))
                e.wait_ge(*dve.before(t, "bias" if keys else "x0"))
                for k in range(2):
                    last = e.matmul(ps[0:ROWS, 1, 0:cols], lhsT=xt[:, k, :], rhs=w[:, k, :], start=k == 0, stop=k == 1)
                last.then_inc(*pe.did("qkv"))
                if keys:
                    for i, (lo, hi) in enumerate(spans):
                        e.wait_ge(*dve.before(t, f"mo{i}"))
                        for u in range(lo, hi):
                            h, k = divmod(u, chunks)
                            if k == 0 or u == lo:
                                e.wait_ge(*dve.now(t, f"f{h}"))
                                e.wait_ge(*act.now(t, f"lin{h}"))
                            last = e.matmul(ps[:, 2 + i, (u - lo) * wide:(u - lo + 1) * wide],
                                            lhsT=feat[:, h, 128 * k:128 * k + 128], rhs=values[:, h, :], start=True, stop=True)
                        last.then_inc(*pe.did(f"mo{i}"))
                else:
                    e.wait_ge(*dve.before(t, "out"))
                    for h in range(H):
                        e.wait_ge(*dve.now(t, f"f{h}"))
                        e.wait_ge(*act.now(t, f"lin{h}"))
                        for m, (lo, hi) in enumerate(((0, 3), (3, chunks))):
                            e.wait_ge(*(act.now(t, f"ft{h - 2}_{m}") if h >= 2 else act.before(t, f"ft{H - 2 + h}_{m}")))
                            for k in range(lo, hi):
                                last = e.transpose(ps[:, 3 + 2 * (h % 2) + m, (k - lo) * ROWS:(k - lo + 1) * ROWS],
                                                   feat[:, h, 128 * k:128 * k + 128], b.ident[0:ROWS, 0:ROWS])
                            last.then_inc(*pe.did(f"ft{h}_{m}"))
                        e.wait_ge(*act.now(t, f"ft{h}_1"))
                        for k in range(chunks):
                            last = e.matmul(ps[0:ROWS, 2, h * wide:(h + 1) * wide], lhsT=featt[:, h % 2, k, :],
                                            rhs=moments[:, h * chunks + k, :], start=k == 0, stop=k == chunks - 1)
                        last.then_inc(*pe.did(f"y{h}"))
                    e.wait_ge(*dve.now(t, "out"))
                    for k in range(2):
                        last = e.transpose(ps[:, 0, k * ROWS:(k + 1) * ROWS], y[:, 128 * k:128 * k + 128], b.ident[0:ROWS, 0:ROWS])
                    last.then_inc(*pe.did("turn1"))
                    e.wait_ge(*act.now(t, "xt1"))
                    for k in range(2):
                        last = e.matmul(ps[0:ROWS, 1, 0:D], lhsT=xt1[:, k, :], rhs=proj[:, k, :], start=k == 0, stop=k == 1)
                    last.then_inc(*pe.did("proj"))

        @block.scalar
        def _(a):
            act.prime(a)
            a.wait_ge(cleared, 3)
            with a.Fori(0, TILES) as t:
                a.wait_ge(*pe.now(t, "turn"))
                a.wait_ge(*pe.before(t, "qkv"))
                a.activation(xt[:].rearrange("p k n -> p (k n)"), ps[:, 0, 0:2 * ROWS], ACT.Copy).then_inc(*act.did("xt"))
                a.wait_ge(*dve.now(t, "unit"))
                a.wait_ge(*(pe.before(t, "mo2") if keys else pe.before(t, f"ft{H - 1}_1")))
                for h in range(H):
                    a.activation(feat[:, h, QUAD:QUAD + HD], unit[:, h, 0:HD], ACT.Copy).then_inc(*act.did(f"lin{h}"))
                if not keys:
                    for h in range(H):
                        for m, (lo, hi) in enumerate(((0, 3), (3, chunks))):
                            a.wait_ge(*pe.now(t, f"ft{h}_{m}"))
                            if m == 0:
                                a.wait_ge(*(pe.now(t, f"y{h - 2}") if h >= 2 else pe.before(t, f"y{H - 2 + h}")))
                            a.activation(featt[:, h % 2, lo:hi, :].rearrange("p k n -> p (k n)"),
                                         ps[:, 3 + 2 * (h % 2) + m, 0:(hi - lo) * ROWS], ACT.Copy).then_inc(*act.did(f"ft{h}_{m}"))
                    a.wait_ge(*pe.now(t, "turn1"))
                    a.wait_ge(*pe.before(t, "proj"))
                    a.activation(xt1[:].rearrange("p k n -> p (k n)"), ps[:, 0, 0:2 * ROWS], ACT.Copy).then_inc(*act.did("xt1"))


def moe(b, ctx):
    nc, ps = b.nc, b.ps
    parts = EF // 128
    xts = b.sb(ctx, "xts", [128, 2, N])
    y = b.sb(ctx, "y", [ROWS, TILES, D])
    gates = b.sb(ctx, "gates", [ROWS, TILES, EXPERTS])
    with ExitStack() as c:
        gw = b.sb(c, "gw", [128, 2, EXPERTS])
        gb = b.sb(c, "gb", [ROWS, EXPERTS])
        b2 = b.sb(c, "b2", [EXPERTS, D])
        load(b, [(gw[:], b.ins["L1_ffn_gate_w"].rearrange("(k p) n -> p k n", p=128)),
                 (gb[:], broadcast(b.ins["L1_ffn_gate_b"], ROWS)), (b2[:], b.ins["L1_ffn_b2"])])
        dve = Steps(b.sem(c, "g_dve"), RowNorm.steps() + ["xn", "logits", "max", "index", "indexf", "gap", "add", "inv", "w2",
                    "one0", "one1", "gates", "y"])
        pool = Steps(b.sem(c, "g_pool"), ["root"])
        pe = Steps(b.sem(c, "g_pe"), ["turn", "logits", "turng", "b2"])
        act = Steps(b.sem(c, "g_act"), ["xt", "xs", "exp", "gt"])
        norm = RowNorm(b, c, dve, pool)
        xn = b.sb(c, "xn", [ROWS, D])
        xt = b.sb(c, "xt", [128, 2, ROWS])
        logits = b.sb(c, "logits", [ROWS, EXPERTS])
        top = b.sb(c, "top", [ROWS, 8])
        index = b.sb(c, "index", [ROWS, 8], U32)
        indexf = b.sb(c, "indexf", [ROWS, 8])
        s = b.sb(c, "s", [ROWS, 4])
        one = b.sb(c, "one", [ROWS, 2, EXPERTS])
        gt = b.sb(c, "gt", [EXPERTS, ROWS])
        block = c.enter_context(nc.Block())

        @block.vector
        def _(v):
            dve.prime(v)
            with v.Fori(0, TILES) as t:
                def step(ins, name):
                    ins.then_inc(*dve.did(name))
                    v.wait_ge(*dve.now(t, name))

                norm.vector(v, t, tile_of(b.x, t), 1e-5)
                v.wait_ge(*pe.before(t, "turn"))
                step(norm.scaled(v, xn[:], tile_of(b.x, t)), "xn")
                v.wait_ge(*pe.now(t, "logits"))
                step(v.tensor_tensor(logits[:], ps[0:ROWS, 1, 0:EXPERTS], gb[:], ALU.add), "logits")
                v.sem_inc(norm.passed, 1)
                step(v.max(top[:], logits[:]), "max")
                v.sem_inc(norm.passed, 1)
                step(v.max_index(index[:], top[:], logits[:]), "index")
                step(v.tensor_scalar(indexf[:], index[:], 1.0, None, ALU.mult), "indexf")
                step(v.tensor_tensor(s[:, 0:1], top[:, 1:2], top[:, 0:1], ALU.subtract), "gap")
                v.wait_ge(*act.now(t, "exp"))
                step(v.tensor_scalar(s[:, 2:3], s[:, 1:2], 1.0, None, ALU.add), "add")
                step(v.reciprocal(s[:, 2:3], s[:, 2:3]), "inv")
                step(v.tensor_tensor(s[:, 3:4], s[:, 1:2], s[:, 2:3], ALU.mult), "w2")
                for i in range(2):
                    step(v.tensor_scalar(one[:, i, :], b.row_no[0:ROWS, 0:EXPERTS], indexf[:, i:i + 1], s[:, 2 + i:3 + i],
                                         ALU.is_equal, ALU.mult), f"one{i}")
                g_t = tile_of(gates, t)
                step(v.tensor_tensor(g_t, one[:, 0, :], one[:, 1, :], ALU.add), "gates")
                v.wait_ge(*pe.now(t, "b2"))
                step(v.tensor_tensor(tile_of(y, t), ps[0:ROWS, 3, 0:D], xn[:], ALU.add), "y")

        @block.gpsimd
        def _(p):
            pool.prime(p)
            with p.Fori(0, TILES) as t:
                norm.gpsimd(p, t)

        @block.tensor
        def _(e):
            pe.prime(e)
            with e.Fori(0, TILES) as t:
                e.wait_ge(*dve.now(t, "xn"))
                e.wait_ge(*act.before(t, "xs"))
                for k in range(2):
                    last = e.transpose(ps[:, 0, k * ROWS:(k + 1) * ROWS], xn[:, 128 * k:128 * k + 128], b.ident[0:ROWS, 0:ROWS])
                last.then_inc(*pe.did("turn"))
                e.wait_ge(*act.now(t, "xt"))
                e.wait_ge(*dve.before(t, "logits"))
                for k in range(2):
                    last = e.matmul(ps[0:ROWS, 1, 0:EXPERTS], lhsT=xt[:, k, :], rhs=gw[:, k, :], start=k == 0, stop=k == 1)
                last.then_inc(*pe.did("logits"))
                e.wait_ge(*dve.now(t, "gates"))
                e.wait_ge(*act.before(t, "gt"))
                for i in range(2):
                    last = e.matmul(ps[0:EXPERTS, 2, 0:ROWS], lhsT=one[:, i, :], rhs=b.ident[0:ROWS, 0:ROWS], start=i == 0, stop=i == 1)
                last.then_inc(*pe.did("turng"))
                e.wait_ge(*act.now(t, "gt"))
                e.wait_ge(*dve.before(t, "y"))
                e.matmul(ps[0:ROWS, 3, 0:D], lhsT=gt[:], rhs=b2[:], start=True, stop=True).then_inc(*pe.did("b2"))

        @block.scalar
        def _(a):
            act.prime(a)
            with a.Fori(0, TILES) as t:
                a.wait_ge(*pe.now(t, "turn"))
                a.wait_ge(*pe.before(t, "logits"))
                a.activation(xt[:].rearrange("p k n -> p (k n)"), ps[:, 0, 0:2 * ROWS], ACT.Copy).then_inc(*act.did("xt"))
                a.activation(xts[:, :, bass.ds(t * ROWS, ROWS)], ps[:, 0, 0:2 * ROWS].rearrange("p (k n) -> p k n", k=2),
                             ACT.Copy).then_inc(*act.did("xs"))
                a.wait_ge(*dve.now(t, "gap"))
                a.activation(s[:, 1:2], s[:, 0:1], ACT.Exp).then_inc(*act.did("exp"))
                a.wait_ge(*pe.now(t, "turng"))
                a.activation(gt[:], ps[0:EXPERTS, 2, 0:ROWS], ACT.Copy).then_inc(*act.did("gt"))

    group = 5
    groups = TILES // group
    split = ((0, 3 * ROWS), (3 * ROWS, 5 * ROWS))
    with ExitStack() as c:
        w1 = b.sb(c, "w1", [128, 2, 2, EF])
        w2 = b.sb(c, "w2", [128, 2, parts, D])
        b1 = b.sb(c, "b1", [128, 2, parts])
        hidden = b.sb(c, "hidden", [128, parts, group * ROWS])
        gates2 = gates[:].rearrange("p t e -> p (t e)")
        dve = Steps(b.sem(c, "e_dve"), [f"y{i}" for i in range(group)])
        pe = Steps(b.sem(c, "e_pe"), [f"h{m}_{i}" for m in range(parts) for i in range(2)] + [f"y{i}" for i in range(group)],
                   lead=2 * groups)
        act = Steps(b.sem(c, "e_act"), [f"h{m}_{i}" for m in range(parts) for i in range(2)], lead=2 * groups)
        loaded = [b.sem(c, f"loaded{i}") for i in range(2)]
        block = c.enter_context(nc.Block())

        @block.sync
        def _(sp):
            with sp.Fori(0, EXPERTS // 2) as r:
                for i in range(2):
                    ex = r * 2 + i
                    sp.wait_ge(*pe.back(ex * groups, groups + 1, f"y{group - 1}"))
                    sp.dma_start(w1[:, i], b.ins["moe_w1"][bass.ds(ex * 128, 128), :].rearrange("p (k f) -> p k f", k=2)).then_inc(loaded[i], 16)
                    sp.dma_start(w2[:, i], b.ins["moe_w2"][bass.ds(ex * 128, 128), :].rearrange("p (k f) -> p k f", k=parts)).then_inc(loaded[i], 16)
                    sp.wait_ge(*act.back(ex * groups, groups + 1, f"h{parts - 1}_1"))
                    sp.dma_start(b1[:, i], b.ins["moe_b1"][bass.ds(ex * 128, 128), :]).then_inc(loaded[i], 16)

        @block.tensor
        def _(e):
            pe.prime(e)
            with e.Fori(0, EXPERTS // 2) as r:
                for i in range(2):
                    with e.Fori(0, groups) as g:
                        e.wait_ge(loaded[i], r * 48 + 48)
                        t = (r * 2 + i) * groups + g
                        for m in range(parts):
                            for n, (lo, hi) in enumerate(split):
                                e.wait_ge(*(act.now(t, f"h{m - 2}_{n}") if m >= 2 else act.before(t, f"h{parts - 2 + m}_{n}")))
                                for k in range(2):
                                    last = e.matmul(ps[:, 2 * (m % 2) + n, 0:hi - lo], lhsT=w1[:, i, k, 128 * m:128 * m + 128],
                                                    rhs=xts[:, k, bass.ds(g * (group * ROWS) + lo, hi - lo)], start=k == 0, stop=k == 1)
                                last.then_inc(*pe.did(f"h{m}_{n}"))
                        e.wait_ge(*act.now(t, f"h{parts - 1}_1"))
                        for j in range(group):
                            e.wait_ge(*(dve.now(t, f"y{j - 4}") if j >= 4 else dve.before(t, f"y{j if j else 4}")))
                            for m in range(parts):
                                last = e.matmul(ps[0:ROWS, 4 + j % 4, 0:D], lhsT=hidden[:, m, j * ROWS:(j + 1) * ROWS],
                                                rhs=w2[:, i, m, :], start=m == 0, stop=m == parts - 1)
                            last.then_inc(*pe.did(f"y{j}"))

        @block.scalar
        def _(a):
            act.prime(a)
            with a.Fori(0, EXPERTS // 2) as r:
                for i in range(2):
                    with a.Fori(0, groups) as g:
                        a.wait_ge(loaded[i], r * 48 + 48)
                        t = (r * 2 + i) * groups + g
                        for m in range(parts):
                            for n, (lo, hi) in enumerate(split):
                                a.wait_ge(*pe.now(t, f"h{m}_{n}"))
                                if m == 0 and n == 0:
                                    a.wait_ge(*pe.before(t, f"y{group - 1}"))
                                a.activation(hidden[:, m, lo:hi], ps[:, 2 * (m % 2) + n, 0:hi - lo], ACT.Relu,
                                             bias=b1[:, i, m:m + 1]).then_inc(*act.did(f"h{m}_{n}"))

        @block.vector
        def _(v):
            dve.prime(v)
            with v.Fori(0, EXPERTS // 2) as r:
                for i in range(2):
                    with v.Fori(0, groups) as g:
                        t = (r * 2 + i) * groups + g
                        for j in range(group):
                            y_t = tile_of(y, g * group + j)
                            gate = gates2[:, bass.ds((g * group + j) * EXPERTS + (r * 2 + i), 1)]
                            v.wait_ge(*pe.now(t, f"y{j}"))
                            v.scalar_tensor_tensor(out=y_t, in0=ps[0:ROWS, 4 + j % 4, 0:D], scalar=gate, in1=y_t, op0=ALU.mult,
                                                   op1=ALU.add).then_inc(*dve.did(f"y{j}"))
                            v.wait_ge(*dve.now(t, f"y{j}"))

    with ExitStack() as c:
        gamma = b.sb(c, "gamma", [ROWS, D])
        beta = b.sb(c, "beta", [ROWS, D])
        load(b, [(gamma[:], broadcast(b.ins["L1_ffn_gamma"], ROWS)), (beta[:], broadcast(b.ins["L1_ffn_beta"], ROWS))])
        dve = Steps(b.sem(c, "o_dve"), RowNorm.steps() + ["y1", "y2", "y3", "x"])
        pool = Steps(b.sem(c, "o_pool"), ["root"])
        stored = b.sem(c, "out_stored")
        norm = RowNorm(b, c, dve, pool)
        block = c.enter_context(nc.Block())

        @block.vector
        def _(v):
            dve.prime(v)
            with v.Fori(0, TILES) as t:
                def step(ins, name):
                    ins.then_inc(*dve.did(name))
                    v.wait_ge(*dve.now(t, name))

                y_t = tile_of(y, t)
                norm.vector(v, t, y_t, 1e-5)
                step(norm.scaled(v, y_t, y_t), "y1")
                step(v.tensor_tensor(y_t, y_t, gamma[:], ALU.mult), "y2")
                step(v.tensor_tensor(y_t, y_t, beta[:], ALU.add), "y3")
                step(v.tensor_tensor(y_t, y_t, tile_of(b.x, t), ALU.add), "x")

        @block.gpsimd
        def _(p):
            pool.prime(p)
            with p.Fori(0, TILES) as t:
                norm.gpsimd(p, t)

        @block.sync
        def _(sp):
            with sp.Fori(0, TILES) as t:
                sp.wait_ge(*dve.now(t, "x"))
                sp.dma_start(b.out[bass.ds(t * ROWS, ROWS), :], tile_of(y, t)).then_inc(stored, 16)
            sp.wait_ge(stored, TILES * 16)


def mix1_factors():
    scale = float(HD) ** 0.25
    f = np.zeros(FEAT)
    for o in range(OFFS):
        f[o * HD:(o + 1) * HD] = 0.5 * (2.0 if 0 < o < HD // 2 else 1.0)
    f[QUAD:QUAD + HD] = scale ** 2
    f[QUAD + HD] = scale ** 4
    return np.ascontiguousarray((f / N).reshape(FEAT // 128, 128).T.astype(np.float32))


def program(nc, ins, out):
    b = Build(nc, ins, out)
    with ExitStack() as whole, ExitStack() as ctx:
        b.whole = whole
        constants(b, ctx)
        acc = b.sb(ctx, "acc", [ROWS, SLOTS * (D + HG)])
        e_all = b.sb(ctx, "e_all", [128, CHUNKS, HG])
        top = b.sb(ctx, "top", [ROWS, SLOTS * HG])

        def attend(c, g, which, source, norm, names, heads):
            w = graph_weights(b, c, *names, heads)
            own = node_tables(b, c, which, source, norm, w, heads)
            edge_scores(b, g, b.score[which], own, heads, e_all, top[:, 0:SLOTS * heads])
            edge_sums(b, g, b.table[which], heads, e_all, top[:, 0:SLOTS * heads], acc[:, 0:SLOTS * (D + heads)])

        def mean(heads, bias_name, into, add):
            with ExitStack() as c:
                bias = b.sb(c, "bias", [ROWS, D])
                load(b, [(bias[:], broadcast(b.ins[bias_name], ROWS))])
                edge_mean(b, acc, heads, bias[:], into, add)

        with ExitStack() as c:
            g = sort_edges(b, c, 0, "src", "dst", True)
            attend(c, g, 0, b.x, True, ("L0_gnn_W", "L0_gnn_a_self", "L0_gnn_a_neigh"), HG)
        with ExitStack() as c:
            gram = b.sb(c, "gram", [128, 2 * H, D + 1])
            kvo = b.sb(c, "kvo", [128, 2 * H, D + 1])
            with ExitStack() as c2:
                mix0_keys(b, gram, *phi_weights(b, c2, "k"))
            mix0_values(b, kvo, gram)
            mix0_queries(b, *phi_weights(b, c, "q"), kvo)
        mean(HG, "L0_gnn_bias", b.x, True)
        with ExitStack() as c:
            chosen = b.sb(c, "chosen", [ROWS, TILES])
            choose_rows(b, c, chosen)
            ffn0(b, chosen)
        clear_semaphores(b)
        with ExitStack() as c:
            b.x1 = b.sb(c, "x1", [ROWS, TILES, D])
            copy_rows(b, b.x1, b.x)
            with ExitStack() as c2:
                g = sort_edges(b, c2, 1, "dst", "src", False)
                with ExitStack() as c3:
                    attend(c3, g, 1, b.x, True, ("L1_gnn_W1", "L1_gnn_a_dst1", "L1_gnn_a_src1"), HG)
                with ExitStack() as c3:
                    y = b.sb(c3, "y", [ROWS, TILES, D])
                    mean(HG, "L1_gnn_b1", y, False)
                    attend(c3, g, 2, y, False, ("L1_gnn_W2", "L1_gnn_a_dst2", "L1_gnn_a_src2"), 1)
            mean(1, "L1_gnn_b2", b.x, True)
            moments = b.sb(c, "moments", [128, H * (FEAT // 128), HD + 1])
            mix1(b, True, moments)
            mix1(b, False, moments)
        with ExitStack() as c:
            moe(b, c)


def clear_semaphores(b):
    with b.nc.Block() as block:
        @block.sync
        def _(sp):
            for used in b.used:
                sp.sem_clear(used)
    b.used = []


def copy_rows(b, into, source):
    with ExitStack() as c:
        copied = b.sem(c, "copied")
        block = c.enter_context(b.nc.Block())

        @block.vector
        def _(v):
            v.tensor_copy(into[:], source[:]).then_inc(copied, 1)


def host_layout(i):
    c = np.ascontiguousarray
    a = {k: np.asarray(v) for k, v in i.items()}
    g = {
        "x": a["x"], "src": a["src"], "dst": a["dst"], "edge_weight": a["edge_weight"],
        "L0_gnn_W": a["L0_gnn_W"].transpose(1, 0, 2).reshape(D, D),
        "Wq_T": a["L0_mix_Wq"].reshape(D, H * KD).T, "Wk_T": a["L0_mix_Wk"].reshape(D, H * KD).T,
        "proj_T": a["L0_mix_proj"].T,
        "bq_columns": a["L0_mix_bq"].reshape(2 * H, 128).T, "bk_columns": a["L0_mix_bk"].reshape(2 * H, 128).T,
        "L0_mix_Wo": a["L0_mix_Wo"].reshape(H * KD, D),
        "bias1_columns": a["L0_mix_bias1"].reshape(2, 128).T,
    }
    g |= {
        "L0_ffn_wr": a["L0_ffn_wr"].reshape(D), "L0_ffn_br": a["L0_ffn_br"], "L0_ffn_w1": a["L0_ffn_w1"],
        "L0_ffn_w2": a["L0_ffn_w2"], "ffn_b1_columns": a["L0_ffn_b1"].reshape(HID // 128, 128).T, "L0_ffn_b2": a["L0_ffn_b2"],
        "L1_gnn_W1": a["L1_gnn_W1"], "L1_gnn_W2": a["L1_gnn_W2"], "L1_gnn_b1": a["L1_gnn_b1"], "L1_gnn_b2": a["L1_gnn_b2"],
        "Wqkv_T": a["L1_mix_Wqkv"].T, "L1_mix_bqkv": a["L1_mix_bqkv"], "Wproj_T": a["L1_mix_Wproj"].T,
        "L1_mix_bproj": a["L1_mix_bproj"], "L1_mix_temperature": a["L1_mix_temperature"].reshape(H),
        "mix1_coef": mix1_factors(),
        "L1_ffn_gate_w": a["L1_ffn_gate_w"], "L1_ffn_gate_b": a["L1_ffn_gate_b"], "L1_ffn_b2": a["L1_ffn_b2"],
        "moe_w1": a["L1_ffn_w1"].reshape(EXPERTS, 2, 128, EF).transpose(0, 2, 1, 3).reshape(EXPERTS * 128, 2 * EF),
        "moe_w2": a["L1_ffn_w2"].reshape(EXPERTS, EF // 128, 128, D).transpose(0, 2, 1, 3).reshape(EXPERTS * 128, EF // 128 * D),
        "moe_b1": a["L1_ffn_b1"].reshape(EXPERTS, EF // 128, 128).transpose(0, 2, 1).reshape(EXPERTS * 128, EF // 128),
        "L1_ffn_gamma": a["L1_ffn_gamma"], "L1_ffn_beta": a["L1_ffn_beta"],
    }
    for n in ("L1_gnn_a_src1", "L1_gnn_a_dst1", "L1_gnn_a_src2", "L1_gnn_a_dst2"):
        g[n] = a[n].reshape(D)
    for n in ("Wq", "Wk", "Wv"):
        g[f"L0_mix_{n}"] = a[f"L0_mix_{n}"].reshape(D, H * KD)
    for n in ("bq", "bk", "bv"):
        g[f"L0_mix_{n}"] = a[f"L0_mix_{n}"].reshape(H * KD)
    for n in ("L0_mix_bo", "L0_mix_g1", "L0_mix_beta1", "L0_mix_bias2", "L0_mix_g2", "L0_mix_beta2", "L0_mix_W1", "L0_mix_W2"):
        g[n] = a[n]
    for n in ("L0_gnn_a_self", "L0_gnn_a_neigh", "L0_gnn_bias"):
        g[n] = a[n].reshape(D)
    return {k: c(v) for k, v in g.items()}


def kernel(**inputs):
    import concourse.bacc as bacc
    from concourse.bass_utils import run_bass_kernel_spmd as run

    nc = bacc.Bacc("TRN2", target_bir_lowering=False, num_devices=1)
    arrays = host_layout(inputs)
    ins = {k: nc.dram_tensor(f"in_{k}", v.shape, mybir.dt.from_np(v.dtype), kind="ExternalInput").ap() for k, v in arrays.items()}
    out = nc.dram_tensor("out_x", (N, D), FP32, kind="ExternalOutput").ap()
    program(nc, ins, out)
    r = run(nc, [{f"in_{k}": v for k, v in arrays.items()}], core_ids=[0])
    return r.results[0]["out_x"]
```

```python
import numpy as np
import concourse.bass as bass
from concourse import mybir
from contextlib import ExitStack

FP32 = mybir.dt.float32
BF16 = mybir.dt.bfloat16
I32 = mybir.dt.int32
U32 = mybir.dt.uint32
ALU = mybir.AluOpType
ACT = mybir.ActivationFunctionType
AX = mybir.AxisListType

N, D = 3125, 256
ROWS = 125
TILES = N // ROWS
SLOTS = TILES + 1
NE = 53125
ECOLS = 416
LAST = NE - 127 * ECOLS
CHUNKS = 448
SET = 8
BIG = 2.0 ** 120
HG = 4
H, KD = 8, 256
KSCALE = KD ** -0.25
KK = 1561
HID = 1024
HD = 32
OFFS = HD // 2 + 1
FEAT = 640
QUAD = OFFS * HD
EXPERTS, EF = 16, 512
GROUP = 5
GROUPS = TILES // GROUP


class Steps:

    def __init__(self, sem, names, lead=1):
        self.sem, self.names, self.lead, self.at = sem, list(names), lead, 0

    def prime(self, eng):
        eng.sem_inc(self.sem, self.lead * len(self.names))

    def did(self, name):
        assert self.names[self.at % len(self.names)] == name, (self.names[self.at % len(self.names)], name)
        self.at += 1
        return self.sem, 1

    def back(self, t, rounds, name):
        assert rounds <= self.lead
        return self.sem, t * len(self.names) + ((self.lead - rounds) * len(self.names) + self.names.index(name) + 1)

    def now(self, t, name):
        return self.back(t, 0, name)

    def before(self, t, name):
        return self.back(t, 1, name)


class Build:

    def __init__(self, nc, ins, out):
        self.nc, self.ins, self.out = nc, ins, out
        self.count = 0
        self.used = []

    def sem(self, ctx, name):
        self.count += 1
        self.used.append(ctx.enter_context(self.nc.semaphore(f"{name}_{self.count}")))
        return self.used[-1]

    def sem_of_gathers(self, name):
        self.count += 1
        return self.whole.enter_context(self.nc.semaphore(f"{name}_{self.count}"))

    def sb(self, ctx, name, shape, dt=FP32):
        self.count += 1
        return ctx.enter_context(self.nc.sbuf_tensor(f"{name}_{self.count}", shape, dt))

    def dram(self, name, shape, dt=FP32):
        return self.nc.dram_tensor(name, shape, dt, kind="Internal").ap()


def constants(b, ctx):
    nc = b.nc
    b.x = b.sb(ctx, "x", [ROWS, TILES, D])
    b.ident = b.sb(ctx, "ident", [128, 128])
    b.identb = b.sb(ctx, "identb", [128, 128], BF16)
    b.before_me = b.sb(ctx, "before_me", [128, 128])
    b.ones = b.sb(ctx, "ones", [128, 128])
    b.onesb = b.sb(ctx, "onesb", [128, 128], BF16)
    b.row_no = b.sb(ctx, "row_no", [128, CHUNKS])
    b.half = b.sb(ctx, "half", [128, 1])
    b.ps = ctx.enter_context(nc.psum_tensor("ps", [128, 8, 512], FP32))
    b.table = [b.dram(f"table{i}", [SLOTS * ROWS, D]) for i in range(3)]
    b.score = [b.dram(f"score{i}", [SLOTS * ROWS, heads]) for i, heads in enumerate((HG, HG, 1))]
    zeros = b.sb(ctx, "zeros", [ROWS, D])
    with ExitStack() as c:
        pool_did = b.sem(c, "const_pool")
        dve_did = b.sem(c, "const_dve")
        loaded = b.sem(c, "x_loaded")
        stored = b.sem(c, "zeros_stored")
        block = c.enter_context(nc.Block())

        @block.sync
        def _(sp):
            sp.dma_start(b.x[:], b.ins["x"].rearrange("(t p) d -> p t d", p=ROWS)).then_inc(loaded, 16)
            sp.wait_ge(dve_did, 4)
            for i in range(3):
                sp.dma_start(b.table[i][N:SLOTS * ROWS, :], zeros[:]).then_inc(stored, 16)
                sp.dma_start(b.score[i][N:SLOTS * ROWS, :], zeros[:, 0:(HG, HG, 1)[i]]).then_inc(stored, 16)
            sp.wait_ge(stored, 96)
            sp.wait_ge(loaded, 16)

        @block.vector
        def _(dve):
            dve.memset(b.ones[:], 1.0).then_inc(dve_did, 1)
            dve.memset(b.onesb[:], 1.0).then_inc(dve_did, 1)
            dve.memset(b.half[:], -0.5).then_inc(dve_did, 1)
            dve.memset(zeros[:], 0.0).then_inc(dve_did, 1)
            dve.wait_ge(pool_did, 2)
            dve.tensor_copy(b.identb[:], b.ident[:]).then_inc(dve_did, 1)

        @block.gpsimd
        def _(pool):
            pool.memset(b.ident[:], 0.0).then_inc(pool_did, 1)
            pool.wait_ge(pool_did, 1)
            pool.affine_select(out=b.ident[:], in_=b.ident[:], compare_op=ALU.not_equal, fill=1.0, base=0,
                               pattern=[[-1, 128]], channel_multiplier=1).then_inc(pool_did, 1)
            pool.wait_ge(dve_did, 1)
            pool.affine_select(out=b.before_me[:], in_=b.ones[:], compare_op=ALU.is_gt, fill=0.0, base=0,
                               pattern=[[1, 128]], channel_multiplier=-1).then_inc(pool_did, 1)
            pool.iota(b.row_no[:], [[1, CHUNKS]], base=0, channel_multiplier=0,
                      allow_small_or_imprecise_dtypes=True).then_inc(pool_did, 1)


class EdgePlan:

    def __init__(self, b, ctx, which):
        self.listed = b.dram(f"listed{which}", [128 * CHUNKS, 4])
        self.tilef = b.sb(ctx, "tilef", [128, CHUNKS])
        self.rec = b.sb(ctx, "rec", [128, ECOLS, 4])
        self.place = b.sb(ctx, "place", [128, ECOLS], I32)


def plan_edges(b, plan, key_name, nbr_name, weighted):
    nc, ps = b.nc, b.ps
    listed, rec, tilef, place = plan.listed, plan.rec, plan.tilef, plan.place
    with ExitStack() as c:
        raw = b.sb(c, "raw", [128, 2, ECOLS], I32)
        start = b.sb(c, "start", [128, SLOTS + 1])
        ge = b.sb(c, "ge", [128, ECOLS])
        inside = b.sb(c, "inside", [128, SLOTS, ECOLS], BF16)
        upto = b.sb(c, "upto", [128, SLOTS, ECOLS])
        small = b.sb(c, "small", [128, 8, SLOTS])
        smalli = b.sb(c, "smalli", [128, SLOTS], I32)
        zero = b.sb(c, "zero", [128, ECOLS])
        pos = b.sb(c, "pos", [128, ECOLS])
        part = b.sb(c, "part", [128, ECOLS])
        posi = b.sb(c, "posi", [128, 2, ECOLS], I32)
        pad = b.sb(c, "pad", [128, CHUNKS, 4])
        loaded, dve_did = b.sem(c, "edges_loaded"), b.sem(c, "sort_dve")
        pe_did, pool_did, padded = b.sem(c, "sort_pe"), b.sem(c, "sort_pool"), b.sem(c, "padded")
        block = c.enter_context(nc.Block())
        links = [0]

        @block.sync
        def _(sp):
            sp.wait_ge(pool_did, 3)
            k = 0
            for i, name in enumerate((key_name, nbr_name)):
                src = b.ins[name]
                sp.dma_start(raw[0:127, i, :], src[0:127 * ECOLS].rearrange("(p c) -> p c", c=ECOLS)).then_inc(loaded, 16)
                sp.dma_start(raw[127:128, i, 0:LAST], src[127 * ECOLS:NE].unsqueeze(0)).then_inc(loaded, 16)
                k += 32
            if weighted:
                src = b.ins["edge_weight"]
                sp.dma_start(ge[0:127, :], src[0:127 * ECOLS].rearrange("(p c) -> p c", c=ECOLS)).then_inc(loaded, 16)
                sp.dma_start(ge[127:128, 0:LAST], src[127 * ECOLS:NE].unsqueeze(0)).then_inc(loaded, 16)
            sp.wait_ge(pool_did, 5)
            sp.dma_start(listed.rearrange("(p c) f -> p (c f)", p=128), pad[:].rearrange("p c f -> p (c f)")).then_inc(padded, 16)
            sp.wait_ge(padded, 16)

        @block.gpsimd
        def _(pool):
            pool.memset(raw[:], N).then_inc(pool_did, 1)
            pool.iota(start[:], [[ROWS, SLOTS + 1]], base=0, channel_multiplier=0,
                      allow_small_or_imprecise_dtypes=True).then_inc(pool_did, 1)
            pool.memset(ge[:], 0.0).then_inc(pool_did, 1)
            pool.memset(pad[:, :, 0:2], float(N)).then_inc(pool_did, 1)
            pool.memset(pad[:, :, 2:4], 0.0).then_inc(pool_did, 1)

        @block.tensor
        def _(pe):
            pe.wait_ge(dve_did, 4 + 3 * SLOTS + 1)
            pe.matmul(ps[:, 0, 0:SLOTS], lhsT=b.before_me[:], rhs=small[:, 0, :], start=True, stop=True).then_inc(pe_did, 1)
            pe.matmul(ps[:, 1, 0:SLOTS], lhsT=b.ones[:], rhs=small[:, 0, :], start=True, stop=True).then_inc(pe_did, 1)

        @block.vector
        def _(dve):
            def link(ins):
                links[0] += 1
                ins.then_inc(dve_did, 1)
                dve.wait_ge(dve_did, links[0])

            link(dve.memset(rec[:], 0.0))
            link(dve.memset(zero[:], 0.0))
            dve.wait_ge(loaded, 96 if weighted else 64)
            dve.wait_ge(pool_did, 2)
            link(dve.tensor_copy(rec[:, :, 0:2].rearrange("p c f -> p f c"), raw[:]))
            if weighted:
                link(dve.tensor_copy(rec[:, :, 2], ge[:]))
            else:
                link(dve.tensor_copy(rec[:, :, 2], zero[:]))
            base = links[0]
            with dve.Fori(0, SLOTS) as t:
                dve.tensor_scalar(ge[:], rec[:, :, 0], start[:, bass.ds(t, 1)], None, ALU.is_ge).then_inc(dve_did, 1)
                dve.wait_ge(dve_did, t * 3 + (base + 1))
                dve.scalar_tensor_tensor(out=inside[:, bass.ds(t, 1), :].rearrange("p a c -> p (a c)"), in0=rec[:, :, 0],
                                         scalar=start[:, bass.ds(t + 1, 1)], in1=ge[:], op0=ALU.is_lt,
                                         op1=ALU.mult).then_inc(dve_did, 1)
                dve.wait_ge(dve_did, t * 3 + (base + 2))
                dve.tensor_tensor_scan(upto[:, bass.ds(t, 1), :].rearrange("p a c -> p (a c)"), zero[:],
                                       inside[:, bass.ds(t, 1), :].rearrange("p a c -> p (a c)"), 0.0, ALU.add,
                                       ALU.add).then_inc(dve_did, 1)
                dve.wait_ge(dve_did, t * 3 + (base + 3))
            links[0] = base + 3 * SLOTS
            link(dve.tensor_copy(small[:, 0, :], upto[:, :, ECOLS - 1]))
            dve.wait_ge(pe_did, 2)
            link(dve.tensor_scalar(smalli[:], ps[:, 1, 0:SLOTS], 127.0, None, ALU.add))
            link(dve.tensor_scalar(smalli[:], smalli[:], 7, None, ALU.arith_shift_right))
            link(dve.tensor_copy(small[:, 1, :], smalli[:]))
            link(dve.tensor_tensor_scan(small[:, 2, :], zero[:, 0:SLOTS], small[:, 1, :], 0.0, ALU.add, ALU.add))
            link(dve.tensor_tensor(small[:, 3, :], small[:, 2, :], small[:, 1, :], ALU.subtract))
            link(dve.tensor_scalar(small[:, 4, :], small[:, 3, :], 128.0, -1.0, ALU.mult, ALU.add))
            link(dve.tensor_tensor(small[:, 5, :], small[:, 4, :], ps[:, 0, 0:SLOTS], ALU.add))
            link(dve.memset(pos[:], 0.0))
            link(dve.memset(tilef[:], 0.0))
            base = links[0]
            with dve.Fori(0, SLOTS) as t:
                dve.scalar_tensor_tensor(out=part[:], in0=upto[:, bass.ds(t, 1), :].rearrange("p a c -> p (a c)"),
                                         scalar=small[:, 5, bass.ds(t, 1)],
                                         in1=inside[:, bass.ds(t, 1), :].rearrange("p a c -> p (a c)"), op0=ALU.add,
                                         op1=ALU.mult).then_inc(dve_did, 1)
                dve.wait_ge(dve_did, t * 3 + (base + 1))
                dve.tensor_tensor(pos[:], pos[:], part[:], ALU.add).then_inc(dve_did, 1)
                dve.scalar_tensor_tensor(out=tilef[:], in0=b.row_no[:], scalar=small[:, 2, bass.ds(t, 1)], in1=tilef[:],
                                         op0=ALU.is_ge, op1=ALU.add).then_inc(dve_did, 1)
                dve.wait_ge(dve_did, t * 3 + (base + 3))
            links[0] = base + 3 * SLOTS
            link(dve.tensor_copy(posi[:, 0, :], pos[:]))
            link(dve.tensor_scalar(posi[:, 1, :], posi[:, 0, :], 7, None, ALU.arith_shift_right))
            link(dve.tensor_scalar(posi[:, 0, :], posi[:, 0, :], 127, None, ALU.bitwise_and))
            link(dve.tensor_copy(pos[:], posi[:, 0, :]))
            link(dve.tensor_copy(part[:], posi[:, 1, :]))
            link(dve.scalar_tensor_tensor(out=pos[:], in0=pos[:], scalar=float(CHUNKS), in1=part[:], op0=ALU.mult, op1=ALU.add))
            link(dve.tensor_copy(place[:], pos[:]))
            link(dve.tensor_scalar(tilef[:], tilef[:], float(TILES), None, ALU.min))


class Scatter:

    def __init__(self, b, ctx, plan):
        self.plan = plan
        self.stage = b.sb(ctx, "stage", [128, 2, SET, 4])
        self.place = b.sb(ctx, "stage_place", [128, 2, SET], I32)
        self.done = [b.sem_of_gathers(f"scattered{i}") for i in range(2)]
        self.copied, self.staged, self.free = b.sem(ctx, "copied"), b.sem(ctx, "staged"), b.sem(ctx, "stage_free")

    def sync(self, sp):
        sp.sem_inc(self.free, 2)
        with sp.Fori(0, ECOLS // (2 * SET)) as r:
            for i in range(2):
                sp.wait_ge(self.done[i], r * (SET * 16) + SET * 16)
                sp.sem_inc(self.free, 1)

    def gpsimd(self, pool):
        rec, place = self.plan.rec, self.plan.place
        with pool.Fori(0, ECOLS // (2 * SET)) as r:
            for i in range(2):
                pool.wait_ge(self.free, r * 2 + (i + 1))
                pool.tensor_copy(self.stage[:, i], rec[:, bass.ds(r * (2 * SET) + i * SET, SET), :]).then_inc(self.copied, 1)
                pool.tensor_copy(self.place[:, i], place[:, bass.ds(r * (2 * SET) + i * SET, SET)]).then_inc(self.copied, 1)
                pool.wait_ge(self.copied, r * 4 + (2 * i + 2))
                pool.sem_inc(self.staged, 1)
                for j in range(SET):
                    pool.indirect_dma_start(self.plan.listed[:, :], bass.IndirectOffsetOnAxis(ap=self.place[:, i, j:j + 1], axis=0),
                                            self.stage[:, i, j, :], None).then_inc(self.done[i], 16)


def listed_edges(b, ctx, plan, weighted):
    got = {
        "nbr": b.sb(ctx, "nbr", [128, CHUNKS], I32),
        "lane": b.sb(ctx, "lane", [128, CHUNKS]),
        "tile": b.sb(ctx, "tile", [1, CHUNKS], I32),
        "w": b.sb(ctx, "w", [128, CHUNKS]) if weighted else None,
    }
    with ExitStack() as c:
        back = b.sb(c, "back", [128, CHUNKS, 4])
        relisted, taken = b.sem(c, "relisted"), b.sem(c, "taken")
        block = c.enter_context(b.nc.Block())

        @block.sync
        def _(sp):
            sp.dma_start(back[:].rearrange("p c f -> p (c f)"), plan.listed.rearrange("(p c) f -> p (c f)", p=128)).then_inc(relisted, 16)

        @block.vector
        def _(dve):
            dve.tensor_copy(got["tile"][:], plan.tilef[0:1, :]).then_inc(taken, 1)
            dve.wait_ge(relisted, 16)
            dve.tensor_copy(got["nbr"][:], back[:, :, 1]).then_inc(taken, 1)
            dve.scalar_tensor_tensor(out=got["lane"][:], in0=plan.tilef[:], scalar=-float(ROWS), in1=back[:, :, 0],
                                     op0=ALU.mult, op1=ALU.add).then_inc(taken, 1)
            if weighted:
                dve.tensor_copy(got["w"][:], back[:, :, 2]).then_inc(taken, 1)
    return got


class RowStats:

    def __init__(self, b, ctx, eps):
        self.b, self.eps = b, eps
        self.stats = b.sb(ctx, "stats", [ROWS, TILES * 6])
        self.mean = b.sb(ctx, "mean", [ROWS, TILES * 2])
        self.root = b.sb(ctx, "root", [ROWS, TILES])
        self.counted, self.rooted = b.sem(ctx, "stats_counted"), b.sem(ctx, "rooted")

    def variance(self):
        return self.mean[:].rearrange("p (t s) -> p t s", s=2)[:, :, 1]

    def vector(self, v, source):
        with v.Fori(0, TILES) as t:
            v.bn_stats(self.stats[:, bass.ds(t * 6, 6)], source[:, bass.ds(t, 1), 0:D].rearrange("p a d -> p (a d)")).then_inc(self.counted, 1)
        v.wait_ge(self.counted, TILES)
        for t in range(TILES):
            v.bn_aggr(self.mean[:, 2 * t:2 * t + 2], self.stats[:, 6 * t:6 * t + 6]).then_inc(self.counted, 1)
        v.wait_ge(self.counted, 2 * TILES)
        v.tensor_scalar(self.variance(), self.variance(), self.eps, None, ALU.add).then_inc(self.counted, 1)
        v.wait_ge(self.rooted, 1)

    def gpsimd(self, p):
        p.wait_ge(self.counted, 2 * TILES + 1)
        p.tensor_tensor(self.root[:], self.variance(), self.b.half[0:ROWS, :].to_broadcast([ROWS, TILES]), ALU.pow).then_inc(self.rooted, 1)

    def means(self, g):
        return self.mean[:].rearrange("p (t s) -> p t s", s=2)[:, bass.ds(g * GROUP, GROUP), 0:1].to_broadcast([ROWS, GROUP, D])

    def roots(self, g):
        return self.root[:, bass.ds(g * GROUP, GROUP)].unsqueeze(2).to_broadcast([ROWS, GROUP, D])


def group_of(source, g):
    return source[:, bass.ds(g * GROUP, GROUP), 0:D]


def over_group(row):
    return row[:].unsqueeze(1).to_broadcast([ROWS, GROUP, D])


def rows_and_columns(b, source, out, xts, eps=None, gamma=None, beta=None):
    nc, ps = b.nc, b.ps
    chain = (["sub", "root"] if eps else ["same"]) + (["gamma", "beta"] if gamma else [])
    with ExitStack() as c:
        dve = Steps(b.sem(c, "rc_dve"), chain)
        pe = Steps(b.sem(c, "rc_pe"), [f"turn{j}" for j in range(GROUP)])
        act = Steps(b.sem(c, "rc_act"), [f"xt{j}" for j in range(GROUP)] + (["out"] if out else []))
        stats = RowStats(b, c, eps) if eps else None
        rows = b.sb(c, "rows", [ROWS, GROUP, D])
        block = c.enter_context(nc.Block())

        @block.vector
        def _(v):
            dve.prime(v)
            if eps:
                stats.vector(v, source)
            with v.Fori(0, GROUPS) as g:
                v.wait_ge(*pe.before(g, f"turn{GROUP - 1}"))
                if out:
                    v.wait_ge(*act.before(g, "out"))
                if eps:
                    v.tensor_tensor(rows[:], group_of(source, g), stats.means(g), ALU.subtract).then_inc(*dve.did("sub"))
                    v.wait_ge(*dve.now(g, "sub"))
                    v.tensor_tensor(rows[:], rows[:], stats.roots(g), ALU.mult).then_inc(*dve.did("root"))
                else:
                    v.tensor_scalar(rows[:], group_of(source, g), 1.0, None, ALU.mult).then_inc(*dve.did("same"))
                if gamma:
                    v.wait_ge(*dve.now(g, "root"))
                    v.tensor_tensor(rows[:], rows[:], over_group(gamma), ALU.mult).then_inc(*dve.did("gamma"))
                    v.wait_ge(*dve.now(g, "gamma"))
                    v.tensor_tensor(rows[:], rows[:], over_group(beta), ALU.add).then_inc(*dve.did("beta"))

        if eps:
            @block.gpsimd
            def _(p):
                stats.gpsimd(p)

        @block.tensor
        def _(e):
            pe.prime(e)
            with e.Fori(0, GROUPS) as g:
                e.wait_ge(*dve.now(g, chain[-1]))
                for j in range(GROUP):
                    e.wait_ge(*act.before(g, f"xt{j}"))
                    for k in range(2):
                        last = e.transpose(ps[:, j, k * ROWS:(k + 1) * ROWS], rows[:, j, 128 * k:128 * k + 128], b.ident[0:ROWS, 0:ROWS])
                    last.then_inc(*pe.did(f"turn{j}"))

        @block.scalar
        def _(a):
            act.prime(a)
            with a.Fori(0, GROUPS) as g:
                for j in range(GROUP):
                    a.wait_ge(*pe.now(g, f"turn{j}"))
                    a.activation(xts[:, :, bass.ds((g * GROUP + j) * ROWS, ROWS)],
                                 ps[:, j, 0:2 * ROWS].rearrange("p (k n) -> p k n", k=2), ACT.Copy).then_inc(*act.did(f"xt{j}"))
                if out:
                    a.activation(group_of(out, g), rows[:], ACT.Copy).then_inc(*act.did("out"))


def add_norm(b, y, eps, gamma_name, beta_name, store):
    nc = b.nc
    with ExitStack() as c:
        gamma = b.sb(c, "gamma", [ROWS, D])
        beta = b.sb(c, "beta", [ROWS, D])
        load(b, [(gamma[:], broadcast(b.ins[gamma_name], ROWS)), (beta[:], broadcast(b.ins[beta_name], ROWS))])
        dve = Steps(b.sem(c, "an_dve"), ["sub", "root", "gamma", "beta", "x"])
        stats = RowStats(b, c, eps)
        stored = b.sem(c, "out_stored")
        block = c.enter_context(nc.Block())

        @block.vector
        def _(v):
            dve.prime(v)
            stats.vector(v, y)
            with v.Fori(0, GROUPS) as g:
                y_g, x_g = group_of(y, g), group_of(b.x, g)
                v.tensor_tensor(y_g, y_g, stats.means(g), ALU.subtract).then_inc(*dve.did("sub"))
                v.wait_ge(*dve.now(g, "sub"))
                v.tensor_tensor(y_g, y_g, stats.roots(g), ALU.mult).then_inc(*dve.did("root"))
                v.wait_ge(*dve.now(g, "root"))
                v.tensor_tensor(y_g, y_g, over_group(gamma), ALU.mult).then_inc(*dve.did("gamma"))
                v.wait_ge(*dve.now(g, "gamma"))
                v.tensor_tensor(y_g, y_g, over_group(beta), ALU.add).then_inc(*dve.did("beta"))
                v.wait_ge(*dve.now(g, "beta"))
                v.tensor_tensor(x_g, x_g, y_g, ALU.add).then_inc(*dve.did("x"))

        @block.gpsimd
        def _(p):
            stats.gpsimd(p)

        if store:
            @block.sync
            def _(sp):
                with sp.Fori(0, GROUPS) as g:
                    sp.wait_ge(*dve.now(g, "x"))
                    sp.dma_start(b.out[bass.ds(g * (GROUP * ROWS), GROUP * ROWS), :].rearrange("(j p) d -> p j d", p=ROWS),
                                 group_of(b.x, g)).then_inc(stored, 16)
                sp.wait_ge(stored, GROUPS * 16)


def tiles_in_pairs(eng, body):
    with eng.Fori(0, TILES // 2) as r:
        for i in range(2):
            body(r * 2 + i, i)
    body(TILES - 1, 0)


def project(b, xts, weights, width, names, consume, vector_first=None, sync=None):
    nc, ps = b.nc, b.ps
    with ExitStack() as c:
        dve = Steps(b.sem(c, "pr_dve"), names, lead=2)
        pe = Steps(b.sem(c, "pr_pe"), ["proj"], lead=2)
        act = Steps(b.sem(c, "pr_act"), ["xt"], lead=2)
        xt = b.sb(c, "xt", [128, 2, 2, ROWS])
        block = c.enter_context(nc.Block())

        @block.scalar
        def _(a):
            act.prime(a)

            def body(t, i):
                a.wait_ge(*pe.back(t, 2, "proj"))
                a.activation(xt[:, i], xts[:, :, bass.ds(t * ROWS, ROWS)], ACT.Copy).then_inc(*act.did("xt"))

            tiles_in_pairs(a, body)

        @block.tensor
        def _(e):
            pe.prime(e)

            def body(t, i):
                e.wait_ge(*act.now(t, "xt"))
                e.wait_ge(*dve.back(t, 2, names[-1]))
                for k in range(2):
                    last = e.matmul(ps[0:ROWS, i, 0:width], lhsT=xt[:, i, k, :], rhs=weights[:, k, 0:width], start=k == 0, stop=k == 1)
                last.then_inc(*pe.did("proj"))

            tiles_in_pairs(e, body)

        @block.vector
        def _(v):
            dve.prime(v)
            if vector_first:
                vector_first(v)

            def body(t, i):
                v.wait_ge(*pe.now(t, "proj"))
                consume(v, t, i, ps[0:ROWS, i, 0:width], dve)

            tiles_in_pairs(v, body)

        if sync:
            @block.sync
            def _(sp):
                sync(sp, dve)


def node_tables(b, ctx, which, xts, weights, heads):
    width = D + 2 * heads
    own = b.sb(ctx, "own", [ROWS, SLOTS * heads])
    table, score = b.table[which], b.score[which]
    with ExitStack() as c:
        stored, rows_free, cleared = b.sem(c, "tab_stored"), b.sem(c, "rows_free"), b.sem(c, "tab_cleared")
        rows = b.sb(c, "rows", [ROWS, 2, width])

        def clear(v):
            v.memset(own[:, TILES * heads:], 0.0).then_inc(cleared, 1)

        def consume(v, t, i, bank, dve):
            v.tensor_scalar(own[:, bass.ds(t * heads, heads)], bank[:, D:D + heads], 1.0, None, ALU.mult).then_inc(*dve.did("own"))
            v.wait_ge(rows_free, t + 1)
            v.tensor_scalar(rows[:, i], bank, 1.0, None, ALU.mult).then_inc(*dve.did("rows"))

        def store(sp, dve):
            sp.sem_inc(rows_free, 2)

            def body(t, i):
                sp.wait_ge(*dve.now(t, "rows"))
                sp.dma_start(table[bass.ds(t * ROWS, ROWS), :], rows[:, i, 0:D]).then_inc(stored, 16)
                sp.dma_start(score[bass.ds(t * ROWS, ROWS), :], rows[:, i, D + heads:width]).then_inc(stored, 16)
                sp.wait_ge(stored, t * 32 + 32)
                sp.sem_inc(rows_free, 1)

            tiles_in_pairs(sp, body)

        project(b, xts, weights, width, ["own", "rows"], consume, clear, store)
    return own


def feed_forward(b, xts, w1, b1, w2, parts, function, names, consume, vector_first=None):
    nc, ps = b.nc, b.ps
    split = ((0, 3 * ROWS), (3 * ROWS, 5 * ROWS))
    with ExitStack() as c:
        hidden = b.sb(c, "hidden", [128, parts, GROUP * ROWS])
        dve = Steps(b.sem(c, "ff_dve"), [f"{n}{j}" for j in range(GROUP) for n in names])
        pe = Steps(b.sem(c, "ff_pe"), [f"h{m}_{n}" for m in range(parts) for n in range(2)] + [f"y{j}" for j in range(GROUP)])
        act = Steps(b.sem(c, "ff_act"), [f"h{m}_{n}" for m in range(parts) for n in range(2)])
        block = c.enter_context(nc.Block())

        @block.tensor
        def _(e):
            pe.prime(e)
            with e.Fori(0, GROUPS) as g:
                for m in range(parts):
                    for n, (lo, hi) in enumerate(split):
                        e.wait_ge(*(act.now(g, f"h{m - 2}_{n}") if m >= 2 else act.before(g, f"h{parts - 2 + m}_{n}")))
                        for k in range(2):
                            last = e.matmul(ps[:, 2 * (m % 2) + n, 0:hi - lo], lhsT=w1[:, k, 128 * m:128 * m + 128],
                                            rhs=xts[:, k, bass.ds(g * (GROUP * ROWS) + lo, hi - lo)], start=k == 0, stop=k == 1)
                        last.then_inc(*pe.did(f"h{m}_{n}"))
                e.wait_ge(*act.now(g, f"h{parts - 1}_1"))
                for j in range(GROUP):
                    e.wait_ge(*(dve.now(g, f"{names[-1]}{j - 4}") if j >= 4 else dve.before(g, f"{names[-1]}{j if j else 4}")))
                    for m in range(parts):
                        last = e.matmul(ps[0:ROWS, 4 + j % 4, 0:D], lhsT=hidden[:, m, j * ROWS:(j + 1) * ROWS],
                                        rhs=w2[:, m, :], start=m == 0, stop=m == parts - 1)
                    last.then_inc(*pe.did(f"y{j}"))

        @block.scalar
        def _(a):
            act.prime(a)
            with a.Fori(0, GROUPS) as g:
                for m in range(parts):
                    for n, (lo, hi) in enumerate(split):
                        a.wait_ge(*pe.now(g, f"h{m}_{n}"))
                        if m == 0 and n == 0:
                            a.wait_ge(*pe.before(g, f"y{GROUP - 1}"))
                        a.activation(hidden[:, m, lo:hi], ps[:, 2 * (m % 2) + n, 0:hi - lo], function,
                                     bias=b1[:, m:m + 1]).then_inc(*act.did(f"h{m}_{n}"))

        @block.vector
        def _(v):
            dve.prime(v)
            if vector_first:
                vector_first(v)
            with v.Fori(0, GROUPS) as g:
                for j in range(GROUP):
                    v.wait_ge(*pe.now(g, f"y{j}"))
                    consume(v, g, j, g * GROUP + j, ps[0:ROWS, 4 + j % 4, 0:D], dve)


SETS = CHUNKS // SET


def slots(eng, slot):
    slot(0, 0, None)
    with eng.Fori(0, SETS // 2 - 1) as r:
        slot(r * 2 + 1, 1, r * 2)
        slot(r * 2 + 2, 0, r * 2 + 1)
    slot(SETS - 1, 1, SETS - 2)
    slot(None, 0, SETS - 1)


def gather_sets(p, b, g, source, idx, got, gathered, pool, staged, used):
    pool.prime(p)
    with p.Fori(0, SETS // 2) as r:
        for i in range(2):
            p.wait_ge(*used(r * 2 + i))
            p.tensor_copy(idx[:, i], g["nbr"][:, bass.ds(r * (2 * SET) + i * SET, SET)]).then_inc(*pool.did("idx"))
            p.wait_ge(*pool.now(r * 2 + i, "idx"))
            p.sem_inc(staged, 1)
            for j in range(SET):
                p.indirect_dma_start(got[:, i, j, :], None, source[:, :],
                                     bass.IndirectOffsetOnAxis(ap=idx[:, i, j:j + 1], axis=0)).then_inc(gathered[i], 16)


def one_hot(v, b, g, sel, i, k0, m):
    return v.tensor_tensor(sel[:, i, 4 * m:4 * m + 4, :], b.row_no[:, 0:ROWS].unsqueeze(1).to_broadcast([128, 4, ROWS]),
                           g["lane"][:, bass.ds(k0 + 4 * m, 4)].unsqueeze(2).to_broadcast([128, 4, ROWS]), ALU.is_equal)


def edge_scores(b, g, score, own, heads, e_all, top):
    nc, ps = b.nc, b.ps
    q = SET * heads
    pairs = SET // 2
    with ExitStack() as c:
        dve_a = Steps(b.sem(c, "sc_dve_a"), ["s0", "s1", "sum", "leak", "e", "hi", "r1", "mid", "r2", "lo"], lead=2)
        dve_b = Steps(b.sem(c, "sc_dve_b"), [n for p in range(pairs) for n in (f"red{p}", f"top{2 * p}", f"top{2 * p + 1}")], lead=2)
        pe_a = Steps(b.sem(c, "sc_pe_a"), ["st", "own", "et"], lead=2)
        pe_b = Steps(b.sem(c, "sc_pe_b"), [f"mx{p}" for p in range(pairs)], lead=2)
        act = Steps(b.sem(c, "sc_act"), ["st", "et"], lead=2)
        pool = Steps(b.sem(c, "sc_pool"), ["idx"])
        staged, const, consv = b.sem(c, "staged"), b.sem(c, "sc_const"), b.sem(c, "sc_consv")
        gathered = [b.sem_of_gathers(f"gathered{i}") for i in range(2)]
        idx = b.sb(c, "idx", [128, 2, SET], I32)
        got = b.sb(c, "got", [128, 2, SET, heads])
        sel = b.sb(c, "sel", [128, 2, SET, ROWS], BF16)
        selt = b.sb(c, "selt", [ROWS, SET, 128])
        z = b.sb(c, "z", [128, q])
        parts = b.sb(c, "parts", [128, 3, q], BF16)
        rest = b.sb(c, "rest", [128, q])
        partst = b.sb(c, "partst", [3 * q, 128], BF16)
        pick = b.sb(c, "pick", [3 * q, q, ROWS], BF16)
        bigi = b.sb(c, "bigi", [128, heads, 128], BF16)
        minus = b.sb(c, "minus", [1, heads * 128], BF16)
        red = b.sb(c, "red", [ROWS, 2, 2, heads])
        turned = ps[:, 0, :].bitcast(BF16)
        block = c.enter_context(nc.Block())

        @block.gpsimd
        def _(p):
            p.memset(pick[:], 0.0).then_inc(const, 1)
            for n in range(3):
                p.wait_ge(const, n + 1)
                p.affine_select(out=pick[:], in_=pick[:], compare_op=ALU.not_equal, fill=1.0, base=-q * n,
                                pattern=[[-1, q], [0, ROWS]], channel_multiplier=1).then_inc(const, 1)
            gather_sets(p, b, g, score, idx, got, gathered, pool, staged, lambda s: dve_a.back(s, 2, "sum"))

        @block.vector
        def _(v):
            dve_a.prime(v)
            dve_b.prime(v)
            v.memset(top[:], -BIG).then_inc(consv, 1)
            v.memset(minus[:], -BIG).then_inc(consv, 1)
            for h in range(heads):
                v.tensor_scalar(bigi[:, h, :], b.ident[:], BIG, None, ALU.mult).then_inc(consv, 1)
            v.wait_ge(consv, 2 + heads)
            tiles = [v.alloc_register(f"score_tile_v{b.count}_{j}") for j in range(SET)]
            p3 = parts[:].rearrange("p n (j h) -> p n j h", h=heads)
            r3 = rest[:].rearrange("p (j h) -> p j h", h=heads)

            def slot(s, i, u):
                if s is not None:
                    v.wait_ge(*pe_b.back(s, 2, f"mx{pairs - 1}"))
                    for m in range(2):
                        one_hot(v, b, g, sel, i, s * SET, m).then_inc(*dve_a.did(f"s{m}"))
                    e_k = e_all[:, bass.ds(s * SET, SET), 0:heads]
                if u is not None:
                    v.reg_load(tiles, g["tile"][0:1, bass.ds(u * SET, SET)])

                def largest(p):
                    if u is not None:
                        v.wait_ge(*pe_b.now(u, f"mx{p}"))
                        v.wait_ge(*(dve_b.now(u, f"top{2 * p - 3}") if p >= 2 else dve_b.back(u, 1, f"top{SET - 3 + 2 * p}")))
                        v.tensor_reduce(red[:, p % 2], ps[0:ROWS, 3 + 2 * (p % 2):5 + 2 * (p % 2), 0:heads * 128]
                                        .rearrange("p j (h e) -> p j h e", h=heads), AX.X, ALU.max).then_inc(*dve_b.did(f"red{p}"))

                def update(j):
                    if u is not None:
                        tile = v.snap(tiles[j], min_val=0, max_val=TILES)
                        top_k = top[:, bass.ds(tile * heads, heads)]
                        v.wait_ge(*(dve_b.now(u, f"top{j - 1}") if j % 2 else dve_b.now(u, f"red{j // 2}")))
                        v.tensor_tensor(top_k, top_k, red[:, j // 2 % 2, j % 2], ALU.max).then_inc(*dve_b.did(f"top{j}"))

                largest(0)
                if s is not None:
                    v.wait_ge(*pe_a.now(s, "own"))
                    v.wait_ge(gathered[i], s * (SET * 8) + (SET * 16 - i * SET * 8))
                    v.tensor_tensor(z[:], ps[:, 1, 0:q], got[:, i].rearrange("p j h -> p (j h)"), ALU.add).then_inc(*dve_a.did("sum"))
                update(0)
                if s is not None:
                    v.wait_ge(*dve_a.now(s, "sum"))
                    v.scalar_tensor_tensor(out=rest[:], in0=z[:], scalar=0.2, in1=z[:], op0=ALU.mult, op1=ALU.max).then_inc(*dve_a.did("leak"))
                update(1)
                if s is not None:
                    v.wait_ge(*dve_a.now(s, "leak"))
                    if g["w"] is not None:
                        v.tensor_tensor(e_k, r3, g["w"][:, bass.ds(s * SET, SET)].unsqueeze(2).to_broadcast([128, SET, heads]),
                                        ALU.mult).then_inc(*dve_a.did("e"))
                    else:
                        v.tensor_scalar(e_k, r3, 1.0, None, ALU.mult).then_inc(*dve_a.did("e"))
                largest(1)
                if s is not None:
                    v.wait_ge(*dve_a.now(s, "e"))
                    v.wait_ge(*pe_a.back(s, 1, "et"))
                    v.tensor_scalar(p3[:, 0], e_k, 1.0, None, ALU.mult).then_inc(*dve_a.did("hi"))
                update(2)
                if s is not None:
                    v.wait_ge(*dve_a.now(s, "hi"))
                    v.tensor_tensor(r3, e_k, p3[:, 0], ALU.subtract).then_inc(*dve_a.did("r1"))
                update(3)
                if s is not None:
                    v.wait_ge(*dve_a.now(s, "r1"))
                    v.tensor_copy(parts[:, 1], rest[:]).then_inc(*dve_a.did("mid"))
                largest(2)
                if s is not None:
                    v.wait_ge(*dve_a.now(s, "mid"))
                    v.tensor_tensor(rest[:], rest[:], parts[:, 1], ALU.subtract).then_inc(*dve_a.did("r2"))
                update(4)
                if s is not None:
                    v.wait_ge(*dve_a.now(s, "r2"))
                    v.tensor_copy(parts[:, 2], rest[:]).then_inc(*dve_a.did("lo"))
                update(5)
                largest(3)
                update(6)
                update(7)
                if s is not None:
                    v.wait_ge(*dve_a.now(s, "lo"))

            slots(v, slot)

        @block.tensor
        def _(e):
            pe_a.prime(e)
            pe_b.prime(e)
            e.wait_ge(const, 4)
            e.wait_ge(consv, 2 + heads)
            tiles = [e.alloc_register(f"score_tile_t{b.count}_{j}") for j in range(SET)]

            def slot(s, i, u):
                def masked(p):
                    if u is None:
                        return
                    e.wait_ge(*(dve_b.now(u, f"red{p - 2}") if p >= 2 else dve_b.back(u, 1, f"red{pairs - 2 + p}")))
                    for j in (2 * p, 2 * p + 1):
                        bank = ps[0:ROWS, 3 + j % 4, 0:heads * 128]
                        e.matmul(bank, lhsT=b.onesb[0:1, 0:ROWS], rhs=minus[:], start=True, stop=False)
                        e.matmul(bank, lhsT=sel[:, 1 - i, j, :], rhs=bigi[:].rearrange("p h e -> p (h e)"), start=False, stop=False)
                        for h in range(heads):
                            last = e.matmul(bank[:, 128 * h:128 * h + 128], lhsT=pick[:, j * heads + h, :], rhs=partst[:],
                                            start=False, stop=h == heads - 1)
                    last.then_inc(*pe_b.did(f"mx{p}"))

                if u is not None:
                    e.wait_ge(*act.now(u, "et"))
                masked(0)
                if s is not None:
                    e.wait_ge(*dve_a.now(s, "s1"))
                    e.wait_ge(*act.back(s, 1, "st"))
                    for j in range(SET):
                        last = e.transpose(turned[0:ROWS, 128 * j:128 * j + 128], sel[:, i, j, :], b.identb[:])
                    last.then_inc(*pe_a.did("st"))
                    e.reg_load(tiles, g["tile"][0:1, bass.ds(s * SET, SET)])
                masked(1)
                if s is not None:
                    e.wait_ge(*act.now(s, "st"))
                    e.wait_ge(*dve_a.back(s, 1, "sum"))
                    for j in range(SET):
                        tile = e.snap(tiles[j], min_val=0, max_val=TILES)
                        last = e.matmul(ps[:, 1, j * heads:(j + 1) * heads], lhsT=selt[:, j, :],
                                        rhs=own[:, bass.ds(tile * heads, heads)], start=True, stop=True)
                    last.then_inc(*pe_a.did("own"))
                masked(2)
                masked(3)
                if s is not None:
                    e.wait_ge(*dve_a.now(s, "lo"))
                    e.wait_ge(*act.back(s, 1, "et"))
                    e.transpose(ps[0:3 * q, 2, :].bitcast(BF16)[:, 0:128], parts[:].rearrange("p n k -> p (n k)"),
                                b.identb[:]).then_inc(*pe_a.did("et"))

            slots(e, slot)

        @block.scalar
        def _(a):
            act.prime(a)

            def slot(s, i, u):
                if s is None:
                    return
                a.wait_ge(*pe_a.now(s, "st"))
                a.wait_ge(*pe_a.back(s, 1, "own"))
                a.activation(selt[:].rearrange("p j e -> p (j e)"), turned[0:ROWS, :], ACT.Copy).then_inc(*act.did("st"))
                a.wait_ge(*pe_a.now(s, "et"))
                a.wait_ge(*pe_b.back(s, 1, f"mx{pairs - 1}"))
                a.activation(partst[:], ps[0:3 * q, 2, :].bitcast(BF16)[:, 0:128], ACT.Copy).then_inc(*act.did("et"))

            slots(a, slot)


def edge_sums(b, g, table, heads, e_all, top, acc):
    nc, ps = b.nc, b.ps
    q = SET * heads
    width = D + heads
    with ExitStack() as c:
        dve_a = Steps(b.sem(c, "su_dve_a"), ["s0", "s1", "diff", "low", "msg0", "msg1"], lead=2)
        dve_b = Steps(b.sem(c, "su_dve_b"), [f"acc{j}" for j in range(SET)], lead=2)
        pe_a = Steps(b.sem(c, "su_pe_a"), ["st0", "st1", "top"], lead=2)
        pe_b = Steps(b.sem(c, "su_pe_b"), [f"sum{j}" for j in range(SET)], lead=2)
        act = Steps(b.sem(c, "su_act"), ["st0", "st1", "ex"], lead=2)
        pool = Steps(b.sem(c, "su_pool"), ["idx"])
        staged, cleared = b.sem(c, "staged"), b.sem(c, "su_cleared")
        gathered = [b.sem_of_gathers(f"gathered{i}") for i in range(2)]
        idx = b.sb(c, "idx", [128, 2, SET], I32)
        got = b.sb(c, "got", [128, 2, SET, D])
        sel = b.sb(c, "sel", [128, 2, SET, ROWS])
        selt = b.sb(c, "selt", [ROWS, SET, 128])
        diff = b.sb(c, "diff", [128, SET, heads])
        msg = b.sb(c, "msg", [128, 2, SET, width])
        block = c.enter_context(nc.Block())

        @block.gpsimd
        def _(p):
            gather_sets(p, b, g, table, idx, got, gathered, pool, staged, lambda s: dve_a.back(s, 2, "msg1"))

        @block.vector
        def _(v):
            dve_a.prime(v)
            dve_b.prime(v)
            v.memset(acc[:], 0.0).then_inc(cleared, 1)
            v.wait_ge(cleared, 1)
            tiles = [v.alloc_register(f"sum_tile_v{b.count}_{j}") for j in range(SET)]

            def slot(s, i, u):
                def add(*chunks):
                    if u is None:
                        return
                    for j in chunks:
                        tile = v.snap(tiles[j], min_val=0, max_val=TILES)
                        v.wait_ge(*pe_b.now(u, f"sum{j}"))
                        v.wait_ge(*(dve_b.now(u, f"acc{j - 1}") if j else dve_b.back(u, 1, f"acc{SET - 1}")))
                        acc_k = acc[:, bass.ds(tile * width, width)]
                        v.tensor_tensor(acc_k, acc_k, ps[0:ROWS, 3 + j % 4, 0:width], ALU.add).then_inc(*dve_b.did(f"acc{j}"))

                if s is not None:
                    v.wait_ge(*pe_b.back(s, 2, f"sum{SET - 1}"))
                    for m in range(2):
                        one_hot(v, b, g, sel, i, s * SET, m).then_inc(*dve_a.did(f"s{m}"))
                if u is not None:
                    v.reg_load(tiles, g["tile"][0:1, bass.ds(u * SET, SET)])
                add(0, 1, 2, 3)
                if s is not None:
                    v.wait_ge(*pe_a.now(s, "top"))
                    v.wait_ge(*act.back(s, 1, "ex"))
                    v.tensor_tensor(diff[:], e_all[:, bass.ds(s * SET, SET), 0:heads],
                                    ps[:, 2, 0:q].rearrange("p (j h) -> p j h", h=heads), ALU.subtract).then_inc(*dve_a.did("diff"))
                add(4)
                if s is not None:
                    v.wait_ge(*dve_a.now(s, "diff"))
                    v.tensor_scalar(diff[:], diff[:], 0.0, None, ALU.min).then_inc(*dve_a.did("low"))
                add(5, 6)

                def weigh(m):
                    part = slice(4 * m, 4 * m + 4)
                    v.tensor_tensor(msg[:, i, part, 0:D].rearrange("p j (h f) -> p j h f", h=heads),
                                    got[:, i, part, :].rearrange("p j (h f) -> p j h f", h=heads),
                                    msg[:, i, part, D:width].unsqueeze(3).to_broadcast([128, 4, heads, D // heads]),
                                    ALU.mult).then_inc(*dve_a.did(f"msg{m}"))

                if s is not None:
                    v.wait_ge(*act.now(s, "ex"))
                    v.wait_ge(gathered[i], s * (SET * 8) + (SET * 16 - i * SET * 8))
                    weigh(0)
                add(7)
                if s is not None:
                    weigh(1)

            slots(v, slot)

        @block.tensor
        def _(e):
            pe_a.prime(e)
            pe_b.prime(e)
            tiles = [e.alloc_register(f"sum_tile_t{b.count}_{j}") for j in range(SET)]

            def slot(s, i, u):
                def total(*chunks):
                    if u is None:
                        return
                    for j in chunks:
                        e.wait_ge(*dve_a.now(u, f"msg{j // 4}"))
                        e.wait_ge(*(dve_b.now(u, f"acc{j - 4}") if j >= 4 else dve_b.back(u, 1, f"acc{SET - 4 + j}")))
                        e.matmul(ps[0:ROWS, 3 + j % 4, 0:width], lhsT=sel[:, 1 - i, j, :], rhs=msg[:, 1 - i, j, :],
                                 start=True, stop=True).then_inc(*pe_b.did(f"sum{j}"))

                total(0, 1)
                if s is not None:
                    for m in range(2):
                        e.wait_ge(*dve_a.now(s, f"s{m}"))
                        e.wait_ge(*act.back(s, 1, f"st{m}"))
                        for j in range(4):
                            last = e.transpose(ps[0:ROWS, m, 128 * j:128 * j + 128], sel[:, i, 4 * m + j, :], b.ident[:])
                        last.then_inc(*pe_a.did(f"st{m}"))
                    e.reg_load(tiles, g["tile"][0:1, bass.ds(s * SET, SET)])
                total(2, 3)
                if s is not None:
                    e.wait_ge(*act.now(s, "st1"))
                    e.wait_ge(*dve_a.back(s, 1, "diff"))
                    for j in range(SET):
                        tile = e.snap(tiles[j], min_val=0, max_val=TILES)
                        last = e.matmul(ps[:, 2, j * heads:(j + 1) * heads], lhsT=selt[:, j, :],
                                        rhs=top[:, bass.ds(tile * heads, heads)], start=True, stop=True)
                    last.then_inc(*pe_a.did("top"))
                total(4, 5, 6, 7)

            slots(e, slot)

        @block.scalar
        def _(a):
            act.prime(a)

            def slot(s, i, u):
                if s is None:
                    return
                for m in range(2):
                    a.wait_ge(*pe_a.now(s, f"st{m}"))
                    if m == 0:
                        a.wait_ge(*pe_a.back(s, 1, "top"))
                    a.activation(selt[:, 4 * m:4 * m + 4, :].rearrange("p j e -> p (j e)"), ps[0:ROWS, m, :],
                                 ACT.Copy).then_inc(*act.did(f"st{m}"))
                a.wait_ge(*dve_a.now(s, "low"))
                a.wait_ge(*pe_b.back(s, 2, f"sum{SET - 1}"))
                a.activation(msg[:, i, :, D:width], diff[:], ACT.Exp).then_inc(*act.did("ex"))

            slots(a, slot)


def edge_mean(b, acc, heads, bias, into, add):
    nc = b.nc
    width = D + heads
    with ExitStack() as c:
        dve = Steps(b.sem(c, "mean_dve"), ["den", "inv", "mean", "bias", "out"])
        den = b.sb(c, "den", [ROWS, heads])
        out = b.sb(c, "mean", [ROWS, D])
        block = c.enter_context(nc.Block())

        @block.vector
        def _(v):
            dve.prime(v)
            with v.Fori(0, TILES) as t:
                v.tensor_scalar(den[:], acc[:, bass.ds(t * width + D, heads)], 1e-30, None, ALU.max).then_inc(*dve.did("den"))
                v.wait_ge(*dve.now(t, "den"))
                v.reciprocal(den[:], den[:]).then_inc(*dve.did("inv"))
                v.wait_ge(*dve.now(t, "inv"))
                v.tensor_tensor(out[:].rearrange("p (h f) -> p h f", h=heads),
                                acc[:, bass.ds(t * width, D)].rearrange("p (h f) -> p h f", h=heads),
                                den[:].unsqueeze(2).to_broadcast([ROWS, heads, D // heads]), ALU.mult).then_inc(*dve.did("mean"))
                v.wait_ge(*dve.now(t, "mean"))
                v.tensor_tensor(out[:], out[:], bias, ALU.add).then_inc(*dve.did("bias"))
                v.wait_ge(*dve.now(t, "bias"))
                into_t = into[:, bass.ds(t, 1), :].rearrange("p a d -> p (a d)")
                if add:
                    v.scalar_tensor_tensor(out=into_t, in0=out[:], scalar=0.0, in1=into_t, op0=ALU.max, op1=ALU.add).then_inc(*dve.did("out"))
                else:
                    v.tensor_scalar(into_t, out[:], 0.0, None, ALU.max).then_inc(*dve.did("out"))
                v.wait_ge(*dve.now(t, "out"))


def broadcast(ap, rows=128):
    return bass.AP(tensor=ap.tensor, offset=ap.offset, ap=[[0, rows], [1, int(np.prod(ap.shape))]])


def graph_weights(b, ctx, w_name, own_name, nbr_name, heads):
    nc = b.nc
    weights = b.sb(ctx, "gw", [128, 2, D + 2 * heads])
    with ExitStack() as c:
        a = b.sb(c, "a", [128, 2, D])
        prod = b.sb(c, "prod", [128, D])
        loaded, done = b.sem(c, "gw_loaded"), b.sem(c, "gw_done")
        block = c.enter_context(nc.Block())

        @block.sync
        def _(sp):
            sp.dma_start(weights[:, :, 0:D], b.ins[w_name].rearrange("(k p) n -> p k n", p=128)).then_inc(loaded, 16)
            for i, name in enumerate((own_name, nbr_name)):
                sp.dma_start(a[:, i, :], broadcast(b.ins[name])).then_inc(loaded, 16)

        @block.vector
        def _(v):
            v.wait_ge(loaded, 48)
            n = 0
            for k in range(2):
                for i in range(2):
                    v.tensor_tensor(prod[:], weights[:, k, 0:D], a[:, i, :], ALU.mult).then_inc(done, 1)
                    v.wait_ge(done, n + 1)
                    v.tensor_reduce(weights[:, k, D + i * heads:D + (i + 1) * heads],
                                    prod[:].rearrange("p (h f) -> p h f", h=heads), AX.X, ALU.add).then_inc(done, 1)
                    v.wait_ge(done, n + 2)
                    n += 2
    return weights


def load(b, pairs):
    with ExitStack() as c:
        loaded = b.sem(c, "loaded")
        block = c.enter_context(b.nc.Block())

        @block.sync
        def _(sp):
            for dst, src in pairs:
                sp.dma_start(dst, src).then_inc(loaded, 16)
            sp.wait_ge(loaded, 16 * len(pairs))


def tile_of(source, t):
    return source[:, bass.ds(t, 1), :].rearrange("p a d -> p (a d)")


def phi_weights(b, ctx, side):
    nc, ps = b.nc, b.ps
    w = b.sb(ctx, "w", [128, 2, H * KD])
    wp = b.sb(ctx, "wp", [128, 2, H * KD])
    bias = b.sb(ctx, "bias", [3, 2, H * KD], BF16)
    with ExitStack() as outer:
        row = b.sb(outer, "row", [1, 2, H * KD])
        project_weights(b, side, w, wp, row)
        for which in range(2):
            split_bias(b, row[:, which, :], bias[:, which, :])
    return w, wp, bias


def project_weights(b, side, w, wp, row):
    nc, ps = b.nc, b.ps
    with ExitStack() as c:
        wt = b.sb(c, "wt", [128, 2 * H, D])
        projt = b.sb(c, "projt", [128, 2, KD])
        column = b.sb(c, "column", [128, 2 * H])
        load(b, [(w[:], b.ins[f"L0_mix_W{side}"].rearrange("(k p) n -> p k n", p=128)),
                 (wt[:], b.ins[f"W{side}_T"].rearrange("(k p) n -> p k n", p=128)),
                 (projt[:], b.ins["proj_T"].rearrange("(k p) n -> p k n", p=128)),
                 (column[:], b.ins[f"b{side}_columns"]),
                 (row[:, 0, :], b.ins[f"L0_mix_b{side}"].unsqueeze(0))])
        pe_did, act_did = b.sem(c, "phw_pe"), b.sem(c, "phw_act")
        block = c.enter_context(nc.Block())

        @block.tensor
        def _(e):
            for h in range(H):
                for m in range(3):
                    n = 3 * h + m
                    if n >= 4:
                        e.wait_ge(act_did, n - 3)
                    for k in range(2):
                        if m < 2:
                            last = e.matmul(ps[:, n % 4, 0:KD], lhsT=wt[:, 2 * h + k, 128 * m:128 * m + 128],
                                            rhs=projt[:, k, :], start=k == 0, stop=k == 1)
                        else:
                            last = e.matmul(ps[0:1, n % 4, 0:KD], lhsT=column[:, 2 * h + k:2 * h + k + 1],
                                            rhs=projt[:, k, :], start=k == 0, stop=k == 1)
                    last.then_inc(pe_did, 1)

        @block.scalar
        def _(a):
            for h in range(H):
                for m in range(3):
                    n = 3 * h + m
                    a.wait_ge(pe_did, n + 1)
                    if m < 2:
                        a.activation(wp[:, m, h * KD:(h + 1) * KD], ps[:, n % 4, 0:KD], ACT.Copy).then_inc(act_did, 1)
                    else:
                        a.activation(row[:, 1, h * KD:(h + 1) * KD], ps[0:1, n % 4, 0:KD], ACT.Copy).then_inc(act_did, 1)


def split_bias(b, row, bias):
    with ExitStack() as c:
        parts = b.sb(c, "parts", [1, 3, H * KD], BF16)
        dve_did, spread = b.sem(c, "split_dve"), b.sem(c, "spread")
        block = c.enter_context(b.nc.Block())

        @block.vector
        def _(v):
            v.tensor_copy(parts[:, 0], row).then_inc(dve_did, 1)
            v.wait_ge(dve_did, 1)
            v.tensor_tensor(row, row, parts[:, 0], ALU.subtract).then_inc(dve_did, 1)
            v.wait_ge(dve_did, 2)
            v.tensor_copy(parts[:, 1], row).then_inc(dve_did, 1)
            v.wait_ge(dve_did, 3)
            v.tensor_tensor(row, row, parts[:, 1], ALU.subtract).then_inc(dve_did, 1)
            v.wait_ge(dve_did, 4)
            v.tensor_copy(parts[:, 2], row).then_inc(dve_did, 1)

        @block.sync
        def _(sp):
            sp.wait_ge(dve_did, 5)
            for i in range(3):
                sp.dma_start(bias[i:i + 1], parts[:, i]).then_inc(spread, 16)
            sp.wait_ge(spread, 48)


def phi_projections(e, b, w, xt, bank, bias, which, col, n):
    out = bank[:, 0:n]
    e.matmul(out, lhsT=b.onesb[0:3, 0:ROWS], rhs=bias[:, which, col:col + n], start=True, stop=False)
    e.matmul(out, lhsT=xt[:, 0, :], rhs=w[:, 0, col:col + n], start=False, stop=False)
    return e.matmul(out, lhsT=xt[:, 1, :], rhs=w[:, 1, col:col + n], start=False, stop=True)


def head_steps(lag):
    order = []
    for h in range(H + lag):
        if h < H:
            order += ([("pair", h // 2)] if h % 2 == 0 else []) + [("u", h)]
        if h >= lag:
            order += [("g", h - lag)]
    return order


def mix0_keys(b, xn, xts, gram, w, wp, bias, plan):
    nc, ps = b.nc, b.ps
    order = head_steps(2)
    with ExitStack() as c:
        dve_order = []
        for h in range(H + 1):
            if h < H:
                dve_order += ([("shift", h // 2)] if h % 2 == 0 else []) + [("phi", h)]
            if h >= 1:
                dve_order += [("add", h - 1)]
        dve = Steps(b.sem(c, "key_dve"), [n for kind, h in dve_order for n in
                    ([f"add{h}_0", f"add{h}_1"] if kind == "add" else [f"{kind}{h}"])])
        pe = Steps(b.sem(c, "key_pe"), [n for kind, h in order for n in
                   ([f"g{h}_0", f"g{h}_1"] if kind == "g" else [f"{kind}{h}"])])
        act = Steps(b.sem(c, "key_act"), ["xt"] + [f"{n}{2 * g + i}" for g in range(H // 2) for n in ("sq", "exp") for i in range(2)])
        cleared = b.sem(c, "key_cleared")
        xt = b.sb(c, "xt", [128, 2, ROWS])
        junk = b.sb(c, "junk", [ROWS, 2, KD])
        sq = b.sb(c, "sq", [ROWS, H])
        shift = b.sb(c, "shift", [ROWS, H])
        phi = b.sb(c, "phi", [ROWS, 2, KD])
        phi1 = b.sb(c, "phi1", [ROWS, 2, KD])
        scatter = Scatter(b, c, plan)
        block = c.enter_context(nc.Block())

        @block.gpsimd
        def _(pool):
            scatter.gpsimd(pool)

        @block.sync
        def _(sp):
            scatter.sync(sp)

        @block.vector
        def _(v):
            dve.prime(v)
            v.memset(gram[:], 0.0).then_inc(cleared, 1)
            v.memset(xn[:, :, D:D + 1], 1.0).then_inc(cleared, 1)
            v.wait_ge(cleared, 2)
            with v.Fori(0, TILES) as t:
                for kind, h in dve_order:
                    if kind == "shift":
                        v.wait_ge(*act.now(t, f"sq{2 * h + 1}"))
                        v.wait_ge(*act.before(t, f"exp{2 * h + 1}"))
                        v.tensor_scalar(shift[:, 2 * h:2 * h + 2], sq[:, 2 * h:2 * h + 2], -0.5 * KSCALE * KSCALE, None,
                                        ALU.mult).then_inc(*dve.did(f"shift{h}"))
                    elif kind == "phi":
                        v.wait_ge(*act.now(t, f"exp{h}"))
                        v.wait_ge(*(pe.now(t, f"g{h - 2}_1") if h >= 2 else pe.before(t, f"g{H - 2 + h}_1")))
                        v.tensor_scalar(phi1[:, h % 2, :], phi[:, h % 2, :], KD ** -0.5, 1e-6, ALU.mult,
                                        ALU.add).then_inc(*dve.did(f"phi{h}"))
                    else:
                        for m in range(2):
                            v.wait_ge(*pe.now(t, f"g{h}_{m}"))
                            v.wait_ge(*dve.before(t, f"add{h}_{m}"))
                            v.tensor_tensor(gram[:, 2 * h + m, :], gram[:, 2 * h + m, :], ps[:, 6 + m, 0:D + 1],
                                            ALU.add).then_inc(*dve.did(f"add{h}_{m}"))

        @block.tensor
        def _(e):
            pe.prime(e)
            with e.Fori(0, TILES) as t:
                e.wait_ge(*act.now(t, "xt"))
                for kind, h in order:
                    if kind == "pair":
                        g = 2 * h + 1
                        e.wait_ge(*(act.now(t, f"sq{g - 4}") if g >= 4 else act.before(t, f"sq{H - 4 + g}")))
                        phi_projections(e, b, w, xt, ps[0:ROWS, 2 + h % 2, :], bias, 0, h * 512, 512).then_inc(*pe.did(f"pair{h}"))
                    elif kind == "u":
                        e.wait_ge(*(act.now(t, f"exp{h - 2}") if h >= 2 else act.before(t, f"exp{H - 2 + h}")))
                        phi_projections(e, b, wp, xt, ps[0:ROWS, 4 + h % 2, :], bias, 1, h * KD, KD).then_inc(*pe.did(f"u{h}"))
                    else:
                        e.wait_ge(*dve.now(t, f"phi{h}"))
                        for m in range(2):
                            e.wait_ge(*(dve.now(t, f"add{h - 1}_{m}") if h else dve.before(t, f"add{H - 1}_{m}")))
                            e.matmul(ps[:, 6 + m, 0:D + 1], lhsT=phi1[:, h % 2, 128 * m:128 * m + 128], rhs=tile_of(xn, t),
                                     start=True, stop=True).then_inc(*pe.did(f"g{h}_{m}"))

        @block.scalar
        def _(a):
            act.prime(a)
            with a.Fori(0, TILES) as t:
                a.wait_ge(*pe.before(t, f"u{H - 1}"))
                a.activation(xt[:], xts[:, :, bass.ds(t * ROWS, ROWS)], ACT.Copy).then_inc(*act.did("xt"))
                for g in range(H // 2):
                    a.wait_ge(*pe.now(t, f"pair{g}"))
                    a.wait_ge(*dve.before(t, f"shift{g}"))
                    for h in (2 * g, 2 * g + 1):
                        a.wait_ge(*(act.now(t, f"sq{h - 2}") if h >= 2 else act.before(t, f"sq{H - 2 + h}")))
                        a.activation(junk[:, h % 2, :], ps[0:ROWS, 2 + g % 2, (h % 2) * KD:(h % 2 + 1) * KD], ACT.Square,
                                     accum_out=sq[:, h:h + 1]).then_inc(*act.did(f"sq{h}"))
                    for h in (2 * g, 2 * g + 1):
                        a.wait_ge(*dve.now(t, f"shift{g}"))
                        a.wait_ge(*pe.now(t, f"u{h}"))
                        a.wait_ge(*(dve.now(t, f"phi{h - 2}") if h >= 2 else dve.before(t, f"phi{H - 2 + h}")))
                        a.activation(phi[:, h % 2, :], ps[0:ROWS, 4 + h % 2, 0:KD], ACT.Exp, bias=shift[:, h:h + 1],
                                     scale=KSCALE).then_inc(*act.did(f"exp{h}"))


def mix0_values(b, kvo, gram):
    nc, ps = b.nc, b.ps
    with ExitStack() as c:
        wv = b.sb(c, "wv", [128, 2, H * KD])
        bv = b.sb(c, "bv", [1, H * KD])
        wo = b.sb(c, "wo", [128, 2 * H, D])
        gt = b.sb(c, "gt", [128, 2, 256])
        sums = b.sb(c, "sums", [1, 256])
        kvt = b.sb(c, "kvt", [128, 2, 256])
        load(b, [(wv[:], b.ins["L0_mix_Wv"].rearrange("(k p) n -> p k n", p=128)),
                 (bv[:], b.ins["L0_mix_bv"].unsqueeze(0)),
                 (wo[:], b.ins["L0_mix_Wo"].rearrange("(k p) n -> p k n", p=128))])
        pe_did, act_did, dve_did = b.sem(c, "val_pe"), b.sem(c, "val_act"), b.sem(c, "val_dve")
        block = c.enter_context(nc.Block())

        @block.tensor
        def _(e):
            for h in range(H):
                if h:
                    e.wait_ge(act_did, 7 * h)
                for k in range(2):
                    for m in range(2):
                        last = e.transpose(ps[:, k, 128 * m:128 * m + 128], gram[:, 2 * h + m, 128 * k:128 * k + 128], b.ident[:])
                    last.then_inc(pe_did, 1)
                for m in range(2):
                    last = e.transpose(ps[0:1, 2, 128 * m:128 * m + 128], gram[:, 2 * h + m, D:D + 1], b.ident[:])
                last.then_inc(pe_did, 1)
                e.wait_ge(act_did, 7 * h + 3)
                for n in range(2):
                    col = h * KD + 128 * n
                    e.matmul(ps[:, 3 + n, 0:256], lhsT=bv[:, col:col + 128], rhs=sums[:], start=True, stop=False)
                    for k in range(2):
                        last = e.matmul(ps[:, 3 + n, 0:256], lhsT=wv[:, k, col:col + 128], rhs=gt[:, k, :], start=False, stop=k == 1)
                    last.then_inc(pe_did, 1)
                e.wait_ge(act_did, 7 * h + 5)
                for m in range(2):
                    for k in range(2):
                        last = e.matmul(ps[:, 5 + m, 0:D], lhsT=kvt[:, k, 128 * m:128 * m + 128], rhs=wo[:, 2 * h + k, :],
                                        start=k == 0, stop=k == 1)
                    last.then_inc(pe_did, 1)

        @block.scalar
        def _(a):
            for h in range(H):
                for k in range(2):
                    a.wait_ge(pe_did, 7 * h + k + 1)
                    a.activation(gt[:, k, :], ps[:, k, 0:256], ACT.Copy).then_inc(act_did, 1)
                a.wait_ge(pe_did, 7 * h + 3)
                a.activation(sums[:], ps[0:1, 2, 0:256], ACT.Copy).then_inc(act_did, 1)
                for n in range(2):
                    a.wait_ge(pe_did, 7 * h + 4 + n)
                    a.activation(kvt[:, n, :], ps[:, 3 + n, 0:256], ACT.Copy).then_inc(act_did, 1)
                for m in range(2):
                    a.wait_ge(pe_did, 7 * h + 6 + m)
                    a.activation(kvo[:, 2 * h + m, 0:D], ps[:, 5 + m, 0:D], ACT.Copy).then_inc(act_did, 1)

        @block.vector
        def _(v):
            v.tensor_copy(kvo[:, :, D:D + 1], gram[:, :, D:D + 1]).then_inc(dve_did, 1)


def mix0_queries(b, y, xts, w, wp, bias, kvo, plan):
    nc, ps = b.nc, b.ps
    order = []
    for h in range(H + 3):
        if h < H:
            order += ([("pair", h // 2)] if h % 2 == 0 else []) + [("u", h)]
        order += [("pt", h - 2)] if 2 <= h < H + 2 else []
        order += [("g", h - 3)] if h >= 3 else []
    with ExitStack() as c:
        bo = b.sb(c, "bo", [ROWS, D])
        load(b, [(bo[:], broadcast(b.ins["L0_mix_bo"], ROWS))])
        dve_order = []
        for h in range(H + 3):
            if h < H:
                dve_order += ([("shift", h // 2)] if h % 2 == 0 else []) + [("phi", h)]
            if h >= 3:
                dve_order += [("add", h - 3)]
        dve = Steps(b.sem(c, "q_dve"), [n for kind, h in dve_order for n in
                    ([f"inv{h}", f"add{h}"] if kind == "add" else [f"{kind}{h}"])])
        pe = Steps(b.sem(c, "q_pe"), [f"{kind}{h}" for kind, h in order])
        act_order = [("sq", 0), ("sq", 1), ("exp", 0), ("exp", 1), ("sq", 2), ("sq", 3)]
        for h in range(H):
            act_order += ([("exp", h + 2)] if h + 2 < H else []) + [("pt", h)]
            act_order += [("sq", h + 3), ("sq", h + 4)] if h % 2 and h + 4 < H else []
        act = Steps(b.sem(c, "q_act"), ["xt"] + [f"{k}{h}" for k, h in act_order])
        started = b.sem(c, "q_started")
        xt = b.sb(c, "xt", [128, 2, ROWS])
        junk = b.sb(c, "junk", [ROWS, 2, KD])
        sq = b.sb(c, "sq", [ROWS, H])
        shift = b.sb(c, "shift", [ROWS, H])
        phi = b.sb(c, "phi", [ROWS, 2, KD])
        phi1 = b.sb(c, "phi1", [ROWS, 2, KD])
        phit = b.sb(c, "phit", [128, 2, 2 * ROWS])
        inv = b.sb(c, "inv", [ROWS, 1])
        scatter = Scatter(b, c, plan)
        block = c.enter_context(nc.Block())

        @block.gpsimd
        def _(pool):
            scatter.gpsimd(pool)

        @block.sync
        def _(sp):
            scatter.sync(sp)

        @block.vector
        def _(v):
            dve.prime(v)
            v.tensor_tensor(y[:, :, 0:D], y[:, :, 0:D], bo[:].unsqueeze(1).to_broadcast([ROWS, TILES, D]), ALU.add).then_inc(started, 1)
            v.wait_ge(started, 1)
            with v.Fori(0, TILES) as t:
                y_t = y[:, bass.ds(t, 1), 0:D].rearrange("p a d -> p (a d)")

                def step(ins, name):
                    ins.then_inc(*dve.did(name))
                    v.wait_ge(*dve.now(t, name))

                for kind, h in dve_order:
                    if kind == "shift":
                        v.wait_ge(*act.now(t, f"sq{2 * h + 1}"))
                        v.wait_ge(*act.before(t, f"exp{2 * h + 1}"))
                        v.tensor_scalar(shift[:, 2 * h:2 * h + 2], sq[:, 2 * h:2 * h + 2], -0.5 * KSCALE * KSCALE, None,
                                        ALU.mult).then_inc(*dve.did(f"shift{h}"))
                    elif kind == "phi":
                        v.wait_ge(*act.now(t, f"exp{h}"))
                        v.wait_ge(*(pe.now(t, f"pt{h - 2}") if h >= 2 else pe.before(t, f"pt{H - 2 + h}")))
                        v.tensor_scalar(phi1[:, h % 2, :], phi[:, h % 2, :], KD ** -0.5, 1e-6, ALU.mult,
                                        ALU.add).then_inc(*dve.did(f"phi{h}"))
                    else:
                        v.wait_ge(*pe.now(t, f"g{h}"))
                        step(v.reciprocal(inv[:], ps[0:ROWS, 7, D:D + 1]), f"inv{h}")
                        step(v.scalar_tensor_tensor(out=y_t, in0=ps[0:ROWS, 7, 0:D], scalar=inv[:], in1=y_t, op0=ALU.mult,
                                                    op1=ALU.add), f"add{h}")

        @block.tensor
        def _(e):
            pe.prime(e)
            with e.Fori(0, TILES) as t:
                e.wait_ge(*act.now(t, "xt"))
                for kind, h in order:
                    if kind == "pair":
                        g = 2 * h + 1
                        e.wait_ge(*(act.now(t, f"sq{g - 4}") if g >= 4 else act.before(t, f"sq{H - 4 + g}")))
                        phi_projections(e, b, w, xt, ps[0:ROWS, 1 + h % 2, :], bias, 0, h * 512, 512).then_inc(*pe.did(f"pair{h}"))
                    elif kind == "u":
                        e.wait_ge(*(act.now(t, f"exp{h - 2}") if h >= 2 else act.before(t, f"exp{H - 2 + h}")))
                        phi_projections(e, b, wp, xt, ps[0:ROWS, 3 + h % 2, :], bias, 1, h * KD, KD).then_inc(*pe.did(f"u{h}"))
                    elif kind == "pt":
                        e.wait_ge(*dve.now(t, f"phi{h}"))
                        e.wait_ge(*(act.now(t, f"pt{h - 2}") if h >= 2 else act.before(t, f"pt{H - 2 + h}")))
                        for m in range(2):
                            last = e.transpose(ps[:, 5 + h % 2, m * ROWS:(m + 1) * ROWS], phi1[:, h % 2, 128 * m:128 * m + 128],
                                               b.ident[0:ROWS, 0:ROWS])
                        last.then_inc(*pe.did(f"pt{h}"))
                    else:
                        e.wait_ge(*act.now(t, f"pt{h}"))
                        e.wait_ge(*(dve.now(t, f"add{h - 1}") if h else dve.before(t, f"add{H - 1}")))
                        for m in range(2):
                            last = e.matmul(ps[0:ROWS, 7, 0:D + 1], lhsT=phit[:, h % 2, m * ROWS:(m + 1) * ROWS],
                                            rhs=kvo[:, 2 * h + m, :], start=m == 0, stop=m == 1)
                        last.then_inc(*pe.did(f"g{h}"))

        @block.scalar
        def _(a):
            act.prime(a)
            with a.Fori(0, TILES) as t:
                a.wait_ge(*pe.before(t, f"u{H - 1}"))
                a.activation(xt[:], xts[:, :, bass.ds(t * ROWS, ROWS)], ACT.Copy).then_inc(*act.did("xt"))
                for kind, h in act_order:
                    g = h // 2
                    if kind == "sq":
                        a.wait_ge(*pe.now(t, f"pair{g}"))
                        a.wait_ge(*dve.before(t, f"shift{g}"))
                        a.wait_ge(*(act.now(t, f"sq{h - 2}") if h >= 2 else act.before(t, f"sq{H - 2 + h}")))
                        a.activation(junk[:, h % 2, :], ps[0:ROWS, 1 + g % 2, (h % 2) * KD:(h % 2 + 1) * KD], ACT.Square,
                                     accum_out=sq[:, h:h + 1]).then_inc(*act.did(f"sq{h}"))
                    elif kind == "exp":
                        a.wait_ge(*dve.now(t, f"shift{g}"))
                        a.wait_ge(*pe.now(t, f"u{h}"))
                        a.wait_ge(*(dve.now(t, f"phi{h - 2}") if h >= 2 else dve.before(t, f"phi{H - 2 + h}")))
                        a.activation(phi[:, h % 2, :], ps[0:ROWS, 3 + h % 2, 0:KD], ACT.Exp, bias=shift[:, h:h + 1],
                                     scale=KSCALE).then_inc(*act.did(f"exp{h}"))
                    else:
                        a.wait_ge(*pe.now(t, f"pt{h}"))
                        a.wait_ge(*(pe.now(t, f"g{h - 2}") if h >= 2 else pe.before(t, f"g{H - 2 + h}")))
                        a.activation(phit[:, h % 2, :], ps[:, 5 + h % 2, 0:2 * ROWS], ACT.Copy).then_inc(*act.did(f"pt{h}"))


def mix0_tail(b, y, xts):
    names = ("g1", "beta1", "bias2")
    with ExitStack() as c:
        vec = {n: b.sb(c, n, [ROWS, D]) for n in names}
        w1 = b.sb(c, "w1", [128, 2, D])
        w2 = b.sb(c, "w2", [128, 2, D])
        bias1 = b.sb(c, "bias1", [128, 2])
        load(b, [(vec[n][:], broadcast(b.ins[f"L0_mix_{n}"], ROWS)) for n in names]
             + [(w1[:], b.ins["L0_mix_W1"].rearrange("(k p) n -> p k n", p=128)),
                (w2[:], b.ins["L0_mix_W2"].rearrange("(k p) n -> p k n", p=128)),
                (bias1[:], b.ins["bias1_columns"])])
        rows_and_columns(b, y, y, xts, 1e-6, vec["g1"], vec["beta1"])
        biased = b.sem(c, "biased")

        def bias(v):
            v.tensor_tensor(y[:, :, 0:D], y[:, :, 0:D], vec["bias2"][:].unsqueeze(1).to_broadcast([ROWS, TILES, D]), ALU.add).then_inc(biased, 1)
            v.wait_ge(biased, 1)

        def consume(v, g, j, t, rows, dve):
            y_t = y[:, bass.ds(t, 1), 0:D].rearrange("p a d -> p (a d)")
            v.tensor_tensor(y_t, y_t, rows, ALU.add).then_inc(*dve.did(f"y{j}"))

        feed_forward(b, xts, w1, bias1, w2, 2, ACT.Relu, ["y"], consume, bias)
    add_norm(b, y, 1e-6, "L0_mix_g2", "L0_mix_beta2", False)


def choose_rows(b, xn, chosen):
    nc, ps = b.nc, b.ps
    weights_row = b.dram("router_row", [N])
    with ExitStack() as c:
        wr = b.sb(c, "wr", [ROWS, D])
        br = b.sb(c, "br", [ROWS, 1])
        load(b, [(wr[:], broadcast(b.ins["L0_ffn_wr"], ROWS)), (br[:], broadcast(b.ins["L0_ffn_br"], ROWS))])
        dve = Steps(b.sem(c, "rt_dve"), ["dot"])
        weight = b.sb(c, "weight", [ROWS, TILES])
        every = b.sb(c, "every", [ROWS, N])
        junk = b.sb(c, "junk", [ROWS, D])
        flags = b.sb(c, "flags", [ROWS, N], BF16)
        above = b.sb(c, "above", [ROWS, 3, TILES])
        tri = b.sb(c, "tri", [ROWS, ROWS])
        tied = b.sb(c, "tied", [ROWS, ROWS])
        added, turned, copied = b.sem(c, "added"), b.sem(c, "turned"), b.sem(c, "copied")
        stored, ranked, tri_ready = b.sem(c, "stored"), b.sem(c, "ranked"), b.sem(c, "tri_ready")
        turned_weight = b.sb(c, "turned_weight", [TILES, ROWS])
        block = c.enter_context(nc.Block())

        @block.gpsimd
        def _(p):
            p.affine_select(out=tri[:], in_=b.ones[0:ROWS, 0:ROWS], compare_op=ALU.is_gt, fill=0.0, base=0,
                            pattern=[[-1, ROWS]], channel_multiplier=1).then_inc(tri_ready, 1)

        @block.tensor
        def _(e):
            e.wait_ge(added, 1)
            e.transpose(ps[0:TILES, 0, 0:ROWS], weight[:], b.ident[0:ROWS, 0:ROWS]).then_inc(turned, 1)

        @block.scalar
        def _(a):
            a.wait_ge(turned, 1)
            a.activation(turned_weight[:], ps[0:TILES, 0, 0:ROWS], ACT.Copy).then_inc(copied, 1)

        @block.sync
        def _(sp):
            sp.wait_ge(copied, 1)
            sp.dma_start(weights_row.rearrange("(t p) -> t p", p=ROWS), turned_weight[:]).then_inc(stored, 16)
            sp.wait_ge(stored, 16)
            sp.dma_start(every[:], broadcast(weights_row, ROWS)).then_inc(stored, 16)

        @block.vector
        def _(v):
            dve.prime(v)
            with v.Fori(0, TILES) as t:
                v.scalar_tensor_tensor(out=junk[:], in0=tile_of(xn, t), scalar=1.0, in1=wr[:], op0=ALU.mult, op1=ALU.mult,
                                       accum_out=weight[:, bass.ds(t, 1)]).then_inc(*dve.did("dot"))
                v.wait_ge(*dve.now(t, "dot"))
            v.tensor_scalar(weight[:], weight[:], br[:], None, ALU.add).then_inc(added, 1)
            v.wait_ge(stored, 32)
            v.wait_ge(added, 1)
            v.wait_ge(tri_ready, 1)
            n = 0
            v.memset(above[:], 0.0).then_inc(ranked, 1)
            v.wait_ge(ranked, 1)
            n = 1

            def count(ins):
                nonlocal n
                n += 1
                ins.then_inc(ranked, 1)
                v.wait_ge(ranked, n)

            for t in range(TILES):
                mine, lo, hi = weight[:, t:t + 1], t * ROWS, (t + 1) * ROWS
                if t:
                    count(v.tensor_scalar(flags[:, 0:lo], every[:, 0:lo], mine, 0.0, ALU.is_ge, ALU.add,
                                          accum_out=above[:, 0, t:t + 1]))
                count(v.tensor_scalar(flags[:, lo:N], every[:, lo:N], mine, 0.0, ALU.is_gt, ALU.add,
                                      accum_out=above[:, 1, t:t + 1]))
                count(v.scalar_tensor_tensor(out=tied[:], in0=every[:, lo:hi], scalar=mine, in1=tri[:], op0=ALU.is_equal,
                                             op1=ALU.mult, accum_out=above[:, 2, t:t + 1]))
            count(v.tensor_tensor(above[:, 0, :], above[:, 0, :], above[:, 1, :], ALU.add))
            count(v.tensor_tensor(above[:, 0, :], above[:, 0, :], above[:, 2, :], ALU.add))
            count(v.scalar_tensor_tensor(out=chosen[:], in0=above[:, 0, :], scalar=float(KK), in1=weight[:], op0=ALU.is_lt,
                                         op1=ALU.mult))


def ffn0(b, xn, xts, chosen):
    parts = HID // 128
    with ExitStack() as c:
        w1 = b.sb(c, "w1", [128, 2, HID])
        w2 = b.sb(c, "w2", [128, parts, D])
        b1 = b.sb(c, "b1", [128, parts])
        b2 = b.sb(c, "b2", [ROWS, D])
        y = b.sb(c, "y", [ROWS, D])
        added = b.sem(c, "xn_added")
        load(b, [(w1[:], b.ins["L0_ffn_w1"].rearrange("(k p) n -> p k n", p=128)),
                 (w2[:], b.ins["L0_ffn_w2"].rearrange("(k p) n -> p k n", p=128)),
                 (b1[:], b.ins["ffn_b1_columns"]), (b2[:], broadcast(b.ins["L0_ffn_b2"], ROWS))])

        def add_xn(v):
            v.tensor_tensor(b.x[:], b.x[:], xn[:, :, 0:D], ALU.add).then_inc(added, 1)
            v.wait_ge(added, 1)

        def consume(v, g, j, t, rows, dve):
            v.wait_ge(*(dve.now(g, f"x{j - 1}") if j else dve.before(g, f"x{GROUP - 1}")))
            v.tensor_tensor(y[:], rows, b2[:], ALU.add).then_inc(*dve.did(f"y{j}"))
            v.wait_ge(*dve.now(g, f"y{j}"))
            v.scalar_tensor_tensor(out=tile_of(b.x, t), in0=y[:], scalar=chosen[:, bass.ds(t, 1)], in1=tile_of(b.x, t),
                                   op0=ALU.mult, op1=ALU.add).then_inc(*dve.did(f"x{j}"))

        feed_forward(b, xts, w1, b1, w2, parts, ACT.Gelu_apprx_tanh, ["y", "x"], consume, add_xn)


def products(unit, n):
    whole = unit[:]
    rows, step = whole.ap[0][1], whole.ap[0][0]
    base = whole.offset + n * (HD + HD // 2)
    two = bass.AP(tensor=whole.tensor, offset=base, ap=[[step, rows], [1, OFFS], [1, HD]])
    one = bass.AP(tensor=whole.tensor, offset=base, ap=[[step, rows], [0, OFFS], [1, HD]])
    return two, one


def mix1(b, keys, xts, moments, y=None):
    nc, ps = b.nc, b.ps
    cols = 2 * D if keys else D
    chunks = FEAT // 128
    units = H * chunks
    wide = HD + 1
    scale = float(HD) ** 0.25
    bank_units = 512 // wide
    spans = [(i * bank_units, min(units, (i + 1) * bank_units)) for i in range(3)]
    with ExitStack() as c:
        w = b.sb(c, "w", [128, 2, cols])
        bias = b.sb(c, "bias", [ROWS, cols])
        rows = b.sb(c, "rows", [ROWS, TILES, D])
        length = b.sb(c, "length", [ROWS, 4, TILES * H])
        first = D if keys else 0
        pairs = [(w[:], b.ins["Wqkv_T"].rearrange("(k p) n -> p k n", p=128)[:, :, first:first + cols]),
                 (bias[:], broadcast(b.ins["L1_mix_bqkv"][first:first + cols], ROWS))]
        if keys:
            coef = b.sb(c, "coef", [128, chunks])
            values = b.sb(c, "values", [ROWS, TILES, H * wide])
            pairs += [(coef[:], b.ins["mix1_coef"])]
        else:
            temp = b.sb(c, "temp", [ROWS, H])
            pairs += [(temp[:], broadcast(b.ins["L1_mix_temperature"], ROWS))]
        load(b, pairs)

        cleared = b.sem(c, "v_cleared")

        def ones_in_values(v):
            v.memset(values[:], 1.0).then_inc(cleared, 1)
            v.wait_ge(cleared, 1)

        def biased(v, t, i, bank, dve):
            if keys:
                v.tensor_tensor(tile_of(values, t).rearrange("p (h e) -> p h e", h=H)[:, :, 1:wide],
                                bank[:, D:2 * D].rearrange("p (h e) -> p h e", h=H),
                                bias[:, D:2 * D].rearrange("p (h e) -> p h e", h=H), ALU.add).then_inc(*dve.did("v"))
            v.tensor_tensor(tile_of(rows, t), bank[:, 0:D], bias[:, 0:D], ALU.add).then_inc(*dve.did("kq"))

        project(b, xts, w, cols, ["v", "kq"] if keys else ["kq"], biased, ones_in_values if keys else None)

        with ExitStack() as c2:
            sq = b.sb(c2, "sq", [ROWS, 2, GROUP * D])
            power = b.sb(c2, "power", [ROWS, TILES * H])
            dve = Steps(b.sem(c2, "ln_dve"), ["sq", "sum"])
            ready, chain, rooted = b.sem(c2, "ln_ready"), b.sem(c2, "ln_chain"), b.sem(c2, "ln_rooted")
            block = c2.enter_context(nc.Block())

            @block.vector
            def _(v):
                dve.prime(v)
                with v.Fori(0, GROUPS) as g:
                    v.wait_ge(*dve.before(g, "sum"))
                    rows_g = group_of(rows, g)
                    v.tensor_tensor(sq[:, 0, :].rearrange("p (j d) -> p j d", d=D), rows_g, rows_g, ALU.mult).then_inc(*dve.did("sq"))
                    v.wait_ge(*dve.now(g, "sq"))
                    v.tensor_reduce(length[:, 0, bass.ds(g * (GROUP * H), GROUP * H)],
                                    sq[:, 0, :].rearrange("p (h i) -> p h i", i=HD), AX.X, ALU.add).then_inc(*dve.did("sum"))
                v.memset(power[:], 0.5).then_inc(ready, 1)
                v.wait_ge(rooted, 1)
                v.tensor_scalar(length[:, 2, :], length[:, 1, :], 1.0 if keys else scale, 1e-12, ALU.mult, ALU.max).then_inc(chain, 1)
                v.wait_ge(chain, 1)
                v.reciprocal(length[:, 3, :], length[:, 2, :]).then_inc(chain, 1)
                v.wait_ge(chain, 2)
                if keys:
                    v.tensor_scalar(length[:, 3, :], length[:, 3, :], scale, None, ALU.mult).then_inc(chain, 1)
                else:
                    v.scalar_tensor_tensor(out=length[:, 3, :].rearrange("p (t h) -> p t h", h=H),
                                           in0=length[:, 3, :].rearrange("p (t h) -> p t h", h=H), scalar=scale * scale,
                                           in1=temp[:].unsqueeze(1).to_broadcast([ROWS, TILES, H]), op0=ALU.mult,
                                           op1=ALU.mult).then_inc(chain, 1)

            @block.gpsimd
            def _(p):
                p.wait_ge(ready, 1)
                p.wait_ge(*dve.now(GROUPS - 1, "sum"))
                p.tensor_tensor(length[:, 1, :], length[:, 0, :], power[:], ALU.pow).then_inc(rooted, 1)

        dve = Steps(b.sem(c, "m1_dve"), ["unit", "again"] + [f"f{h}" for h in range(H)], lead=2)
        dve_o = Steps(b.sem(c, "m1_out"), ["div", "out"], lead=2)
        pe = Steps(b.sem(c, "m1_pe"), ["sums"] if keys else
                   [n for h in range(H + 1) for n in ([f"ft{h}_0", f"ft{h}_1"] if h < H else []) + ([f"y{h - 1}"] if h else [])], lead=2)
        act = Steps(b.sem(c, "m1_act"), ["lin"] + (["values"] if keys else [n for h in range(H) for n in (f"ft{h}_0", f"ft{h}_1")]), lead=2)
        cleared = b.sem(c, "m1_cleared")
        unit = b.sb(c, "unit", [ROWS, 2, H, HD + HD // 2])
        feat = b.sb(c, "feat", [ROWS, 2, H, FEAT])
        if keys:
            zeros = b.sb(c, "zeros", [1, 512], BF16)
            mine = b.sb(c, "mine", [ROWS, 2, H * wide])
        else:
            featt = b.sb(c, "featt", [128, 2, chunks, ROWS])
            inv = b.sb(c, "inv", [ROWS, H])
        block = c.enter_context(nc.Block())
        clears = 3 if keys else 2
        last_read = "sums" if keys else f"ft{H - 1}_1"

        @block.vector
        def _(v):
            dve.prime(v)
            v.memset(feat[:, :, :, QUAD:FEAT], 0.0).then_inc(cleared, 1)
            if keys:
                v.memset(zeros[:], 0.0).then_inc(cleared, 1)
            v.wait_ge(cleared, clears - 1)
            v.memset(feat[:, :, :, QUAD + HD:QUAD + HD + 1], 1.0).then_inc(cleared, 1)

            def features(t, i):
                v.wait_ge(*act.back(t, 2, "lin"))
                v.tensor_tensor(unit[:, i, :, 0:HD], tile_of(rows, t).rearrange("p (h i) -> p h i", h=H),
                                length[:, 3, bass.ds(t * H, H)].unsqueeze(2).to_broadcast([ROWS, H, HD]), ALU.mult).then_inc(*dve.did("unit"))
                v.wait_ge(*dve.now(t, "unit"))
                v.tensor_scalar(unit[:, i, :, HD:], unit[:, i, :, 0:HD // 2], 1.0, None, ALU.mult).then_inc(*dve.did("again"))
                v.wait_ge(*dve.now(t, "again"))
                v.wait_ge(*pe.back(t, 2, last_read))
                for h in range(H):
                    two, one = products(unit, i * H + h)
                    v.tensor_tensor(feat[:, i, h, 0:QUAD].rearrange("p (o i) -> p o i", i=HD), two, one, ALU.mult).then_inc(*dve.did(f"f{h}"))

            def divided(t, i):
                v.wait_ge(*pe.now(t, f"y{H - 1}"))
                v.wait_ge(*dve_o.before(t, "out"))
                sums = ps[0:ROWS, 6 + i, 0:H * wide].rearrange("p (h e) -> p h e", h=H)
                v.reciprocal(inv[:], sums[:, :, 0]).then_inc(*dve_o.did("div"))
                v.wait_ge(*dve_o.now(t, "div"))
                v.tensor_tensor(tile_of(y, t).rearrange("p (h e) -> p h e", h=H), sums[:, :, 1:wide],
                                inv[:].unsqueeze(2).to_broadcast([ROWS, H, HD]), ALU.mult).then_inc(*dve_o.did("out"))

            if keys:
                tiles_in_pairs(v, features)
            else:
                dve_o.prime(v)
                features(0, 0)
                with v.Fori(0, TILES // 2) as r:
                    for i in range(2):
                        features(r * 2 + (i + 1), 1 - i)
                        divided(r * 2 + i, i)
                divided(TILES - 1, 0)
            if keys:
                v.wait_ge(*pe.now(TILES - 1, "sums"))
                for i, (lo, hi) in enumerate(spans):
                    v.tensor_scalar(moments[:, lo:hi, :].rearrange("p u e -> p (u e)"), ps[:, i, 0:(hi - lo) * wide], 1.0, None,
                                    ALU.mult).then_inc(cleared, 1)
                v.wait_ge(cleared, clears + 3)
                for h in range(H):
                    part = moments[:, h * chunks:(h + 1) * chunks, :]
                    v.tensor_tensor(part, part, coef[:].unsqueeze(2).to_broadcast([128, chunks, wide]), ALU.mult).then_inc(cleared, 1)

        @block.tensor
        def _(e):
            pe.prime(e)
            e.wait_ge(cleared, clears)

            def summed(t, i):
                for u in range(units):
                    h, k = divmod(u, chunks)
                    if k == 0:
                        e.wait_ge(*dve.now(t, f"f{h}"))
                    if u == 0:
                        e.wait_ge(*act.now(t, "values"))
                    lo, hi = spans[u // bank_units]
                    last = e.matmul(ps[:, u // bank_units, (u - lo) * wide:(u - lo + 1) * wide],
                                    lhsT=feat[:, i, h, 128 * k:128 * k + 128],
                                    rhs=mine[:, i, h * wide:(h + 1) * wide],
                                    start=False, stop=isinstance(t, int) and u == hi - 1)
                last.then_inc(*pe.did("sums"))

            def multiplied(t, i):
                e.wait_ge(*act.now(t, "lin"))
                e.wait_ge(*dve_o.back(t, 2, "out"))
                for h in range(H + 1):
                    if h < H:
                        e.wait_ge(*dve.now(t, f"f{h}"))
                        for m, (lo, hi) in enumerate(((0, 3), (3, chunks))):
                            e.wait_ge(*(act.now(t, f"ft{h - 2}_{m}") if h >= 2 else act.before(t, f"ft{H - 2 + h}_{m}")))
                            for k in range(lo, hi):
                                last = e.transpose(ps[:, 2 * (h % 2) + m, (k - lo) * ROWS:(k - lo + 1) * ROWS],
                                                   feat[:, i, h, 128 * k:128 * k + 128], b.ident[0:ROWS, 0:ROWS])
                            last.then_inc(*pe.did(f"ft{h}_{m}"))
                    if h:
                        e.wait_ge(*act.now(t, f"ft{h - 1}_1"))
                        for k in range(chunks):
                            last = e.matmul(ps[0:ROWS, 6 + i, (h - 1) * wide:h * wide], lhsT=featt[:, (h - 1) % 2, k, :],
                                            rhs=moments[:, (h - 1) * chunks + k, :], start=k == 0, stop=k == chunks - 1)
                        last.then_inc(*pe.did(f"y{h - 1}"))

            if keys:
                for i, (lo, hi) in enumerate(spans):
                    e.matmul(ps[:, i, 0:(hi - lo) * wide], lhsT=zeros[:, 0:128], rhs=zeros[:, 0:(hi - lo) * wide], start=True, stop=False)
                tiles_in_pairs(e, summed)
            else:
                tiles_in_pairs(e, multiplied)

        @block.scalar
        def _(a):
            act.prime(a)
            a.wait_ge(cleared, clears)

            def body(t, i):
                a.wait_ge(*dve.now(t, "unit"))
                a.wait_ge(*pe.back(t, 2, last_read))
                a.activation(feat[:, i, :, QUAD:QUAD + HD], unit[:, i, :, 0:HD], ACT.Copy).then_inc(*act.did("lin"))
                if keys:
                    a.activation(mine[:, i], tile_of(values, t), ACT.Copy).then_inc(*act.did("values"))
                else:
                    for h in range(H):
                        for m, (lo, hi) in enumerate(((0, 3), (3, chunks))):
                            a.wait_ge(*pe.now(t, f"ft{h}_{m}"))
                            if m == 0:
                                a.wait_ge(*(pe.now(t, f"y{h - 2}") if h >= 2 else pe.before(t, f"y{H - 2 + h}")))
                            a.activation(featt[:, h % 2, lo:hi, :].rearrange("p k n -> p (k n)"),
                                         ps[:, 2 * (h % 2) + m, 0:(hi - lo) * ROWS], ACT.Copy).then_inc(*act.did(f"ft{h}_{m}"))

            tiles_in_pairs(a, body)


def mix1_output(b, y, xts):
    with ExitStack() as c:
        proj = b.sb(c, "proj", [128, 2, D])
        bproj = b.sb(c, "bproj", [ROWS, D])
        load(b, [(proj[:], b.ins["Wproj_T"].rearrange("(k p) n -> p k n", p=128)), (bproj[:], broadcast(b.ins["L1_mix_bproj"], ROWS))])
        rows_and_columns(b, y, None, xts)
        biased = b.sem(c, "biased")

        def bias(v):
            v.tensor_tensor(b.x[:], b.x[:], bproj[:].unsqueeze(1).to_broadcast([ROWS, TILES, D]), ALU.add).then_inc(biased, 1)
            v.wait_ge(biased, 1)

        def consume(v, t, i, bank, dve):
            v.tensor_tensor(tile_of(b.x, t), tile_of(b.x, t), bank, ALU.add).then_inc(*dve.did("x"))

        project(b, xts, proj, D, ["x"], consume, bias)


def moe(b, ctx):
    nc, ps = b.nc, b.ps
    parts = EF // 128
    xts = b.sb(ctx, "xts", [128, 2, N])
    y = b.sb(ctx, "y", [ROWS, TILES, D])
    gates = b.sb(ctx, "gates", [ROWS, TILES, EXPERTS])
    rows_and_columns(b, b.x, y, xts, 1e-5)
    with ExitStack() as c:
        gw = b.sb(c, "gw", [128, 2, EXPERTS])
        gb = b.sb(c, "gb", [ROWS, EXPERTS])
        b2 = b.sb(c, "b2", [EXPERTS, D])
        logits = b.sb(c, "logits", [ROWS, TILES, EXPERTS])
        load(b, [(gw[:], b.ins["L1_ffn_gate_w"].rearrange("(k p) n -> p k n", p=128)),
                 (gb[:], broadcast(b.ins["L1_ffn_gate_b"], ROWS)), (b2[:], b.ins["L1_ffn_b2"])])

        def biased(v, t, i, bank, dve):
            v.tensor_tensor(tile_of(logits, t), bank, gb[:], ALU.add).then_inc(*dve.did("logits"))

        project(b, xts, gw, EXPERTS, ["logits"], biased)
        choose_experts(b, logits, gates)
        add_second_biases(b, gates, b2, y)

    group = 5
    groups = TILES // group
    split = ((0, 3 * ROWS), (3 * ROWS, 5 * ROWS))
    with ExitStack() as c:
        w1 = b.sb(c, "w1", [128, 2, 2, EF])
        w2 = b.sb(c, "w2", [128, 2, parts, D])
        b1 = b.sb(c, "b1", [128, 2, parts])
        hidden = b.sb(c, "hidden", [128, parts, group * ROWS])
        gates2 = gates[:].rearrange("p t e -> p (t e)")
        dve = Steps(b.sem(c, "e_dve"), [f"y{i}" for i in range(group)])
        pe = Steps(b.sem(c, "e_pe"), [f"h{m}_{i}" for m in range(parts) for i in range(2)] + [f"y{i}" for i in range(group)],
                   lead=2 * groups)
        act = Steps(b.sem(c, "e_act"), [f"h{m}_{i}" for m in range(parts) for i in range(2)], lead=2 * groups)
        loaded = [b.sem(c, f"loaded{i}") for i in range(2)]
        block = c.enter_context(nc.Block())

        @block.sync
        def _(sp):
            with sp.Fori(0, EXPERTS // 2) as r:
                for i in range(2):
                    ex = r * 2 + i
                    sp.wait_ge(*pe.back(ex * groups, groups + 1, f"y{group - 1}"))
                    sp.dma_start(w1[:, i], b.ins["moe_w1"][bass.ds(ex * 128, 128), :].rearrange("p (k f) -> p k f", k=2)).then_inc(loaded[i], 16)
                    sp.dma_start(w2[:, i], b.ins["moe_w2"][bass.ds(ex * 128, 128), :].rearrange("p (k f) -> p k f", k=parts)).then_inc(loaded[i], 16)
                    sp.wait_ge(*act.back(ex * groups, groups + 1, f"h{parts - 1}_1"))
                    sp.dma_start(b1[:, i], b.ins["moe_b1"][bass.ds(ex * 128, 128), :]).then_inc(loaded[i], 16)

        @block.tensor
        def _(e):
            pe.prime(e)
            with e.Fori(0, EXPERTS // 2) as r:
                for i in range(2):
                    with e.Fori(0, groups) as g:
                        e.wait_ge(loaded[i], r * 48 + 48)
                        t = (r * 2 + i) * groups + g
                        for m in range(parts):
                            for n, (lo, hi) in enumerate(split):
                                e.wait_ge(*(act.now(t, f"h{m - 2}_{n}") if m >= 2 else act.before(t, f"h{parts - 2 + m}_{n}")))
                                for k in range(2):
                                    last = e.matmul(ps[:, 2 * (m % 2) + n, 0:hi - lo], lhsT=w1[:, i, k, 128 * m:128 * m + 128],
                                                    rhs=xts[:, k, bass.ds(g * (group * ROWS) + lo, hi - lo)], start=k == 0, stop=k == 1)
                                last.then_inc(*pe.did(f"h{m}_{n}"))
                        e.wait_ge(*act.now(t, f"h{parts - 1}_1"))
                        for j in range(group):
                            e.wait_ge(*(dve.now(t, f"y{j - 4}") if j >= 4 else dve.before(t, f"y{j if j else 4}")))
                            for m in range(parts):
                                last = e.matmul(ps[0:ROWS, 4 + j % 4, 0:D], lhsT=hidden[:, m, j * ROWS:(j + 1) * ROWS],
                                                rhs=w2[:, i, m, :], start=m == 0, stop=m == parts - 1)
                            last.then_inc(*pe.did(f"y{j}"))

        @block.scalar
        def _(a):
            act.prime(a)
            with a.Fori(0, EXPERTS // 2) as r:
                for i in range(2):
                    with a.Fori(0, groups) as g:
                        a.wait_ge(loaded[i], r * 48 + 48)
                        t = (r * 2 + i) * groups + g
                        for m in range(parts):
                            for n, (lo, hi) in enumerate(split):
                                a.wait_ge(*pe.now(t, f"h{m}_{n}"))
                                if m == 0 and n == 0:
                                    a.wait_ge(*pe.before(t, f"y{group - 1}"))
                                a.activation(hidden[:, m, lo:hi], ps[:, 2 * (m % 2) + n, 0:hi - lo], ACT.Relu,
                                             bias=b1[:, i, m:m + 1]).then_inc(*act.did(f"h{m}_{n}"))

        @block.vector
        def _(v):
            dve.prime(v)
            with v.Fori(0, EXPERTS // 2) as r:
                for i in range(2):
                    with v.Fori(0, groups) as g:
                        t = (r * 2 + i) * groups + g
                        for j in range(group):
                            y_t = tile_of(y, g * group + j)
                            gate = gates2[:, bass.ds((g * group + j) * EXPERTS + (r * 2 + i), 1)]
                            v.wait_ge(*pe.now(t, f"y{j}"))
                            v.scalar_tensor_tensor(out=y_t, in0=ps[0:ROWS, 4 + j % 4, 0:D], scalar=gate, in1=y_t, op0=ALU.mult,
                                                   op1=ALU.add).then_inc(*dve.did(f"y{j}"))
                            v.wait_ge(*dve.now(t, f"y{j}"))

    add_norm(b, y, 1e-5, "L1_ffn_gamma", "L1_ffn_beta", True)


def choose_experts(b, logits, gates):
    all3 = [ROWS, TILES, EXPERTS]
    with ExitStack() as c:
        places = b.sb(c, "places", all3)
        best = b.sb(c, "best", [ROWS, 2, TILES])
        place = b.sb(c, "place", [ROWS, 2, TILES])
        one = b.sb(c, "one", [ROWS, 2, TILES * EXPERTS])
        weight = b.sb(c, "weight", [ROWS, 4, TILES])
        dve_did, exp_did = b.sem(c, "ce_dve"), b.sem(c, "ce_exp")
        block = c.enter_context(b.nc.Block())
        count = [0]
        index = b.row_no[0:ROWS, 0:EXPERTS].unsqueeze(1).to_broadcast(all3)
        ones = [one[:, i, :].rearrange("p (t e) -> p t e", e=EXPERTS) for i in range(2)]

        def spread(row):
            return row.unsqueeze(2).to_broadcast(all3)

        @block.vector
        def _(v):
            def step(ins):
                count[0] += 1
                ins.then_inc(dve_did, 1)
                v.wait_ge(dve_did, count[0])

            for i in range(2):
                step(v.tensor_reduce(best[:, i, :], logits[:], AX.X, ALU.max))
                step(v.tensor_tensor(ones[i], logits[:], spread(best[:, i, :]), ALU.is_equal))
                step(v.scalar_tensor_tensor(out=places[:], in0=index, scalar=-float(EXPERTS), in1=ones[i], op0=ALU.add, op1=ALU.mult))
                step(v.tensor_reduce(place[:, i, :], places[:], AX.X, ALU.min))
                step(v.tensor_scalar(place[:, i, :], place[:, i, :], float(EXPERTS), None, ALU.add))
                step(v.tensor_tensor(ones[i], index, spread(place[:, i, :]), ALU.is_equal))
                if i == 0:
                    step(v.scalar_tensor_tensor(out=logits[:], in0=ones[0], scalar=-3e38, in1=logits[:], op0=ALU.mult, op1=ALU.add))
            step(v.tensor_tensor(weight[:, 0, :], best[:, 1, :], best[:, 0, :], ALU.subtract))
            v.wait_ge(exp_did, 1)
            step(v.tensor_scalar(weight[:, 2, :], weight[:, 1, :], 1.0, None, ALU.add))
            step(v.reciprocal(weight[:, 2, :], weight[:, 2, :]))
            step(v.tensor_tensor(weight[:, 3, :], weight[:, 1, :], weight[:, 2, :], ALU.mult))
            for i in range(2):
                step(v.tensor_tensor(ones[i], ones[i], spread(weight[:, 2 + i, :]), ALU.mult))
            step(v.tensor_tensor(gates[:], ones[0], ones[1], ALU.add))

        @block.scalar
        def _(a):
            a.wait_ge(dve_did, 14)
            a.activation(weight[:, 1, :], weight[:, 0, :], ACT.Exp).then_inc(exp_did, 1)


def add_second_biases(b, gates, b2, y):
    nc, ps = b.nc, b.ps
    with ExitStack() as c:
        dve_a = Steps(b.sem(c, "sb_copied"), ["gates"], lead=2)
        dve_b = Steps(b.sem(c, "sb_added"), ["y"], lead=2)
        pe_a = Steps(b.sem(c, "sb_turned"), ["turn"], lead=2)
        pe_b = Steps(b.sem(c, "sb_multiplied"), ["b2"], lead=2)
        act = Steps(b.sem(c, "sb_act"), ["gt"], lead=2)
        mine = b.sb(c, "mine", [ROWS, 2, EXPERTS])
        gt = b.sb(c, "gt", [EXPERTS, 2, ROWS])
        block = c.enter_context(nc.Block())

        def lagged(eng, first, second):
            first(0, 0)
            with eng.Fori(0, TILES // 2) as r:
                for i in range(2):
                    first(r * 2 + (i + 1), 1 - i)
                    second(r * 2 + i, i)
            second(TILES - 1, 0)

        @block.vector
        def _(v):
            dve_a.prime(v)
            dve_b.prime(v)

            def copied(t, i):
                v.wait_ge(*pe_a.back(t, 2, "turn"))
                v.tensor_scalar(mine[:, i, :], tile_of(gates, t), 1.0, None, ALU.mult).then_inc(*dve_a.did("gates"))

            def added(t, i):
                v.wait_ge(*pe_b.now(t, "b2"))
                v.tensor_tensor(tile_of(y, t), tile_of(y, t), ps[0:ROWS, 2 + i, 0:D], ALU.add).then_inc(*dve_b.did("y"))

            lagged(v, copied, added)

        @block.tensor
        def _(e):
            pe_a.prime(e)
            pe_b.prime(e)

            def turned(t, i):
                e.wait_ge(*dve_a.now(t, "gates"))
                e.wait_ge(*act.back(t, 2, "gt"))
                e.transpose(ps[0:EXPERTS, i, 0:ROWS], mine[:, i, :], b.ident[0:ROWS, 0:ROWS]).then_inc(*pe_a.did("turn"))

            def multiplied(t, i):
                e.wait_ge(*act.now(t, "gt"))
                e.wait_ge(*dve_b.back(t, 2, "y"))
                e.matmul(ps[0:ROWS, 2 + i, 0:D], lhsT=gt[:, i, :], rhs=b2[:], start=True, stop=True).then_inc(*pe_b.did("b2"))

            lagged(e, turned, multiplied)

        @block.scalar
        def _(a):
            act.prime(a)

            def body(t, i):
                a.wait_ge(*pe_a.now(t, "turn"))
                a.wait_ge(*pe_b.back(t, 2, "b2"))
                a.activation(gt[:, i, :], ps[0:EXPERTS, i, 0:ROWS], ACT.Copy).then_inc(*act.did("gt"))

            tiles_in_pairs(a, body)


def mix1_factors():
    scale = float(HD) ** 0.25
    f = np.zeros(FEAT)
    for o in range(OFFS):
        f[o * HD:(o + 1) * HD] = 0.5 * (2.0 if 0 < o < HD // 2 else 1.0)
    f[QUAD:QUAD + HD] = scale ** 2
    f[QUAD + HD] = scale ** 4
    return np.ascontiguousarray((f / N).reshape(FEAT // 128, 128).T.astype(np.float32))


def program(nc, ins, out):
    b = Build(nc, ins, out)
    with ExitStack() as whole, ExitStack() as ctx:
        b.whole = whole
        constants(b, ctx)

        def attend(g, which, xts, names, heads, bias_name, into, add):
            with ExitStack() as c:
                width = D + heads
                acc = b.sb(c, "acc", [ROWS, SLOTS * width])
                with ExitStack() as c2:
                    e_all = b.sb(c2, "e_all", [128, CHUNKS, heads])
                    top = b.sb(c2, "top", [ROWS, SLOTS * heads])
                    own = node_tables(b, c2, which, xts, graph_weights(b, c2, *names, heads), heads)
                    edge_scores(b, g, b.score[which], own, heads, e_all, top)
                    edge_sums(b, g, b.table[which], heads, e_all, top, acc)
                bias = b.sb(c, "bias", [ROWS, D])
                load(b, [(bias[:], broadcast(b.ins[bias_name], ROWS))])
                edge_mean(b, acc, heads, bias[:], into, add)

        plan = [EdgePlan(b, ctx, i) for i in range(2)]
        with ExitStack() as c:
            xts = b.sb(c, "xts", [128, 2, N])
            kvo = b.sb(c, "kvo", [128, 2 * H, D + 1])
            plan_edges(b, plan[0], "src", "dst", True)
            plan_edges(b, plan[1], "dst", "src", False)
            xn = b.sb(c, "xn", [ROWS, TILES, D + 1])
            rows_and_columns(b, b.x, xn, xts, 1e-5)
            with ExitStack() as c2:
                gram = b.sb(c2, "gram", [128, 2 * H, D + 1])
                with ExitStack() as c3:
                    mix0_keys(b, xn, xts, gram, *phi_weights(b, c3, "k"), plan[0])
                mix0_values(b, kvo, gram)
            clear_semaphores(b)
            with ExitStack() as c2:
                mix0_queries(b, xn, xts, *phi_weights(b, c2, "q"), kvo, plan[1])
            with ExitStack() as c2:
                g = listed_edges(b, c2, plan[0], True)
                attend(g, 0, xts, ("L0_gnn_W", "L0_gnn_a_self", "L0_gnn_a_neigh"), HG, "L0_gnn_bias", b.x, True)
            clear_semaphores(b)
            mix0_tail(b, xn, xts)
        with ExitStack() as c:
            xts = b.sb(c, "xts", [128, 2, N])
            xn = b.sb(c, "xn", [ROWS, TILES, D])
            chosen = b.sb(c, "chosen", [ROWS, TILES])
            rows_and_columns(b, b.x, xn, xts, 1e-5)
            choose_rows(b, xn, chosen)
            ffn0(b, xn, xts, chosen)
        clear_semaphores(b)
        with ExitStack() as c:
            xts = b.sb(c, "xts", [128, 2, N])
            with ExitStack() as c2:
                g = listed_edges(b, c2, plan[1], False)
                rows_and_columns(b, b.x, None, xts, 1e-5)
                y = b.sb(c2, "y", [ROWS, TILES, D])
                attend(g, 1, xts, ("L1_gnn_W1", "L1_gnn_a_dst1", "L1_gnn_a_src1"), HG, "L1_gnn_b1", y, False)
                yts = b.sb(c2, "yts", [128, 2, N])
                rows_and_columns(b, y, None, yts)
                attend(g, 2, yts, ("L1_gnn_W2", "L1_gnn_a_dst2", "L1_gnn_a_src2"), 1, "L1_gnn_b2", b.x, True)
            moments = b.sb(c, "moments", [128, H * (FEAT // 128), HD + 1])
            mix1(b, True, xts, moments)
            y = b.sb(c, "y", [ROWS, TILES, D])
            mix1(b, False, xts, moments, y)
            mix1_output(b, y, xts)
        clear_semaphores(b)
        with ExitStack() as c:
            moe(b, c)


def clear_semaphores(b):
    with b.nc.Block() as block:
        @block.sync
        def _(sp):
            for used in b.used:
                sp.sem_clear(used)
    b.used = []


def host_layout(i):
    c = np.ascontiguousarray
    a = {k: np.asarray(v) for k, v in i.items()}
    g = {
        "x": a["x"], "src": a["src"], "dst": a["dst"], "edge_weight": a["edge_weight"],
        "L0_gnn_W": a["L0_gnn_W"].transpose(1, 0, 2).reshape(D, D),
        "Wq_T": a["L0_mix_Wq"].reshape(D, H * KD).T, "Wk_T": a["L0_mix_Wk"].reshape(D, H * KD).T,
        "proj_T": a["L0_mix_proj"].T,
        "bq_columns": a["L0_mix_bq"].reshape(2 * H, 128).T, "bk_columns": a["L0_mix_bk"].reshape(2 * H, 128).T,
        "L0_mix_Wo": a["L0_mix_Wo"].reshape(H * KD, D),
        "bias1_columns": a["L0_mix_bias1"].reshape(2, 128).T,
    }
    g |= {
        "L0_ffn_wr": a["L0_ffn_wr"].reshape(D), "L0_ffn_br": a["L0_ffn_br"], "L0_ffn_w1": a["L0_ffn_w1"],
        "L0_ffn_w2": a["L0_ffn_w2"], "ffn_b1_columns": a["L0_ffn_b1"].reshape(HID // 128, 128).T, "L0_ffn_b2": a["L0_ffn_b2"],
        "L1_gnn_W1": a["L1_gnn_W1"], "L1_gnn_W2": a["L1_gnn_W2"], "L1_gnn_b1": a["L1_gnn_b1"], "L1_gnn_b2": a["L1_gnn_b2"],
        "Wqkv_T": a["L1_mix_Wqkv"].T, "L1_mix_bqkv": a["L1_mix_bqkv"], "Wproj_T": a["L1_mix_Wproj"].T,
        "L1_mix_bproj": a["L1_mix_bproj"], "L1_mix_temperature": a["L1_mix_temperature"].reshape(H),
        "mix1_coef": mix1_factors(),
        "L1_ffn_gate_w": a["L1_ffn_gate_w"], "L1_ffn_gate_b": a["L1_ffn_gate_b"], "L1_ffn_b2": a["L1_ffn_b2"],
        "moe_w1": a["L1_ffn_w1"].reshape(EXPERTS, 2, 128, EF).transpose(0, 2, 1, 3).reshape(EXPERTS * 128, 2 * EF),
        "moe_w2": a["L1_ffn_w2"].reshape(EXPERTS, EF // 128, 128, D).transpose(0, 2, 1, 3).reshape(EXPERTS * 128, EF // 128 * D),
        "moe_b1": a["L1_ffn_b1"].reshape(EXPERTS, EF // 128, 128).transpose(0, 2, 1).reshape(EXPERTS * 128, EF // 128),
        "L1_ffn_gamma": a["L1_ffn_gamma"], "L1_ffn_beta": a["L1_ffn_beta"],
    }
    for n in ("L1_gnn_a_src1", "L1_gnn_a_dst1", "L1_gnn_a_src2", "L1_gnn_a_dst2"):
        g[n] = a[n].reshape(D)
    for n in ("Wq", "Wk", "Wv"):
        g[f"L0_mix_{n}"] = a[f"L0_mix_{n}"].reshape(D, H * KD)
    for n in ("bq", "bk", "bv"):
        g[f"L0_mix_{n}"] = a[f"L0_mix_{n}"].reshape(H * KD)
    for n in ("L0_mix_bo", "L0_mix_g1", "L0_mix_beta1", "L0_mix_bias2", "L0_mix_g2", "L0_mix_beta2", "L0_mix_W1", "L0_mix_W2"):
        g[n] = a[n]
    for n in ("L0_gnn_a_self", "L0_gnn_a_neigh", "L0_gnn_bias"):
        g[n] = a[n].reshape(D)
    return {k: c(v) for k, v in g.items()}


def kernel(**inputs):
    import concourse.bacc as bacc
    from concourse.bass_utils import run_bass_kernel_spmd as run

    nc = bacc.Bacc("TRN2", target_bir_lowering=False, num_devices=1)
    arrays = host_layout(inputs)
    ins = {k: nc.dram_tensor(f"in_{k}", v.shape, mybir.dt.from_np(v.dtype), kind="ExternalInput").ap() for k, v in arrays.items()}
    out = nc.dram_tensor("out_x", (N, D), FP32, kind="ExternalOutput").ap()
    program(nc, ins, out)
    r = run(nc, [{f"in_{k}": v for k, v in arrays.items()}], core_ids=[0])
    return r.results[0]["out_x"]
```
